# Optimizing a Trainium2 kernel written in Bass

```python
import numpy as np
import jax
import jax.numpy as jnp

def _softmax(x, axis=-1):
    return jax.nn.softmax(x, axis=axis)

def _gelu(x):
    return jax.nn.gelu(x, approximate=True)

def _silu(x):
    return jax.nn.silu(x)

def _sigmoid(x):
    return jax.nn.sigmoid(x)

def _layernorm(x, axis=-1, eps=1e-05):
    m = jnp.mean(x, axis=axis, keepdims=True)
    v = jnp.var(x, axis=axis, keepdims=True)
    return (x - m) / jnp.sqrt(v + eps)

def _scatter_add(tgt, idx, src, axis=0):
    return tgt.at[idx].add(src)

def _segment_sum(src, seg, n):
    return jax.ops.segment_sum(src, seg, n)
kernel_name = 'mk_early_fusion_d1_tok_img256_r4_47b9ef'

def setup_inputs(seed: int=0):
    np.random.seed(seed)
    _w = jnp.asarray

    def _rec_inputs():
        import jax
        import jax.numpy as jnp
        _rk = jax.random.key(seed)
        x = 7.22013e-05 + 1.00017 * jax.random.normal(jax.random.fold_in(_rk, 1), (2, 64, 64, 64), jnp.float32)
        txt = 0.00220843 + 2.0805 * jax.random.normal(jax.random.fold_in(_rk, 2), (2, 77, 64), jnp.float32)
        return (x, txt)
    x, txt = _rec_inputs()

    def _L0_tok_setup():
        import jax, jax.numpy as jnp
        import numpy as np
        K = 3
        PAD = (K - 1) // 2
        BN_EPS = 1e-05

        def _unfold(x):
            b, c, h, w = x.shape
            xp = jnp.pad(x, ((0, 0), (0, 0), (PAD, PAD), (PAD, PAD)))
            shifts = [xp[:, :, i:i + h, j:j + w] for i in range(K) for j in range(K)]
            return jnp.stack(shifts, axis=2)
        key = jax.random.key(seed)
        ks = jax.random.split(key, 4)
        b, c, h, w = (8, 64, 64, 64)
        cr = c // 4
        x = jax.random.normal(ks[0], (b, c, h, w), dtype=jnp.float32)
        conv1_w = jax.random.normal(ks[1], (cr, c), dtype=jnp.float32) * (1.0 / np.sqrt(c))
        conv1_b = jnp.zeros((cr,), dtype=jnp.float32)
        bn_gamma = jnp.ones((cr,), dtype=jnp.float32)
        bn_beta = jnp.zeros((cr,), dtype=jnp.float32)
        bn_mean = jnp.zeros((cr,), dtype=jnp.float32)
        bn_var = jnp.ones((cr,), dtype=jnp.float32)
        conv2_w = jax.random.normal(ks[2], (K * K, cr), dtype=jnp.float32) * (1.0 / np.sqrt(cr))
        conv2_b = jnp.zeros((K * K,), dtype=jnp.float32)
        return {'x': x, 'conv1_w': conv1_w, 'conv1_b': conv1_b, 'bn_gamma': bn_gamma, 'bn_beta': bn_beta, 'bn_mean': bn_mean, 'bn_var': bn_var, 'conv2_w': conv2_w, 'conv2_b': conv2_b}
    _L0_tok_all = _L0_tok_setup()
    _L0_tok_in = {k: v for k, v in _L0_tok_all.items() if k in ('conv1_w', 'conv1_b', 'bn_gamma', 'bn_beta', 'bn_mean', 'bn_var', 'conv2_w', 'conv2_b')}
    del _L0_tok_all

    def _L0_attn_setup():
        import jax, jax.numpy as jnp
        import numpy as np
        import math
        PI = math.pi

        def _encode_phase(x, w1, b1, w2, b2):
            h = jnp.tanh(jnp.einsum('bld,ed->ble', x, w1) + b1)
            return jnp.tanh(jnp.einsum('bld,kd->blk', h, w2) + b2) * PI
        key = jax.random.key(seed)
        ks = jax.random.split(key, 12)
        B, L, D, K = (2, 512, 64, 32)
        s = 0.02
        return {'x': jax.random.normal(ks[0], (B, L, D), dtype=jnp.float32), 'kw1': jax.random.normal(ks[1], (D, D), dtype=jnp.float32) * s, 'kb1': jnp.zeros((D,), dtype=jnp.float32), 'kw2': jax.random.normal(ks[2], (K, D), dtype=jnp.float32) * s, 'kb2': jnp.zeros((K,), dtype=jnp.float32), 'qw1': jax.random.normal(ks[3], (D, D), dtype=jnp.float32) * s, 'qb1': jnp.zeros((D,), dtype=jnp.float32), 'qw2': jax.random.normal(ks[4], (K, D), dtype=jnp.float32) * s, 'qb2': jnp.zeros((K,), dtype=jnp.float32), 'vw': jax.random.normal(ks[5], (D, D), dtype=jnp.float32) * s, 'vb': jnp.zeros((D,), dtype=jnp.float32)}
    _L0_attn_all = _L0_attn_setup()
    _L0_attn_in = {k: v for k, v in _L0_attn_all.items() if k in ('kw1', 'kb1', 'kw2', 'kb2', 'qw1', 'qb1', 'qw2', 'qb2', 'vw', 'vb')}
    del _L0_attn_all

    def _L0_ffn_setup():
        import jax, jax.numpy as jnp
        import numpy as np
        B, S, H, NH, NE = (4, 256, 64, 4, 4)
        D = H // NH
        EPS = 1e-08

        def layernorm(x, g, b):
            m = jnp.mean(x, axis=-1, keepdims=True)
            v = jnp.mean((x - m) ** 2, axis=-1, keepdims=True)
            return (x - m) / jnp.sqrt(v + EPS) * g + b
        key = jax.random.key(seed)
        ks = jax.random.split(key, 18)
        sc = 0.05
        return {'x': jax.random.normal(ks[0], (B, S, H), jnp.float32), 'hl_w': jax.random.normal(ks[1], (NH, D, H), jnp.float32) * sc, 'hl_b': jax.random.normal(ks[2], (NH, D), jnp.float32) * sc, 'wq': jax.random.normal(ks[3], (NH, NE, D, D), jnp.float32) * sc, 'wk': jax.random.normal(ks[4], (NH, D, D), jnp.float32) * sc, 'wv': jax.random.normal(ks[5], (NH, D, D), jnp.float32) * sc, 'gate_w': jax.random.normal(ks[6], (NH, NE, NE * D), jnp.float32) * sc, 'gate_b': jax.random.normal(ks[7], (NH, NE), jnp.float32) * sc, 'ln_g': jnp.ones((D,), jnp.float32), 'ln_b': jnp.zeros((D,), jnp.float32), 'fc1_w': jax.random.normal(ks[8], (D, D), jnp.float32) * sc, 'fc1_b': jax.random.normal(ks[9], (D,), jnp.float32) * sc, 'fc2_w': jax.random.normal(ks[10], (D, D), jnp.float32) * sc, 'fc2_b': jax.random.normal(ks[11], (D,), jnp.float32) * sc, 'fnorm_g': jnp.ones((D,), jnp.float32), 'fnorm_b': jnp.zeros((D,), jnp.float32), 'fgate_w': jax.random.normal(ks[12], (NH, H), jnp.float32) * sc}
    _L0_ffn_all = _L0_ffn_setup()
    _L0_ffn_in = {k: v for k, v in _L0_ffn_all.items() if k in ('hl_w', 'hl_b', 'wq', 'wk', 'wv', 'gate_w', 'gate_b', 'ln_g', 'ln_b', 'fc1_w', 'fc1_b', 'fc2_w', 'fc2_b', 'fnorm_g', 'fnorm_b', 'fgate_w')}
    del _L0_ffn_all
    return {'x': x, 'txt': txt, 'L0_tok_conv1_w': _L0_tok_in['conv1_w'], 'L0_tok_conv1_b': _L0_tok_in['conv1_b'], 'L0_tok_bn_gamma': _L0_tok_in['bn_gamma'], 'L0_tok_bn_beta': _L0_tok_in['bn_beta'], 'L0_tok_bn_mean': _L0_tok_in['bn_mean'], 'L0_tok_bn_var': _L0_tok_in['bn_var'], 'L0_tok_conv2_w': _L0_tok_in['conv2_w'], 'L0_tok_conv2_b': _L0_tok_in['conv2_b'], 'L0_attn_kw1': _L0_attn_in['kw1'], 'L0_attn_kb1': _L0_attn_in['kb1'], 'L0_attn_kw2': _L0_attn_in['kw2'], 'L0_attn_kb2': _L0_attn_in['kb2'], 'L0_attn_qw1': _L0_attn_in['qw1'], 'L0_attn_qb1': _L0_attn_in['qb1'], 'L0_attn_qw2': _L0_attn_in['qw2'], 'L0_attn_qb2': _L0_attn_in['qb2'], 'L0_attn_vw': _L0_attn_in['vw'], 'L0_attn_vb': _L0_attn_in['vb'], 'L0_ffn_hl_w': _L0_ffn_in['hl_w'], 'L0_ffn_hl_b': _L0_ffn_in['hl_b'], 'L0_ffn_wq': _L0_ffn_in['wq'], 'L0_ffn_wk': _L0_ffn_in['wk'], 'L0_ffn_wv': _L0_ffn_in['wv'], 'L0_ffn_gate_w': _L0_ffn_in['gate_w'], 'L0_ffn_gate_b': _L0_ffn_in['gate_b'], 'L0_ffn_ln_g': _L0_ffn_in['ln_g'], 'L0_ffn_ln_b': _L0_ffn_in['ln_b'], 'L0_ffn_fc1_w': _L0_ffn_in['fc1_w'], 'L0_ffn_fc1_b': _L0_ffn_in['fc1_b'], 'L0_ffn_fc2_w': _L0_ffn_in['fc2_w'], 'L0_ffn_fc2_b': _L0_ffn_in['fc2_b'], 'L0_ffn_fnorm_g': _L0_ffn_in['fnorm_g'], 'L0_ffn_fnorm_b': _L0_ffn_in['fnorm_b'], 'L0_ffn_fgate_w': _L0_ffn_in['fgate_w']}

def reference(x, txt, L0_tok_conv1_w, L0_tok_conv1_b, L0_tok_bn_gamma, L0_tok_bn_beta, L0_tok_bn_mean, L0_tok_bn_var, L0_tok_conv2_w, L0_tok_conv2_b, L0_attn_kw1, L0_attn_kb1, L0_attn_kw2, L0_attn_kb2, L0_attn_qw1, L0_attn_qb1, L0_attn_qw2, L0_attn_qb2, L0_attn_vw, L0_attn_vb, L0_ffn_hl_w, L0_ffn_hl_b, L0_ffn_wq, L0_ffn_wk, L0_ffn_wv, L0_ffn_gate_w, L0_ffn_gate_b, L0_ffn_ln_g, L0_ffn_ln_b, L0_ffn_fc1_w, L0_ffn_fc1_b, L0_ffn_fc2_w, L0_ffn_fc2_b, L0_ffn_fnorm_g, L0_ffn_fnorm_b, L0_ffn_fgate_w):
    import jax
    import jax.numpy as jnp

    def _L0_tok_ref(x, conv1_w, conv1_b, bn_gamma, bn_beta, bn_mean, bn_var, conv2_w, conv2_b):
        import jax, jax.numpy as jnp
        import numpy as np
        K = 3
        PAD = (K - 1) // 2
        BN_EPS = 1e-05

        def _unfold(x):
            b, c, h, w = x.shape
            xp = jnp.pad(x, ((0, 0), (0, 0), (PAD, PAD), (PAD, PAD)))
            shifts = [xp[:, :, i:i + h, j:j + w] for i in range(K) for j in range(K)]
            return jnp.stack(shifts, axis=2)
        b, c, h, w = x.shape
        y = jnp.einsum('oc,bchw->bohw', conv1_w, x) + conv1_b[None, :, None, None]
        y = (y - bn_mean[None, :, None, None]) * (bn_gamma[None, :, None, None] * jax.lax.rsqrt(bn_var + BN_EPS)[None, :, None, None]) + bn_beta[None, :, None, None]
        y = jax.nn.relu(y)
        wdyn = jnp.einsum('ok,bkhw->bohw', conv2_w, y) + conv2_b[None, :, None, None]
        patches = _unfold(x)
        out = jnp.einsum('bckhw,bkhw->bchw', patches, wdyn)
        return out.reshape(b, h * w, c)

    def _L0_attn_ref(x, kw1, kb1, kw2, kb2, qw1, qb1, qw2, qb2, vw, vb):
        import jax, jax.numpy as jnp
        import numpy as np
        import math
        PI = math.pi

        def _encode_phase(x, w1, b1, w2, b2):
            h = jnp.tanh(jnp.einsum('bld,ed->ble', x, w1) + b1)
            return jnp.tanh(jnp.einsum('bld,kd->blk', h, w2) + b2) * PI
        B, L, D = x.shape
        key_phase = _encode_phase(x, kw1, kb1, kw2, kb2)
        query_phase = _encode_phase(x, qw1, qb1, qw2, qb2)
        K = key_phase.shape[-1]
        value = jnp.einsum('bld,ed->ble', x, vw) + vb
        cos_k = jnp.cos(key_phase)[..., None]
        sin_k = jnp.sin(key_phase)[..., None]
        v_exp = value[:, :, None, :]
        mem_real = jnp.cumsum(cos_k * v_exp, axis=1)
        mem_imag = jnp.cumsum(sin_k * v_exp, axis=1)
        cos_q = jnp.cos(query_phase)[..., None]
        sin_q = jnp.sin(query_phase)[..., None]
        retrieved = jnp.sum(mem_real * cos_q + mem_imag * sin_q, axis=2)
        positions = jnp.arange(1, L + 1, dtype=x.dtype)
        norm = jnp.sqrt(positions * K)[None, :, None]
        return retrieved / norm

    def _L0_ffn_ref(x, hl_w, hl_b, wq, wk, wv, gate_w, gate_b, ln_g, ln_b, fc1_w, fc1_b, fc2_w, fc2_b, fnorm_g, fnorm_b, fgate_w):
        import jax, jax.numpy as jnp
        import numpy as np
        B, S, H, NH, NE = (4, 256, 64, 4, 4)
        D = H // NH
        EPS = 1e-08

        def layernorm(x, g, b):
            m = jnp.mean(x, axis=-1, keepdims=True)
            v = jnp.mean((x - m) ** 2, axis=-1, keepdims=True)
            return (x - m) / jnp.sqrt(v + EPS) * g + b
        b, s, h = x.shape
        nh, d, _ = wk.shape
        ne = wq.shape[1]
        sx = jnp.einsum('bsh,ndh->bnsd', x, hl_w) + hl_b[None, :, None, :]
        pad = sx == 0
        q = jnp.einsum('bnsd,neod->bneso', sx, wq)
        k = jnp.einsum('bnsd,nod->bnso', sx, wk)
        v = jnp.einsum('bnsd,nod->bnso', sx, wv)
        causal = jnp.where(jnp.tril(jnp.ones((s, s), bool)), 0.0, -jnp.inf).astype(x.dtype)
        scores = jnp.einsum('bnesd,bntd->bnest', q, k) * d ** 0.5 + causal
        att = jax.nn.softmax(scores, axis=-1)
        qkv = jnp.einsum('bnest,bntd->bnesd', att, v)
        qkv = jnp.where(pad[:, :, None], 0.0, qkv)
        out = jnp.transpose(qkv, (0, 1, 3, 2, 4)).reshape(b, nh, s, ne * d)
        gs = jax.nn.softmax(jnp.einsum('bnsf,nef->bnse', out, gate_w) + gate_b[None, :, None, :], axis=-1)
        mixed = jnp.einsum('bnsed,bnse->bnsd', out.reshape(b, nh, s, ne, d), gs)
        resid = sx[jnp.arange(nh), jnp.arange(nh)]
        hn = layernorm(mixed + resid, ln_g, ln_b)
        f_n = jnp.transpose(hn, (0, 2, 1, 3)).reshape(b, s, h)
        fx = f_n.reshape(b, s, nh, d)
        pm = fx == 0
        hx = jnp.where(pm, 0.0, fx @ fc1_w.T + fc1_b)
        hx = jax.nn.relu(hx)
        hx = jnp.where(pm, 0.0, hx @ fc2_w.T + fc2_b)
        hx = layernorm(hx + fx, fnorm_g, fnorm_b)
        fout = hx.reshape(b, s, h)
        fg = jax.nn.softmax(fout @ fgate_w.T, axis=-1)
        return (fout.reshape(b, s, nh, d) * fg[..., None]).reshape(b, s, h)
    h = _L0_tok_ref(x, L0_tok_conv1_w, L0_tok_conv1_b, L0_tok_bn_gamma, L0_tok_bn_beta, L0_tok_bn_mean, L0_tok_bn_var, L0_tok_conv2_w, L0_tok_conv2_b)
    h = jnp.concatenate([h, txt], axis=1)
    h = h + _L0_attn_ref(_layernorm(h, axis=-1), L0_attn_kw1, L0_attn_kb1, L0_attn_kw2, L0_attn_kb2, L0_attn_qw1, L0_attn_qb1, L0_attn_qw2, L0_attn_qb2, L0_attn_vw, L0_attn_vb)
    h = h + _L0_ffn_ref(_layernorm(h, axis=-1), L0_ffn_hl_w, L0_ffn_hl_b, L0_ffn_wq, L0_ffn_wk, L0_ffn_wv, L0_ffn_gate_w, L0_ffn_gate_b, L0_ffn_ln_g, L0_ffn_ln_b, L0_ffn_fc1_w, L0_ffn_fc1_b, L0_ffn_fc2_w, L0_ffn_fc2_b, L0_ffn_fnorm_g, L0_ffn_fnorm_b, L0_ffn_fgate_w)
    return h

_drawn_inputs = setup_inputs


def setup_inputs(seed=0):
    import zlib

    import numpy as np

    out = dict(_drawn_inputs(seed))
    spreads = {'L0_tok_conv1_b': (0.0, 0.8),
     'L0_tok_bn_gamma': (1.0, 0.6),
     'L0_tok_bn_beta': (0.0, 0.528),
     'L0_tok_bn_mean': (0.0, 0.8),
     'L0_tok_bn_var': (1.0, 0.6),
     'L0_tok_conv2_b': (0.0, 0.8),
     'L0_attn_kb1': (0.0, 0.8),
     'L0_attn_kb2': (0.0, 0.1),
     'L0_attn_qb1': (0.0, 0.8),
     'L0_attn_qb2': (0.0, 0.1),
     'L0_attn_vb': (0.0, 0.1),
     'L0_ffn_ln_g': (1.0, 0.6),
     'L0_ffn_ln_b': (0.0, 0.8),
     'L0_ffn_fnorm_g': (1.0, 0.6),
     'L0_ffn_fnorm_b': (0.0, 0.8)}
    factors = {'txt': 5.023,
     'L0_attn_kw1': 8.0,
     'L0_attn_kw2': 8.0,
     'L0_attn_qw1': 8.0,
     'L0_attn_qw2': 8.0,
     'L0_ffn_hl_w': 4.727,
     'L0_ffn_hl_b': 8.0,
     'L0_ffn_wq': 8.0,
     'L0_ffn_wk': 8.0,
     'L0_ffn_wv': 8.0,
     'L0_ffn_gate_w': 8.0,
     'L0_ffn_gate_b': 8.0,
     'L0_ffn_fc1_w': 8.0,
     'L0_ffn_fc1_b': 8.0,
     'L0_ffn_fc2_w': 8.0,
     'L0_ffn_fc2_b': 8.0,
     'L0_ffn_fgate_w': 8.0}
    for name, (base, spread) in spreads.items():
        noise = np.random.default_rng([zlib.crc32(name.encode()), seed]).standard_normal(out[name].shape)
        drawn = base * np.exp(spread * noise) if base else spread * noise
        out[name] = jnp.asarray(drawn.astype(out[name].dtype))
    for name, factor in factors.items():
        out[name] = (out[name] * factor).astype(out[name].dtype)
    return out
```

```python
import numpy as np
import concourse.bass as bass
from concourse import mybir
from contextlib import ExitStack

BATCH, CH, ROWS, COLS, TEXT = 2, 64, 64, 64, 77
FEAT = 64
IMAGE = CH * ROWS
TOKENS = IMAGE + TEXT
P = 128
TILES = -(-TOKENS // P)
PADDED = TILES * P
TAPS = 9
REDUCED = 16
PHASES = 32
NH, NE, HD = 4, 4, 16
HEADS = BATCH * NH
TURNS = HEADS
BN_EPS, LN_EPS, FFN_EPS = 1e-5, 1e-5, 1e-8
BANK = 512
CHUNKS = [(c, min(BANK, PADDED - c)) for c in range(0, PADDED, BANK)]
NEG = -3.0e38
PI_BELOW = 3.1415925

WIDTHS = [
    ("conv1", 32), ("conv2", TAPS * P), ("bn", 5), ("conv2_b", TAPS),
    ("kw1", P), ("qw1", P), ("kb1", 1), ("qb1", 1), ("kw2", P), ("qw2", P), ("kb2", 1), ("qb2", 1),
    ("vw", P), ("vb", P), ("hl", P), ("hl_b", 1), ("wk", P), ("wq", NE * P), ("wv", P),
    ("gate", 16), ("gate_b", 32), ("ln_g", HD), ("ln_b", HD), ("fc1", P), ("fc1_b", 1), ("fc2", P),
    ("fc2_b", P), ("fn_g", HD), ("fn_b", HD), ("fgate", 8),
    ("ident", P), ("keep", P), ("neg_s", P), ("neg_t", P), ("inv_norm", TILES), ("fold", 32), ("phase", 3),
]
AT, _n = {}, 0
for _name, _w in WIDTHS:
    AT[_name] = (_n, _n + _w)
    _n += _w
PACKED = _n


def build(nc, x, txt, packed, out):
    fp32, bf16 = mybir.dt.float32, mybir.dt.bfloat16
    ALU, ACT, AX = mybir.AluOpType, mybir.ActivationFunctionType, mybir.AxisListType
    top = ExitStack()

    def sem(name):
        return top.enter_context(nc.semaphore(name))

    tokens_dram = nc.dram_tensor("tokens_scratch", [BATCH, IMAGE, FEAT], fp32, kind="Internal").ap()
    keys_dram = nc.dram_tensor("keys_scratch", [3, P + HD, PADDED], bf16, kind="Internal").ap()
    queries_dram = nc.dram_tensor("queries_scratch", [3, P + HD, NE, PADDED], bf16, kind="Internal").ap()

    with top:
        def sb(stack, name, shape, dt=fp32):
            return stack.enter_context(nc.sbuf_tensor(name, shape, dt))

        def pb(stack, name, shape, dt=fp32):
            return stack.enter_context(nc.psum_tensor(name, shape, dt))

        con = sb(top, "con", [P, PACKED])
        hid = sb(top, "hid", [P, TILES, BATCH * FEAT])

        def const(name, p0=0, p1=P, c0=0, c1=None):
            a, b = AT[name]
            return con[p0:p1, a + c0:(b if c1 is None else a + c1)]

        class Chain:
            def __init__(self, name):
                self.sem, self.n = sem(name), 0

            def __call__(self, eng, ins):
                self.n += 1
                ins.then_inc(self.sem, 1)
                eng.wait_ge(self.sem, self.n)

        def normalise_vector(dve, chain, data, cent, work, stat, groups, width, eps, squares, centred, varred, rooted):
            def wide(s):
                return s.unsqueeze(2).to_broadcast([P, groups, width])
            chain(dve, nc.vector.tensor_reduce(stat[:, 0, 0:groups], data, AX.X, ALU.add))
            chain(dve, nc.vector.tensor_scalar(stat[:, 0, 0:groups], stat[:, 0, 0:groups], 1.0 / width, None, ALU.mult))
            chain(dve, nc.vector.tensor_tensor(cent, data, wide(stat[:, 0, 0:groups]), ALU.subtract))
            nc.vector.tensor_scalar(stat[:, 3, 0:1], stat[:, 0, 0:1], 0.0, None, ALU.mult).then_inc(centred, 1)
            dve.wait_ge(squares, 1)
            chain(dve, nc.vector.tensor_reduce(stat[:, 1, 0:groups], work, AX.X, ALU.add))
            nc.vector.tensor_scalar(stat[:, 1, 0:groups], stat[:, 1, 0:groups], 1.0 / width, eps, ALU.mult, ALU.add)\
                .then_inc(varred, 1)
            dve.wait_ge(rooted, 1)
            chain(dve, nc.vector.reciprocal(stat[:, 2, 0:groups], stat[:, 2, 0:groups]))
            chain(dve, nc.vector.tensor_tensor(cent, cent, wide(stat[:, 2, 0:groups]), ALU.mult))

        def normalise_scalar(act, cent, work, stat, groups, squares, centred, varred, rooted):
            act.wait_ge(centred, 1)
            nc.scalar.activation(work, cent, ACT.Square).then_inc(squares, 1)
            act.wait_ge(varred, 1)
            nc.scalar.activation(stat[:, 2, 0:groups], stat[:, 1, 0:groups], ACT.Sqrt).then_inc(rooted, 1)

        with ExitStack() as st:
            x_sb = sb(st, "x_sb", [P, ROWS * COLS])
            xpad = sb(st, "xpad", [P, ROWS + 2, COLS + 2])
            red = sb(st, "red", [BATCH * REDUCED, ROWS * COLS])
            acc = sb(st, "acc", [P, ROWS * COLS])
            prod = sb(st, "prod", [P, 4, BANK])
            bn = sb(st, "bn", [BATCH * REDUCED, 4])
            ps_red = [pb(st, f"ps_red{k}", [P, BANK]) for k in range(2)]
            ps_tap = [pb(st, f"ps_tap{k}", [P, BANK]) for k in range(4)]
            con_in, x_in, pad_zero, xpad_done = sem("con_in"), sem("x_in"), sem("pad_zero"), sem("xpad_done")
            bn_var, bn_root, bn_done = sem("bn_var"), sem("bn_root"), sem("bn_done")
            red_mm, red_done, tap_mm, tap_prod, tap_added = (sem(n) for n in ("red_mm", "red_done", "tap_mm", "tap_prod", "tap_added"))
            tok_out, hid_in, hid_zero = sem("tok_out"), sem("hid_in"), sem("hid_zero")
            own = Chain("tok_vector")
            NPX = ROWS * COLS // BANK
            R = BANK // COLS
            QR = BATCH * REDUCED
            with nc.Block() as block:
                @block.sync
                def _(sp):
                    sp.dma_start(x_sb[:, :], x.rearrange("b c h w -> (b c) (h w)")).then_inc(x_in, 16)
                    sp.dma_start(con[:, :], packed).then_inc(con_in, 16)
                    sp.wait_ge(hid_zero, 1)
                    sp.dma_start(hid[0:TEXT, TILES - 1, :].rearrange("p (b f) -> p b f", b=BATCH),
                                 txt.rearrange("b t f -> t b f")).then_inc(hid_in, 16)
                    tok_v = tokens_dram.rearrange("b (c h) w -> (b c) (h w)", c=CH)
                    for q in range(NPX):
                        sp.wait_ge(tap_added, q * TAPS + TAPS)
                        sp.dma_start(tok_v[:, q * BANK:(q + 1) * BANK], acc[:, q * BANK:(q + 1) * BANK]).then_inc(tok_out, 16)
                    sp.wait_ge(tok_out, 16 * NPX)
                    for b in range(BATCH):
                        sp.dma_start(hid[:, 0:TILES - 1, b * FEAT:(b + 1) * FEAT],
                                     tokens_dram[b].rearrange("(i p) f -> p i f", p=P)).then_inc(hid_in, 16)
                    sp.wait_ge(hid_in, 16 * (1 + BATCH))

                @block.tensor
                def _(pe):
                    pe.wait_ge(x_in, 16)
                    pe.wait_ge(con_in, 16)
                    for q in range(NPX):
                        if q >= 2:
                            pe.wait_ge(red_done, q - 1)
                        nc.tensor.matmul(ps_red[q % 2][0:QR, :], const("conv1"), x_sb[:, q * BANK:(q + 1) * BANK],
                                         start=True, stop=True).then_inc(red_mm, 1)
                    for q in range(NPX):
                        pe.wait_ge(red_done, q + 1)
                        for k in range(TAPS):
                            n = q * TAPS + k
                            if n >= 4:
                                pe.wait_ge(tap_prod, n - 3)
                            nc.tensor.matmul(ps_tap[n % 4][:, :], const("conv2", 0, QR, k * P, (k + 1) * P),
                                             red[:, q * BANK:(q + 1) * BANK], start=True, stop=True).then_inc(tap_mm, 1)

                @block.scalar
                def _(act):
                    act.wait_ge(x_in, 16)
                    act.wait_ge(pad_zero, 1)
                    nc.scalar.activation(xpad[:, 1:ROWS + 1, 1:COLS + 1],
                                         x_sb[:, :].rearrange("p (h w) -> p h w", h=ROWS), ACT.Copy).then_inc(xpad_done, 1)
                    act.wait_ge(bn_var, 1)
                    nc.scalar.activation(bn[:, 1:2], bn[:, 0:1], ACT.Sqrt).then_inc(bn_root, 1)
                    act.wait_ge(bn_done, 1)
                    for q in range(NPX):
                        act.wait_ge(red_mm, q + 1)
                        nc.scalar.activation(red[:, q * BANK:(q + 1) * BANK], ps_red[q % 2][0:QR, :], ACT.Relu,
                                             bias=bn[:, 3:4], scale=bn[:, 2:3]).then_inc(red_done, 1)

                @block.vector
                def _(dve):
                    nc.vector.memset(xpad[:, :, :], 0.0).then_inc(pad_zero, 1)
                    dve.wait_ge(con_in, 16)
                    b1, gamma, beta, mean, var = (const("bn", 0, QR, k, k + 1) for k in range(5))
                    nc.vector.tensor_scalar(bn[:, 0:1], var, BN_EPS, None, ALU.add).then_inc(bn_var, 1)
                    dve.wait_ge(bn_root, 1)
                    own(dve, nc.vector.reciprocal(bn[:, 2:3], bn[:, 1:2]))
                    own(dve, nc.vector.tensor_tensor(bn[:, 2:3], bn[:, 2:3], gamma, ALU.mult))
                    own(dve, nc.vector.tensor_tensor(bn[:, 3:4], b1, mean, ALU.subtract))
                    own(dve, nc.vector.tensor_tensor(bn[:, 3:4], bn[:, 3:4], bn[:, 2:3], ALU.mult))
                    nc.vector.tensor_tensor(bn[:, 3:4], bn[:, 3:4], beta, ALU.add).then_inc(bn_done, 1)
                    dve.wait_ge(xpad_done, 1)
                    for q in range(NPX):
                        for k in range(TAPS):
                            n = q * TAPS + k
                            dve.wait_ge(tap_mm, n + 1)
                            if n >= 4:
                                dve.wait_ge(tap_added, n - 3)
                            di, dj = k // 3, k % 3
                            nc.vector.scalar_tensor_tensor(
                                prod[:, n % 4, :].rearrange("p (r w) -> p r w", w=COLS),
                                ps_tap[n % 4][:, :].rearrange("p (r w) -> p r w", w=COLS), const("conv2_b", 0, P, k, k + 1),
                                xpad[:, q * R + di:q * R + di + R, dj:dj + COLS], ALU.add, ALU.mult).then_inc(tap_prod, 1)

                @block.gpsimd
                def _(pool):
                    nc.gpsimd.memset(hid[:, TILES - 1, :], 0.0).then_inc(hid_zero, 1)
                    for q in range(NPX):
                        a = acc[:, q * BANK:(q + 1) * BANK]
                        for k in range(TAPS):
                            n = q * TAPS + k
                            pool.wait_ge(tap_prod, n + 1)
                            if k == 0:
                                ins = nc.gpsimd.tensor_copy(a, prod[:, n % 4, :])
                            else:
                                pool.wait_ge(tap_added, n)
                                ins = nc.gpsimd.tensor_tensor(a, a, prod[:, n % 4, :], ALU.add)
                            ins.then_inc(tap_added, 1)

        HALF = BATCH * FEAT
        GROUPS = TILES * BATCH
        with ExitStack() as st:
            stat = sb(st, "stat", [P, 4, GROUPS])
            cent = sb(st, "cent", [P, TILES, HALF])
            work = sb(st, "work", [P, TILES, HALF])
            normT = sb(st, "normT", [P, PADDED])
            hkq = sb(st, "hkq", [P, 2, 2, BANK])
            feat = [sb(st, f"feat{k}", [P, PADDED]) for k in range(2)]
            fold_abs = [cent[:, :, :].rearrange("p i f -> p (i f)"), work[:, :, :].rearrange("p i f -> p (i f)")]
            ps = [pb(st, f"ps2_{k}", [P, BANK]) for k in range(8)]
            names = ("squares", "centred", "varred", "rooted")
            ln1 = [sem("ln1_" + n) for n in names]
            ln1_done, tr_mm, tr_done = sem("ln1_done"), sem("tr_mm"), sem("tr_done")
            l1_mm, l1_done, l2_mm, l2_done, abs_done, feat_done = (
                sem(n) for n in ("l1_mm", "l1_done", "l2_mm", "l2_done", "abs_done", "feat_done"))
            own = Chain("phase_vector")
            with nc.Block() as block:
                v3 = lambda a: a[:, :, :].rearrange("p i (b f) -> p (i b) f", b=BATCH)

                @block.vector
                def _(dve):
                    normalise_vector(dve, own, v3(hid), v3(cent), v3(work), stat, GROUPS, FEAT, LN_EPS, *ln1)
                    nc.vector.tensor_scalar(stat[:, 3, 0:1], stat[:, 0, 0:1], 0.0, None, ALU.mult).then_inc(ln1_done, 1)
                    for k in range(2):
                        dve.wait_ge(l2_done, 2 * len(CHUNKS))
                        nc.vector.scalar_tensor_tensor(fold_abs[k], feat[k][:, :], const("phase", 0, P, 0, 1), feat[k][:, :],
                                                       ALU.mult, ALU.max).then_inc(abs_done, 1)

                @block.tensor
                def _(pe):
                    pe.wait_ge(ln1_done, 1)
                    for c, (c0, w) in enumerate(CHUNKS):
                        if c >= 2:
                            pe.wait_ge(tr_done, c - 1)
                        for t in range(w // P):
                            last = nc.tensor.transpose(ps[c % 2][:, t * P:(t + 1) * P], cent[:, c0 // P + t, :], const("ident"))
                        last.then_inc(tr_mm, 1)
                    for c in range(len(CHUNKS) + 1):
                        if c < len(CHUNKS):
                            c0, w = CHUNKS[c]
                            pe.wait_ge(tr_done, c + 1)
                            for k, name in enumerate(("kw1", "qw1")):
                                n = 2 * c + k
                                if n >= 2:
                                    pe.wait_ge(l1_done, n - 1)
                                nc.tensor.matmul(ps[2 + k][:, 0:w], const(name), normT[:, c0:c0 + w], start=True, stop=True)\
                                    .then_inc(l1_mm, 1)
                        if c >= 1:
                            c0, w = CHUNKS[c - 1]
                            for k, name in enumerate(("kw2", "qw2")):
                                n = 2 * (c - 1) + k
                                pe.wait_ge(l1_done, n + 1)
                                if n >= 4:
                                    pe.wait_ge(l2_done, n - 3)
                                nc.tensor.matmul(ps[4 + n % 4][:, 0:w], const(name), hkq[:, (c - 1) % 2, k, 0:w],
                                                 start=True, stop=True).then_inc(l2_mm, 1)

                @block.scalar
                def _(act):
                    normalise_scalar(act, v3(cent), v3(work), stat, GROUPS, *ln1)
                    for c, (c0, w) in enumerate(CHUNKS):
                        act.wait_ge(tr_mm, c + 1)
                        nc.scalar.activation(normT[:, c0:c0 + w], ps[c % 2][:, 0:w], ACT.Copy).then_inc(tr_done, 1)
                    for c in range(len(CHUNKS) + 1):
                        if c < len(CHUNKS):
                            c0, w = CHUNKS[c]
                            for k, name in enumerate(("kb1", "qb1")):
                                n = 2 * c + k
                                act.wait_ge(l1_mm, n + 1)
                                if n >= 4:
                                    act.wait_ge(l2_mm, n - 3)
                                nc.scalar.activation(hkq[:, c % 2, k, 0:w], ps[2 + k][:, 0:w], ACT.Tanh, bias=const(name))\
                                    .then_inc(l1_done, 1)
                        if c >= 1:
                            c0, w = CHUNKS[c - 1]
                            for k, name in enumerate(("kb2", "qb2")):
                                n = 2 * (c - 1) + k
                                act.wait_ge(l2_mm, n + 1)
                                nc.scalar.activation(feat[k][:, c0:c0 + w], ps[4 + n % 4][:, 0:w], ACT.Tanh, bias=const(name))\
                                    .then_inc(l2_done, 1)
                    for k in range(2):
                        act.wait_ge(abs_done, k + 1)
                        nc.scalar.activation(feat[k][:, :], fold_abs[k], ACT.Sin, bias=const("phase", 0, P, 2, 3),
                                             scale=const("phase", 0, P, 1, 2)).then_inc(feat_done, 1)

            val = sb(st, "val", [P, 2, HALF])
            keyT = sb(st, "keyT", [P, 2, P])
            att = sb(st, "att", [P, 2, BATCH, P])
            state = sb(st, "state", [P, 2, HALF])
            v_mm, v_sb, kt_mm, kt_sb, a_mm, a_sb, m_mm, m_sb, o_mm, o_sb, st_zero = (
                sem(n) for n in ("v_mm", "v_sb", "kt_mm", "kt_sb", "a_mm", "a_sb", "m_mm", "m_sb", "o_mm", "o_sb", "st_zero"))
            ps_v, ps_kt, ps_a, ps_m, ps_o = ps[0], ps[1], (ps[2], ps[3]), (ps[4], ps[7]), (ps[5], ps[6])
            with nc.Block() as block:
                @block.tensor
                def _(pe):
                    for i in range(TILES + 1):
                        if i < TILES:
                            t = slice(i * P, (i + 1) * P)
                            if i >= 1:
                                pe.wait_ge(v_sb, i)
                                pe.wait_ge(kt_sb, i)
                                pe.wait_ge(a_sb, 2 * i)
                            nc.tensor.matmul(ps_v[:, 0:HALF], normT[:, t], const("vw"), start=True, stop=True).then_inc(v_mm, 1)
                            nc.tensor.transpose(ps_kt[:, 0:P], feat[0][:, t], const("ident")).then_inc(kt_mm, 1)
                            for b in range(BATCH):
                                r = slice(b * FEAT, (b + 1) * FEAT)
                                nc.tensor.matmul(ps_a[b][:, 0:P], feat[0][r, t], feat[1][r, t], start=True, stop=True)\
                                    .then_inc(a_mm, 1)
                        if i >= 1:
                            j = i - 1
                            t = slice(j * P, (j + 1) * P)
                            if j == 0:
                                pe.wait_ge(st_zero, 2)
                            else:
                                pe.wait_ge(m_sb, BATCH * j)
                            if j >= 2:
                                pe.wait_ge(o_sb, j - 1)
                            o = ps_o[j % 2][:, 0:HALF]
                            nc.tensor.matmul(o, feat[1][:, t], state[:, j % 2, :], start=True, stop=False)
                            pe.wait_ge(v_sb, j + 1)
                            pe.wait_ge(a_sb, 2 * j + 2)
                            for b in range(BATCH):
                                f = slice(b * FEAT, (b + 1) * FEAT)
                                last = nc.tensor.matmul(o[:, f], att[:, j % 2, b, :], val[:, j % 2, f], start=False, stop=(b == 1))
                            last.then_inc(o_mm, 1)
                            if j < TILES - 1:
                                pe.wait_ge(kt_sb, j + 1)
                                nc.tensor.matmul(ps_m[j % 2][:, 0:HALF], keyT[:, j % 2, :], val[:, j % 2, :], start=True,
                                                 stop=True).then_inc(m_mm, 1)

                @block.scalar
                def _(act):
                    for i in range(TILES):
                        act.wait_ge(kt_mm, i + 1)
                        if i >= 2:
                            act.wait_ge(m_mm, i - 1)
                        nc.scalar.activation(keyT[:, i % 2, :], ps_kt[:, 0:P], ACT.Copy).then_inc(kt_sb, 1)

                @block.vector
                def _(dve):
                    for k in range(2):
                        nc.vector.memset(state[:, k, :], 0.0).then_inc(st_zero, 1)
                    for i in range(TILES + 1):
                        if i < TILES:
                            dve.wait_ge(v_mm, i + 1)
                            if i >= 2:
                                dve.wait_ge(o_mm, i - 1)
                                dve.wait_ge(m_mm, i - 1)
                            nc.vector.tensor_tensor(val[:, i % 2, :], ps_v[:, 0:HALF], const("vb"), ALU.add).then_inc(v_sb, 1)
                            for b in range(BATCH):
                                dve.wait_ge(a_mm, 2 * i + b + 1)
                                nc.vector.tensor_tensor(att[:, i % 2, b, :], ps_a[b][:, 0:P], const("keep"), ALU.mult)\
                                    .then_inc(a_sb, 1)
                        if i >= 1:
                            j = i - 1
                            dve.wait_ge(o_mm, j + 1)
                            nc.vector.scalar_tensor_tensor(hid[:, j, :], ps_o[j % 2][:, 0:HALF], const("inv_norm", 0, P, j, j + 1),
                                                           hid[:, j, :], ALU.mult, ALU.add).then_inc(o_sb, 1)
                            if j < TILES - 1:
                                dve.wait_ge(m_mm, j + 1)
                                dve.wait_ge(m_sb, BATCH * j) if j else dve.wait_ge(st_zero, 2)
                                for b in range(BATCH):
                                    f = slice(b * FEAT, (b + 1) * FEAT)
                                    nc.vector.tensor_tensor(state[f, (j + 1) % 2, f], state[f, j % 2, f], ps_m[j % 2][f, f], ALU.add)\
                                        .then_inc(m_sb, 1)

        mid = top.enter_context(ExitStack())
        sx_tok = sb(mid, "sx_tok", [P, TILES, P])
        values = sb(mid, "values", [P, HEADS, TILES * 32])
        with ExitStack() as st:
            stat = sb(st, "stat3", [P, 4, GROUPS])
            cent = sb(st, "cent3", [P, TILES, HALF])
            work = sb(st, "work3", [P, TILES, HALF])
            normT = work[:, :, :].rearrange("p i f -> p (i f)")
            sxT = cent[:, :, :].rearrange("p i f -> p (i f)")
            part = sb(st, "part", [P, 2, 3, PADDED], bf16)
            rest = sb(st, "rest", [P, 3, BANK])
            ps = [pb(st, f"ps3_{k}", [P, BANK]) for k in range(8)]
            ln2 = [sem("ln2_" + n) for n in names]
            (ln2_done, tr2_mm, tr2_done, sx_mm, sx_done, sxt_mm, sxt_done, val_mm, val_done, val_zero, val_one,
             proj_mm, part1, rest1, part2, part3, part_out) = (sem(n) for n in (
                "ln2_done", "tr2_mm", "tr2_done", "sx_mm", "sx_done", "sxt_mm", "sxt_done", "val_mm", "val_done",
                "val_zero", "val_one", "proj_mm", "part1", "rest1", "part2", "part3", "part_out"))
            own = Chain("proj_vector")
            NC = len(CHUNKS)
            MATS = 1 + NE
            vals = values[:, :, :].rearrange("p h (i f) -> p h i f", f=32)
            with nc.Block() as block:
                @block.vector
                def _(dve):
                    normalise_vector(dve, own, v3(hid), v3(cent), v3(work), stat, GROUPS, FEAT, LN_EPS, *ln2)
                    nc.vector.tensor_scalar(stat[:, 3, 0:1], stat[:, 0, 0:1], 0.0, None, ALU.mult).then_inc(ln2_done, 1)
                    dve.wait_ge(val_one, HEADS)
                    for c, (c0, w) in enumerate(CHUNKS):
                        dve.wait_ge(sxt_mm, c + 1)
                        nc.vector.tensor_copy(sx_tok[:, :, :].rearrange("p i f -> p (i f)")[:, c0:c0 + w], ps[c % 2][:, 0:w])\
                            .then_inc(sxt_done, 1)
                        dve.wait_ge(val_mm, c + 1)
                        nt = w // P
                        for t in range(nt):
                            last = nc.vector.tensor_copy(
                                vals[:, :, c0 // P + t, 0:HD],
                                ps[2 + c % 2][:, t * P:(t + 1) * P].rearrange("p (h f) -> p h f", f=HD))
                        last.then_inc(val_done, 1)
                    for m in range(MATS):
                        for c, (c0, w) in enumerate(CHUNKS):
                            n = m * NC + c
                            dve.wait_ge(part1, n + 1)
                            if n >= 3:
                                dve.wait_ge(part3, n - 2)
                            nc.vector.scalar_tensor_tensor(rest[:, n % 3, 0:w], ps[4 + n % 4][:, 0:w], 1.0 if m == 0 else float(HD) ** 0.5,
                                                           part[:, m % 2, 0, c0:c0 + w], ALU.mult, ALU.subtract).then_inc(rest1, 1)

                @block.tensor
                def _(pe):
                    pe.wait_ge(ln2_done, 1)
                    for c, (c0, w) in enumerate(CHUNKS):
                        if c >= 2:
                            pe.wait_ge(tr2_done, c - 1)
                        for t in range(w // P):
                            last = nc.tensor.transpose(ps[c % 2][:, t * P:(t + 1) * P], cent[:, c0 // P + t, :], const("ident"))
                        last.then_inc(tr2_mm, 1)
                    pe.wait_ge(tr2_done, NC)
                    for c, (c0, w) in enumerate(CHUNKS):
                        if c >= 2:
                            pe.wait_ge(sx_done, c - 1)
                        nc.tensor.matmul(ps[2 + c % 2][:, 0:w], const("hl"), normT[:, c0:c0 + w], start=True, stop=True).then_inc(sx_mm, 1)
                    pe.wait_ge(sx_done, NC)
                    for c, (c0, w) in enumerate(CHUNKS):
                        if c >= 2:
                            pe.wait_ge(sxt_done, c - 1)
                            pe.wait_ge(val_done, c - 1)
                        for t in range(w // P):
                            last = nc.tensor.transpose(ps[c % 2][:, t * P:(t + 1) * P], sxT[:, c0 + t * P:c0 + (t + 1) * P], const("ident"))
                        last.then_inc(sxt_mm, 1)
                        for t in range(w // P):
                            last = nc.tensor.matmul(ps[2 + c % 2][:, t * P:(t + 1) * P], sxT[:, c0 + t * P:c0 + (t + 1) * P], const("wv"),
                                                    start=True, stop=True)
                        last.then_inc(val_mm, 1)
                    for m in range(MATS):
                        wt = const("wk") if m == 0 else const("wq", 0, P, (m - 1) * P, m * P)
                        for c, (c0, w) in enumerate(CHUNKS):
                            n = m * NC + c
                            if n >= 4:
                                pe.wait_ge(rest1, n - 3)
                            nc.tensor.matmul(ps[4 + n % 4][:, 0:w], wt, sxT[:, c0:c0 + w], start=True, stop=True).then_inc(proj_mm, 1)

                @block.scalar
                def _(act):
                    normalise_scalar(act, v3(cent), v3(work), stat, GROUPS, *ln2)
                    act.wait_ge(ln2_done, 1)
                    for c, (c0, w) in enumerate(CHUNKS):
                        act.wait_ge(tr2_mm, c + 1)
                        nc.scalar.activation(normT[:, c0:c0 + w], ps[c % 2][:, 0:w], ACT.Copy).then_inc(tr2_done, 1)
                    act.wait_ge(tr2_mm, NC)
                    for c, (c0, w) in enumerate(CHUNKS):
                        act.wait_ge(sx_mm, c + 1)
                        nc.scalar.activation(sxT[:, c0:c0 + w], ps[2 + c % 2][:, 0:w], ACT.Identity, bias=const("hl_b")).then_inc(sx_done, 1)
                    for m in range(MATS):
                        if m >= 2:
                            act.wait_ge(part_out, 32 * (m - 1))
                        for c in range(NC + 1):
                            if c < NC:
                                c0, w = CHUNKS[c]
                                n = m * NC + c
                                act.wait_ge(proj_mm, n + 1)
                                nc.scalar.activation(part[:, m % 2, 0, c0:c0 + w], ps[4 + n % 4][:, 0:w], ACT.Copy,
                                                     scale=1.0 if m == 0 else float(HD) ** 0.5).then_inc(part1, 1)
                            if c >= 1:
                                c0, w = CHUNKS[c - 1]
                                n = m * NC + c - 1
                                act.wait_ge(rest1, n + 1)
                                nc.scalar.activation(part[:, m % 2, 1, c0:c0 + w], rest[:, n % 3, 0:w], ACT.Copy).then_inc(part2, 1)

                @block.gpsimd
                def _(pool):
                    nc.gpsimd.memset(values[:, :, :], 0.0).then_inc(val_zero, 1)
                    pool.wait_ge(val_zero, 1)
                    for h in range(HEADS):
                        nc.gpsimd.memset(vals[:, h, :, HD:HD + 1], 1.0).then_inc(val_one, 1)
                    for m in range(MATS):
                        if m >= 2:
                            pool.wait_ge(part_out, 32 * (m - 1))
                        for c, (c0, w) in enumerate(CHUNKS):
                            n = m * NC + c
                            pool.wait_ge(part2, n + 1)
                            nc.gpsimd.tensor_tensor(part[:, m % 2, 2, c0:c0 + w], rest[:, n % 3, 0:w], part[:, m % 2, 1, c0:c0 + w],
                                                    ALU.subtract).then_inc(part3, 1)

                @block.sync
                def _(sp):
                    for m in range(MATS):
                        sp.wait_ge(part3, (m + 1) * NC)
                        dst = keys_dram if m == 0 else queries_dram[:, :, m - 1, :]
                        sp.dma_start(dst[:, 0:P, :].rearrange("a p t -> p a t"), part[:, m % 2, :, :]).then_inc(part_out, 16)
                        sp.dma_start(dst[:, P:P + HD, :].rearrange("a p t -> p a t"), part[0:HD, m % 2, :, :]).then_inc(part_out, 16)
                        sp.wait_ge(part_out, 32 * (m + 1))

        attn = sb(mid, "attn", [P, TILES, HEADS, NE * HD])
        K6 = 6 * HD
        KM = K6 + 3 * NE
        QSLOTS = 3
        QGROUPS = -(-TILES // 4)
        assert QGROUPS % QSLOTS == 0
        RING = 3
        with ExitStack() as st:
            keys = sb(st, "keys", [P, PADDED], bf16)
            query = sb(st, "query", [P, QSLOTS, NE, BANK], bf16)
            vhead = sb(st, "vhead", [P, TILES * 32])
            NP = 8
            prob = sb(st, "prob", [P, NP, BANK])
            osum = sb(st, "osum", [P, BANK])
            identb = sb(st, "identb", [P, P], bf16)
            negs = sb(st, "negs", [P, P], bf16)
            negt = sb(st, "negt", [P, NE, P], bf16)
            pmax = sb(st, "pmax", [P, 2, NE, 8])
            nmax = sb(st, "nmax", [P, 2, NE])
            mrest = sb(st, "mrest", [P, NE])
            mpart = sb(st, "mpart", [P, 2, NE * 32], bf16)
            rden = sb(st, "rden", [P, NE])
            ps_max = [pb(st, f"ps_max{k}", [P, 2 * BANK]) for k in range(2)]
            ps_ring = [pb(st, f"ps_ring{k}", [P, BANK]) for k in range(RING)]
            ps_av = pb(st, "ps_av", [P, BANK])

            prep, head_go, head_done, heads_clear = sem("prep"), sem("head_go"), sem("head_done"), sem("heads_clear")
            k_in = [sem(f"k_in{k}") for k in range(3)]
            q_in = [sem(f"q_in{k}") for k in range(QSLOTS)]
            turns = sem("turns")
            (v_in, qk_mm, exp_done, av_mm, av_read, fold_mm, divided, max_mm, max_read, row_max, split_a, split_b, split_c, max_split,
             bias_mm, bias_in, rec_done) = loop_sems = [sem(n) for n in (
                "v_in", "qk_mm", "exp_done", "av_mm", "av_read", "fold_mm", "divided", "max_mm", "max_read", "row_max", "split_a",
                "split_b", "split_c", "max_split", "bias_mm", "bias_in", "rec_done")]

            def max_items(i):
                length = (i + 1) * P
                full, tail = length // (2 * BANK), length % (2 * BANK)
                items = [[(e, u * 2 * BANK, 2 * BANK)] for u in range(full) for e in range(NE)]
                if tail > BANK:
                    items += [[(e, full * 2 * BANK, tail)] for e in range(NE)]
                elif tail:
                    items += [[(e, full * 2 * BANK, tail), (e + 1, full * 2 * BANK, tail)] for e in range(0, NE, 2)]
                return items, full + (tail > 0)

            LAG_AV, LAG_READ, LAG_FOLD, LAG_BIAS = 3, 4, 8, 6
            blocks = [(i, j) for i in range(TILES) for j in range(i + 1)]
            first = {i: i * (i + 1) // 2 for i in range(TILES + 1)}
            steps = []
            max_at = [len(max_items(i)[0]) for i in range(TILES)]
            max_queue = [(i, k, sum(w for _, _, w in max_items(i)[0][k]) / BANK) for i in range(TILES) for k in range(max_at[i])]
            LEAD = 44

            row_ready = {}
            k_now = 0
            biased = 0

            def next_max():
                i, k, work = max_queue.pop(0)
                steps.append(("max", i, k))
                if k == max_at[i] - 1:
                    steps.append(("rowmax", i, 0))
                    row_ready[i] = k_now
                return work

            pending = {}
            def at_slot(k, step):
                pending.setdefault(k, []).append(step)
            for i in range(TILES):
                end = first[i + 1] - 1
                for g in range(0, i + 1, 4):
                    at_slot(min(first[i] + g + 3, end) + LAG_AV, ("av", i, g))
                at_slot(end + LAG_READ, ("read", i, 0))
                next_end = first[min(i + 2, TILES)] - 1 if i + 1 < TILES else end + LAG_FOLD
                at_slot(min(end + LAG_FOLD, next_end + LAG_READ), ("fold", i, 0))
            ahead = 0.0
            while max_queue[0][0] < 2:
                ahead += next_max()
            total = len(blocks)
            order = {"fold": 0, "read": 1, "av": 2}
            for k in range(total + LAG_FOLD + 1):
                for s in sorted(pending.get(k, []), key=lambda s: (order[s[0]], s[1], s[2])):
                    steps.append(s)
                k_now = k
                while biased < TILES and (k == first[biased] or k >= row_ready.get(biased, k) + LAG_BIAS):
                    steps.append(("bias", biased, 0))
                    biased += 1
                if k < total:
                    i, j = blocks[k]
                    steps.append(("score", i, j))
                    goal = first[min(i + 2, TILES)] + (j + 1) * (min(i + 3, TILES) if i + 2 < TILES else 0) / (i + 1)
                    goal = min(goal, k + 1 + LEAD)
                    while max_queue and (ahead + 1 <= goal or (j == i and max_queue[0][0] <= i + 1)):
                        ahead += next_max()
            uses = [s for s in steps if s[0] in ("score", "bias", "fold")]
            bank_of = {s: n % RING for n, s in enumerate(uses)}
            use_before = {s: (uses[n - RING] if n >= RING else None) for n, s in enumerate(uses)}
            KPIECES = [(0, 16 * P), (16 * P, 32 * P), (32 * P, PADDED)]
            nblock = {b: n for n, b in enumerate(blocks)}
            nmaxes = {(i, k): sum(max_at[:i]) + k for i in range(TILES) for k in range(max_at[i])}
            av_groups = {}
            for s in steps:
                if s[0] == "av":
                    av_groups[(s[1], s[2])] = len(av_groups)
            group_of = {(i, j): av_groups[(i, j // 4 * 4)] for i, j in blocks}

            with nc.Block() as block:
                @block.sync
                def _(sp):
                    def load_keys(head_row, piece):
                        c0, c1 = KPIECES[piece]
                        for k in range(3):
                            r0 = (0, 3 * HD, 5 * HD)[k]
                            sp.dma_start(keys[r0:r0 + (3 - k) * HD, c0:c1],
                                         keys_dram[0:3 - k, bass.ds(head_row, HD), c0:c1]).then_inc(k_in[piece], 16)

                    def load_queries(head_row, g):
                        w = min(BANK, PADDED - g * BANK)
                        for k in range(3):
                            r0 = (0, 3 * HD, 5 * HD)[k]
                            for c in range(3 - k):
                                sp.dma_start(query[r0 + c * HD:r0 + (c + 1) * HD, g % QSLOTS, :, 0:w],
                                             queries_dram[k, bass.ds(head_row, HD), :, g * BANK:g * BANK + w])\
                                    .then_inc(q_in[g % QSLOTS], 16)

                    load_keys(0, 0)
                    load_queries(0, 0)
                    load_queries(0, 1)
                    load_keys(0, 1)
                    load_keys(0, 2)
                    with sp.Fori(0, TURNS) as h:
                        for g in range(2, QGROUPS + 2):
                            if g >= QSLOTS:
                                sp.wait_ge(qk_mm, first[4 * (g - QSLOTS + 1)])
                            if g < QGROUPS:
                                load_queries(h * HD, g)
                            else:
                                load_queries(h * HD + HD, g - QGROUPS)
                        for piece in range(3):
                            sp.wait_ge(qk_mm, first[TILES - 1] + KPIECES[piece][1] // P)
                            load_keys(h * HD + HD, piece)
                        sp.wait_ge(head_done, 4 * h + 4)
                        sp.sem_inc(turns, 1)
                        for s in loop_sems:
                            sp.sem_clear(s)
                        sp.sem_inc(heads_clear, 1)
                    for piece in range(3):
                        sp.wait_ge(k_in[piece], 48 * (TURNS + 1))
                    for g in range(2):
                        sp.wait_ge(q_in[g], 96 * (TURNS * QGROUPS // QSLOTS + 1))

                @block.gpsimd
                def _(pool):
                    nc.gpsimd.memset(keys[K6:P, :], 1.0).then_inc(prep, 1)
                    pool.wait_ge(prep, 1)
                    nc.gpsimd.memset(mpart[:, :, :], 0.0).then_inc(prep, 1)
                    nc.gpsimd.tensor_copy(identb[:, :], const("ident")).then_inc(prep, 1)
                    nc.gpsimd.tensor_copy(negs[:, :], const("neg_s")).then_inc(prep, 1)
                    for e in range(NE):
                        nc.gpsimd.tensor_copy(negt[:, e, :], const("neg_t")).then_inc(prep, 1)
                    pool.wait_ge(prep, 4 + NE)
                    with pool.Fori(0, TURNS) as h:
                        for c0, c1 in ((0, 4 * 32), (4 * 32, TILES * 32)):
                            nc.gpsimd.tensor_copy(vhead[:, c0:c1].unsqueeze(1), values[:, bass.ds(h, 1), c0:c1]).then_inc(v_in, 1)
                        for i in range(TILES):
                            diag = [mpart[:, i % 2, 4 * a:].rearrange("p c -> p c")[:, 0:3 * 33 + 1:33] for a in range(3)]
                            pool.wait_ge(row_max, i + 1)
                            if i >= 2:
                                pool.wait_ge(bias_mm, i - 1)
                            nc.gpsimd.tensor_copy(diag[0], nmax[:, i % 2, :]).then_inc(split_a, 1)
                            pool.wait_ge(split_a, i + 1)
                            nc.gpsimd.tensor_tensor(mrest[:, :], nmax[:, i % 2, :], diag[0], ALU.subtract).then_inc(split_b, 1)
                            pool.wait_ge(split_b, i + 1)
                            nc.gpsimd.tensor_copy(diag[1], mrest[:, :]).then_inc(split_c, 1)
                            pool.wait_ge(split_c, i + 1)
                            nc.gpsimd.tensor_tensor(diag[2], mrest[:, :], diag[1], ALU.subtract).then_inc(max_split, 1)
                        pool.wait_ge(max_split, TILES)
                        pool.sem_inc(head_done, 1)
                        pool.wait_ge(heads_clear, h + 1)

                @block.scalar
                def _(act):
                    with act.Fori(0, TURNS) as h:
                        for kind, i, j in steps:
                            if kind == "score":
                                n = nblock[(i, j)]
                                act.wait_ge(qk_mm, n + 1)
                                if n >= NP:
                                    act.wait_ge(av_mm, group_of[blocks[n - NP]] + 1)
                                nc.scalar.activation(prob[:, n % NP, :], ps_ring[bank_of[(kind, i, j)]][:, :], ACT.Exp).then_inc(exp_done, 1)
                            elif kind == "bias":
                                act.wait_ge(bias_mm, i + 1)
                                nc.scalar.activation(query[K6:KM, i // 4 % QSLOTS, :, i % 4 * P:(i % 4 + 1) * P],
                                                     ps_ring[bank_of[(kind, i, j)]][K6:KM, :].rearrange("p (e s) -> p e s", e=NE), ACT.Copy).then_inc(bias_in, 1)
                            elif kind == "read":
                                act.wait_ge(av_mm, av_groups[(i, i // 4 * 4)] + 1)
                                if i >= 1:
                                    act.wait_ge(fold_mm, i)
                                k = min(P, 32 * (i + 1))
                                nc.scalar.activation(osum[0:k, :], ps_av[0:k, :], ACT.Copy).then_inc(av_read, 1)
                        act.wait_ge(av_read, TILES)
                        act.wait_ge(exp_done, total)
                        act.wait_ge(divided, TILES)
                        act.sem_inc(head_done, 1)
                        act.wait_ge(heads_clear, h + 1)

                @block.vector
                def _(dve):
                    with dve.Fori(0, TURNS) as h:
                        for kind, i, j in steps:
                            if kind == "max":
                                n = nmaxes[(i, j)]
                                items, parts = max_items(i)
                                pieces = items[j]
                                e0, key0, w = pieces[0]
                                dve.wait_ge(max_mm, n + 1)
                                src = ps_max[n % 2][:, 0:w] if len(pieces) == 1 else \
                                    ps_max[n % 2][:, :].rearrange("p (a c) -> p a c", a=2)[:, :, 0:w]
                                u = key0 // (2 * BANK)
                                if len(pieces) == 1:
                                    dst = pmax[:, i % 2, e0, u:u + 1]
                                else:
                                    dst = pmax[:, i % 2, e0:e0 + 2, u]
                                nc.vector.tensor_reduce(dst, src, AX.X, ALU.max).then_inc(max_read, 1)
                            elif kind == "rowmax":
                                parts = max_items(i)[1]
                                dve.wait_ge(max_read, nmaxes[(i, max_at[i] - 1)] + 1)
                                if i >= 2:
                                    dve.wait_ge(max_split, i - 1)
                                nc.vector.tensor_reduce(nmax[:, i % 2, :], pmax[:, i % 2, :, 0:parts], AX.X, ALU.max, negate=True)\
                                    .then_inc(row_max, 1)
                            elif kind == "fold":
                                dve.wait_ge(fold_mm, i + 1)
                                o = ps_ring[bank_of[(kind, i, j)]][:, 0:NE * 32].rearrange("p (e f) -> p e f", e=NE)
                                nc.vector.reciprocal(rden[:, :], o[:, :, HD]).then_inc(rec_done, 1)
                                dve.wait_ge(rec_done, i + 1)
                                nc.vector.tensor_tensor(
                                    attn[:, i, bass.ds(h, 1), :].rearrange("p a (e f) -> p (a e) f", e=NE), o[:, :, 0:HD],
                                    rden[:, :].unsqueeze(2).to_broadcast([P, NE, HD]), ALU.mult).then_inc(divided, 1)
                        dve.wait_ge(row_max, TILES)
                        dve.wait_ge(divided, TILES)
                        dve.sem_inc(head_done, 1)
                        dve.wait_ge(heads_clear, h + 1)

                @block.tensor
                def _(pe):
                    pe.wait_ge(prep, 4 + NE)
                    with pe.Fori(0, TURNS) as h:
                        loaded = -1
                        for step in steps:
                            kind, i, j = step
                            slot, s = i // 4 % QSLOTS, slice(i % 4 * P, (i % 4 + 1) * P)
                            if kind in ("score", "bias", "fold"):
                                bank = ps_ring[bank_of[step]]
                                before = use_before[step]
                                if before:
                                    if before[0] == "score":
                                        pe.wait_ge(exp_done, nblock[before[1:]] + 1)
                                    else:
                                        pe.wait_ge(bias_in if before[0] == "bias" else divided, before[1] + 1)
                            if kind == "max":
                                n = nmaxes[(i, j)]
                                if i // 4 > loaded:
                                    loaded = i // 4
                                    pe.wait_ge(q_in[slot], 96 * (QGROUPS // QSLOTS) * h + 96 * (loaded // QSLOTS + 1))
                                if j == 0 and i * P in [c0 for c0, _ in KPIECES]:
                                    pe.wait_ge(k_in[[c0 for c0, _ in KPIECES].index(i * P)], 48 * h + 48)
                                if n >= 2:
                                    pe.wait_ge(max_read, n - 1)
                                for a, (e, key0, w) in enumerate(max_items(i)[0][j]):
                                    for c in range(0, w, BANK):
                                        cw = min(BANK, w - c)
                                        diag = key0 + c + cw == (i + 1) * P
                                        o = ps_max[n % 2][:, a * BANK + c:a * BANK + c + cw]
                                        last = nc.tensor.matmul(o, query[0:K6, slot, e, s], keys[0:K6, key0 + c:key0 + c + cw],
                                                                start=True, stop=not diag)
                                        if diag:
                                            last = nc.tensor.matmul(o[:, cw - P:cw], identb[:, :], negs[:, :], start=False, stop=True)
                                last.then_inc(max_mm, 1)
                            elif kind == "bias":
                                pe.wait_ge(max_split, i + 1)
                                for e in range(NE):
                                    last = nc.tensor.matmul(bank[K6:K6 + 32, e * P:(e + 1) * P], mpart[:, i % 2, e * 32:(e + 1) * 32],
                                                            identb[:, :], start=True, stop=True)
                                last.then_inc(bias_mm, 1)
                            elif kind == "score":
                                n = nblock[(i, j)]
                                if j == 0:
                                    pe.wait_ge(bias_in, i + 1)
                                o = bank[:, :].rearrange("p (e s) -> p e s", e=NE)
                                last = nc.tensor.matmul(o, keys[0:KM, j * P:(j + 1) * P], query[0:KM, slot, :, s], start=True, stop=(j < i))
                                if j == i:
                                    last = nc.tensor.matmul(o, identb[:, :], negt[:, :, :], start=False, stop=True)
                                last.then_inc(qk_mm, 1)
                            elif kind == "av":
                                hi = min(j + 3, i)
                                pe.wait_ge(exp_done, nblock[(i, hi)] + 1)
                                if j == 0 and i >= 1:
                                    pe.wait_ge(av_read, i)
                                if (i, j) in ((0, 0), (4, 4)):
                                    pe.wait_ge(v_in, 1 + (i > 0))
                                for jj in range(j, hi + 1):
                                    q = jj % 4
                                    last = nc.tensor.matmul(ps_av[32 * q:32 * q + 32, :], vhead[:, jj * 32:(jj + 1) * 32],
                                                            prob[:, nblock[(i, jj)] % NP, :], start=(jj < 4), stop=(jj + 4 > i))
                                last.then_inc(av_mm, 1)
                            elif kind == "fold":
                                pe.wait_ge(av_read, i + 1)
                                k = min(P, 32 * (i + 1))
                                for e in range(NE):
                                    last = nc.tensor.matmul(bank[:, e * 32:(e + 1) * 32], osum[0:k, e * P:(e + 1) * P],
                                                            const("fold", 0, k), start=True, stop=True)
                                last.then_inc(fold_mm, 1)
                        pe.wait_ge(divided, TILES)
                        pe.sem_inc(head_done, 1)
                        pe.wait_ge(heads_clear, h + 1)

        with ExitStack() as st:
            nz = sb(st, "nz", [P, TILES, P])
            gT = sb(st, "gT", [P, 2, BANK])
            gate = sb(st, "gate_w", [P, TILES, HEADS * NE])
            gsum = sb(st, "gsum", [P, 2, TILES * HEADS])
            mix = sb(st, "mix", [P, TILES, P])
            prodg = sb(st, "prodg", [P, 1, TILES, NE * HD])
            stat = sb(st, "stat5", [P, 4, TILES * HEADS])
            ps = [pb(st, f"ps5_{k}", [P, BANK]) for k in range(8)]
            fT = values[:, 0:4, :].rearrange("p h c -> p (h c)")
            hT = values[:, 4:8, :].rearrange("p h c -> p (h c)")
            flat = lambda a: a[:, :, :].rearrange("p i f -> p (i f)")
            G = TILES * HEADS
            g16 = lambda a: a[:, :, :].rearrange("p i (g d) -> p (i g) d", d=HD)
            (g_masked, gt_mm, gt_sb, gl_mm, g_sub, g_exp, fn_done, ft_mm, ft_sb, f1_mm, f1_relu, f1_done, f2_mm, fout_done, fo_mm, fo_sb,
             fg_mm, fg_sub, fg_exp, final, stored) = (sem(n) for n in (
                "g_masked", "gt_mm", "gt_sb", "gl_mm", "g_sub", "g_exp", "fn_done", "ft_mm", "ft_sb", "f1_mm", "f1_relu", "f1_done", "f2_mm",
                "fout_done", "fo_mm", "fo_sb", "fg_mm", "fg_sub", "fg_exp", "final", "stored"))
            f2_read = sem("f2_read")
            ln3 = [sem("ln3_" + n) for n in names]
            ln4 = [sem("ln4_" + n) for n in names]
            own = Chain("ffn_vector")
            scratch = attn[:, :, :, :].rearrange("p h i f -> p (h i f)")
            cent = scratch[:, 0:PADDED].rearrange("p (g d) -> p g d", d=HD)
            work = scratch[:, PADDED:2 * PADDED].rearrange("p (g d) -> p g d", d=HD)
            NTP = (TILES + 15) // 16

            def broad(row):
                return row.unsqueeze(1).to_broadcast([P, G, HD])

            with nc.Block() as block:
                @block.vector
                def _(dve):
                    own(dve, nc.vector.tensor_scalar(flat(nz), flat(sx_tok), 0.0, None, ALU.not_equal))
                    for h in range(HEADS):
                        a = attn[:, :, h, :].rearrange("p i (e d) -> p i e d", e=NE)
                        own(dve, nc.vector.tensor_tensor(
                            a, a, nz[:, :, h * HD:(h + 1) * HD].unsqueeze(2).to_broadcast([P, TILES, NE, HD]), ALU.mult))
                    nc.vector.memset(stat[:, 3, 0:1], 0.0).then_inc(g_masked, 1)
                    dve.wait_ge(gl_mm, TILES)
                    for k in range(NTP):
                        nt = min(16, TILES - 16 * k)
                        own(dve, nc.vector.tensor_tensor(
                            gate[:, 16 * k:16 * k + nt, :], ps[2 + k][:, 0:32 * nt].rearrange("p (i c) -> p i c", c=32),
                            const("gate_b").unsqueeze(1).to_broadcast([P, nt, 32]), ALU.add))
                    gate4 = gate[:, :, :].rearrange("p i (g e) -> p (i g) e", e=NE)
                    own(dve, nc.vector.tensor_reduce(gsum[:, 0, :], gate4, AX.X, ALU.max))
                    nc.vector.tensor_tensor(gate4, gate4, gsum[:, 0, :].unsqueeze(2).to_broadcast([P, G, NE]), ALU.subtract).then_inc(g_sub, 1)
                    dve.wait_ge(g_exp, 1)
                    own(dve, nc.vector.tensor_reduce(gsum[:, 1, :], gate4, AX.X, ALU.add))
                    own(dve, nc.vector.reciprocal(gsum[:, 1, :], gsum[:, 1, :]))
                    own(dve, nc.vector.tensor_tensor(gate4, gate4, gsum[:, 1, :].unsqueeze(2).to_broadcast([P, G, NE]), ALU.mult))
                    for h in range(HEADS):
                        a = attn[:, :, h, :].rearrange("p i (e d) -> p i e d", e=NE)
                        own(dve, nc.vector.tensor_tensor(
                            prodg[:, 0, :, :].rearrange("p i (e d) -> p i e d", e=NE), a,
                            gate[:, :, h * NE:(h + 1) * NE].unsqueeze(3).to_broadcast([P, TILES, NE, HD]), ALU.mult))
                        own(dve, nc.vector.tensor_reduce(mix[:, :, h * HD:(h + 1) * HD],
                                                         prodg[:, 0, :, :].rearrange("p i (e d) -> p i d e", e=NE), AX.X, ALU.add))
                    for b in range(BATCH):
                        for n0, n1 in ((0, 1), (1, NH)):
                            m = mix[:, :, (b * NH + n0) * HD:(b * NH + n1) * HD]
                            src = min(n0, BATCH - 1) * NH
                            own(dve, nc.vector.tensor_tensor(m, m, sx_tok[:, :, (src + n0) * HD:(src + n1) * HD], ALU.add))
                    normalise_vector(dve, own, g16(mix), cent, work, stat, G, HD, FFN_EPS, *ln3)
                    own(dve, nc.vector.tensor_tensor(cent, cent, broad(const("ln_g")), ALU.mult))
                    nc.vector.tensor_tensor(g16(mix), cent, broad(const("ln_b")), ALU.add).then_inc(fn_done, 1)
                    for c, (c0, w) in enumerate(CHUNKS):
                        dve.wait_ge(f1_relu, c + 1)
                        nc.vector.scalar_tensor_tensor(hT[:, c0:c0 + w], fT[:, c0:c0 + w], 0.0, hT[:, c0:c0 + w],
                                                       ALU.not_equal, ALU.mult).then_inc(f1_done, 1)
                    c3 = cent.rearrange("p (i g) d -> p i (g d)", i=TILES)
                    for c, (c0, w) in enumerate(CHUNKS):
                        dve.wait_ge(f2_mm, c + 1)
                        i0, nt = c0 // P, w // P
                        cc = c3[:, i0:i0 + nt, :]
                        nc.vector.tensor_tensor(cc, ps[c % 2][:, 0:w].rearrange("p (i f) -> p i f", f=P),
                                                const("fc2_b").unsqueeze(1).to_broadcast([P, nt, P]), ALU.add).then_inc(f2_read, 1)
                    dve.wait_ge(f2_read, len(CHUNKS))
                    own(dve, nc.vector.scalar_tensor_tensor(cent, g16(mix), 0.0, cent, ALU.not_equal, ALU.mult))
                    own(dve, nc.vector.tensor_tensor(g16(mix), cent, g16(mix), ALU.add))
                    normalise_vector(dve, own, g16(mix), cent, work, stat, G, HD, FFN_EPS, *ln4)
                    own(dve, nc.vector.tensor_tensor(cent, cent, broad(const("fn_g")), ALU.mult))
                    nc.vector.tensor_tensor(g16(mix), cent, broad(const("fn_b")), ALU.add).then_inc(fout_done, 1)
                    dve.wait_ge(fg_mm, TILES)
                    lg = ps[2][:, 0:G].rearrange("p (g n) -> p g n", n=NH)
                    own(dve, nc.vector.tensor_reduce(stat[:, 0, 0:GROUPS], lg, AX.X, ALU.max))
                    fgv = gsum[:, 0, :].rearrange("p (g n) -> p g n", n=NH)
                    nc.vector.tensor_tensor(fgv, lg, stat[:, 0, 0:GROUPS].unsqueeze(2).to_broadcast([P, GROUPS, NH]), ALU.subtract)\
                        .then_inc(fg_sub, 1)
                    dve.wait_ge(fg_exp, 1)
                    own(dve, nc.vector.tensor_reduce(stat[:, 1, 0:GROUPS], fgv, AX.X, ALU.add))
                    own(dve, nc.vector.reciprocal(stat[:, 1, 0:GROUPS], stat[:, 1, 0:GROUPS]))
                    own(dve, nc.vector.tensor_tensor(fgv, fgv, stat[:, 1, 0:GROUPS].unsqueeze(2).to_broadcast([P, GROUPS, NH]), ALU.mult))
                    own(dve, nc.vector.tensor_tensor(g16(mix), g16(mix), gsum[:, 0, :].unsqueeze(2).to_broadcast([P, G, HD]), ALU.mult))
                    nc.vector.tensor_tensor(flat(mix), flat(mix), flat(hid), ALU.add).then_inc(final, 1)

                @block.tensor
                def _(pe):
                    pe.wait_ge(g_masked, 1)
                    for i in range(TILES + 1):
                        if i < TILES:
                            if i >= 2:
                                pe.wait_ge(gt_sb, i - 1)
                            for p in range(NE):
                                last = nc.tensor.transpose(ps[i % 2][:, p * P:(p + 1) * P], attn[:, i, 2 * p:2 * p + 2, :].rearrange("p h f -> p (h f)"), const("ident"))
                            last.then_inc(gt_mm, 1)
                        if i >= 1:
                            j = i - 1
                            pe.wait_ge(gt_sb, j + 1)
                            for p in range(NE):
                                c = 32 * (j % 16) + 8 * p
                                last = nc.tensor.matmul(ps[2 + j // 16][:, c:c + 8], gT[:, j % 2, p * P:(p + 1) * P],
                                                        const("gate", 0, P, 8 * (p % 2), 8 * (p % 2) + 8), start=True, stop=True)
                            last.then_inc(gl_mm, 1)
                    pe.wait_ge(fn_done, 1)
                    for c, (c0, w) in enumerate(CHUNKS):
                        if c >= 2:
                            pe.wait_ge(ft_sb, c - 1)
                        for t in range(w // P):
                            last = nc.tensor.transpose(ps[c % 2][:, t * P:(t + 1) * P], mix[:, c0 // P + t, :], const("ident"))
                        last.then_inc(ft_mm, 1)
                    for c, (c0, w) in enumerate(CHUNKS):
                        pe.wait_ge(ft_sb, c + 1)
                        if c >= 2:
                            pe.wait_ge(f1_relu, c - 1)
                        nc.tensor.matmul(ps[2 + c % 2][:, 0:w], const("fc1"), fT[:, c0:c0 + w], start=True, stop=True).then_inc(f1_mm, 1)
                    for c, (c0, w) in enumerate(CHUNKS):
                        pe.wait_ge(f1_done, c + 1)
                        if c >= 2:
                            pe.wait_ge(f2_read, c - 1)
                        for t in range(w // P):
                            last = nc.tensor.matmul(ps[c % 2][:, t * P:(t + 1) * P], hT[:, c0 + t * P:c0 + (t + 1) * P], const("fc2"),
                                                    start=True, stop=True)
                        last.then_inc(f2_mm, 1)
                    pe.wait_ge(fout_done, 1)
                    for c, (c0, w) in enumerate(CHUNKS):
                        if c >= 2:
                            pe.wait_ge(fo_sb, c - 1)
                        for t in range(w // P):
                            last = nc.tensor.transpose(ps[c % 2][:, t * P:(t + 1) * P], mix[:, c0 // P + t, :], const("ident"))
                        last.then_inc(fo_mm, 1)
                    for i in range(TILES):
                        pe.wait_ge(fo_sb, i // 4 + 1)
                        nc.tensor.matmul(ps[2][:, i * 8:(i + 1) * 8], fT[:, i * P:(i + 1) * P], const("fgate"), start=True, stop=True)\
                            .then_inc(fg_mm, 1)

                @block.scalar
                def _(act):
                    for i in range(TILES):
                        act.wait_ge(gt_mm, i + 1)
                        if i >= 2:
                            act.wait_ge(gl_mm, i - 1)
                        nc.scalar.activation(gT[:, i % 2, :], ps[i % 2][:, :], ACT.Copy).then_inc(gt_sb, 1)
                    act.wait_ge(g_sub, 1)
                    nc.scalar.activation(flat(gate), flat(gate), ACT.Exp).then_inc(g_exp, 1)
                    normalise_scalar(act, cent, work, stat, G, *ln3)
                    for c, (c0, w) in enumerate(CHUNKS):
                        act.wait_ge(ft_mm, c + 1)
                        nc.scalar.activation(fT[:, c0:c0 + w], ps[c % 2][:, 0:w], ACT.Copy).then_inc(ft_sb, 1)
                    for c, (c0, w) in enumerate(CHUNKS):
                        act.wait_ge(f1_mm, c + 1)
                        nc.scalar.activation(hT[:, c0:c0 + w], ps[2 + c % 2][:, 0:w], ACT.Relu, bias=const("fc1_b")).then_inc(f1_relu, 1)
                    normalise_scalar(act, cent, work, stat, G, *ln4)
                    for c, (c0, w) in enumerate(CHUNKS):
                        act.wait_ge(fo_mm, c + 1)
                        nc.scalar.activation(fT[:, c0:c0 + w], ps[c % 2][:, 0:w], ACT.Copy).then_inc(fo_sb, 1)
                    act.wait_ge(fg_sub, 1)
                    nc.scalar.activation(gsum[:, 0, :], gsum[:, 0, :], ACT.Exp).then_inc(fg_exp, 1)

                @block.sync
                def _(sp):
                    sp.wait_ge(final, 1)
                    for b in range(BATCH):
                        f = slice(b * FEAT, (b + 1) * FEAT)
                        sp.dma_start(out[b, 0:IMAGE, :].rearrange("(i p) f -> p i f", p=P), mix[:, 0:TILES - 1, f]).then_inc(stored, 16)
                        sp.dma_start(out[b, IMAGE:TOKENS, :], mix[0:TEXT, TILES - 1, f]).then_inc(stored, 16)
                    sp.wait_ge(stored, 16 * 2 * BATCH)


def pack_constants(w):
    c = np.zeros((P, PACKED), np.float32)

    def put(name, array, p0=0, c0=0):
        a = AT[name][0] + c0
        c[p0:p0 + array.shape[0], a:a + array.shape[1]] = array

    def diagonal(name, block, copies, c0=0):
        for k in range(copies):
            put(name, block, k * block.shape[0], c0 + k * block.shape[1])

    def row(name, vector):
        put(name, np.broadcast_to(vector[None, :], (P, vector.shape[0])))

    def column(name, vector, copies):
        put(name, np.tile(vector, copies)[:, None])

    diagonal("conv1", w["L0_tok_conv1_w"].T, BATCH)
    for k in range(TAPS):
        for b in range(BATCH):
            tap = np.broadcast_to(w["L0_tok_conv2_w"][k][:, None], (REDUCED, CH))
            put("conv2", tap, b * REDUCED, k * P + b * CH)
    for k, name in enumerate(("conv1_b", "bn_gamma", "bn_beta", "bn_mean", "bn_var")):
        put("bn", np.tile(w["L0_tok_" + name], BATCH)[:, None], 0, k)
    row("conv2_b", w["L0_tok_conv2_b"])
    for s in "kq":
        diagonal(s + "w1", w[f"L0_attn_{s}w1"].T, BATCH)
        column(s + "b1", w[f"L0_attn_{s}b1"], BATCH)
        diagonal(s + "w2", np.concatenate([w[f"L0_attn_{s}w2"].T] * 2, axis=1), BATCH)
        column(s + "b2", w[f"L0_attn_{s}b2"], 2 * BATCH)
    diagonal("vw", w["L0_attn_vw"].T, BATCH)
    row("vb", np.tile(w["L0_attn_vb"], BATCH))
    hl = w["L0_ffn_hl_w"].reshape(NH * HD, FEAT)
    diagonal("hl", hl.T, BATCH)
    column("hl_b", w["L0_ffn_hl_b"].reshape(-1), BATCH)
    for b in range(BATCH):
        for n in range(NH):
            r = (b * NH + n) * HD
            put("wk", w["L0_ffn_wk"][n].T, r, r)
            put("wv", w["L0_ffn_wv"][n].T, r, r)
            for e in range(NE):
                put("wq", w["L0_ffn_wq"][n, e].T, r, e * P + r)
    for n in range(NH):
        put("gate", w["L0_ffn_gate_w"][n].T, n % 2 * FEAT, n // 2 * 8 + n % 2 * NE)
    row("gate_b", np.tile(w["L0_ffn_gate_b"].reshape(-1), BATCH))
    row("ln_g", w["L0_ffn_ln_g"])
    row("ln_b", w["L0_ffn_ln_b"])
    diagonal("fc1", w["L0_ffn_fc1_w"].T, HEADS)
    column("fc1_b", w["L0_ffn_fc1_b"], HEADS)
    diagonal("fc2", w["L0_ffn_fc2_w"].T, HEADS)
    row("fc2_b", np.tile(w["L0_ffn_fc2_b"], HEADS))
    row("fn_g", w["L0_ffn_fnorm_g"])
    row("fn_b", w["L0_ffn_fnorm_b"])
    diagonal("fgate", w["L0_ffn_fgate_w"].T, BATCH)
    a = np.arange(P)
    put("ident", np.eye(P, dtype=np.float32))
    put("keep", (a[:, None] <= a[None, :]).astype(np.float32))
    put("neg_s", np.where(a[None, :] > a[:, None], NEG, 0.0).astype(np.float32))
    put("neg_t", np.where(a[:, None] > a[None, :], NEG, 0.0).astype(np.float32))
    pos = (a[:, None] + P * np.arange(TILES)[None, :] + 1).astype(np.float64)
    put("inv_norm", (1.0 / np.sqrt(pos * PHASES)).astype(np.float32))
    put("fold", (a[:, None] % 32 == np.arange(32)[None, :]).astype(np.float32))
    cosine = (a // PHASES % 2 == 1)
    put("phase", np.stack([np.where(cosine, -1.0, 1.0), np.where(cosine, -PI_BELOW, PI_BELOW),
                           np.where(cosine, np.pi / 2, 0.0)], axis=1).astype(np.float32))
    return c


def kernel(**inputs):
    import concourse.bacc as _bacc
    from concourse.bass_utils import run_bass_kernel_spmd as _run

    inputs = {k: np.ascontiguousarray(v) for k, v in inputs.items()}
    arrays = {"x_dram": inputs["x"], "txt_dram": inputs["txt"], "packed_dram": pack_constants(inputs)}
    nc = _bacc.Bacc("TRN2", target_bir_lowering=False, num_devices=1)
    args = [nc.dram_tensor(n, a.shape, mybir.dt.from_np(a.dtype), kind="ExternalInput").ap() for n, a in arrays.items()]
    out = nc.dram_tensor("out_dram", (BATCH, TOKENS, FEAT), mybir.dt.float32, kind="ExternalOutput").ap()
    build(nc, *args, out)
    r = _run(nc, [arrays], core_ids=[0])
    return r.results[0]["out_dram"]
```

```python
import numpy as np
import concourse.bass as bass
from concourse import mybir
from contextlib import ExitStack

BATCH, CH, ROWS, COLS, TEXT = 2, 64, 64, 64, 77
FEAT = 64
IMAGE = CH * ROWS
TOKENS = IMAGE + TEXT
P = 128
TILES = -(-TOKENS // P)
PADDED = TILES * P
TAPS = 9
REDUCED = 16
PHASES = 32
NH, NE, HD = 4, 4, 16
HEADS = BATCH * NH
TURNS = HEADS
BN_EPS, LN_EPS, FFN_EPS = 1e-5, 1e-5, 1e-8
BANK = 512
CHUNKS = [(c, min(BANK, PADDED - c)) for c in range(0, PADDED, BANK)]
NEG = -3.0e38
PI_BELOW = 3.1415925

WIDTHS = [
    ("conv1", 32), ("conv2", TAPS * P), ("bn", 5), ("conv2_b", TAPS),
    ("kw1", P), ("qw1", P), ("kb1", 1), ("qb1", 1), ("kw2", P), ("qw2", P), ("kb2", 1), ("qb2", 1),
    ("vw", P), ("vb", P), ("hl", P), ("hl_b", 1), ("wk", P), ("wq", NE * P), ("wv", P),
    ("gate", 16), ("gate_b", 32), ("ln_g", HD), ("ln_b", HD), ("fc1", P), ("fc1_b", 1), ("fc2", P),
    ("fc2_b", P), ("fn_g", HD), ("fn_b", HD), ("fgate", 8),
    ("ident", P), ("keep", P), ("neg_s", P), ("neg_t", P), ("inv_norm", TILES), ("phase", 3),
]
AT, _n = {}, 0
for _name, _w in WIDTHS:
    AT[_name] = (_n, _n + _w)
    _n += _w
PACKED = _n


def build(nc, x, txt, packed, out):
    fp32, bf16 = mybir.dt.float32, mybir.dt.bfloat16
    ALU, ACT, AX = mybir.AluOpType, mybir.ActivationFunctionType, mybir.AxisListType
    top = ExitStack()

    def sem(name):
        return top.enter_context(nc.semaphore(name))

    tokens_dram = nc.dram_tensor("tokens_scratch", [BATCH, IMAGE, FEAT], fp32, kind="Internal").ap()
    keys_dram = nc.dram_tensor("keys_scratch", [3, P + HD, PADDED], bf16, kind="Internal").ap()
    queries_dram = nc.dram_tensor("queries_scratch", [3, P + HD, NE, PADDED], bf16, kind="Internal").ap()

    with top:
        def sb(stack, name, shape, dt=fp32):
            return stack.enter_context(nc.sbuf_tensor(name, shape, dt))

        def pb(stack, name, shape, dt=fp32):
            return stack.enter_context(nc.psum_tensor(name, shape, dt))

        con = sb(top, "con", [P, PACKED])
        hid = sb(top, "hid", [P, TILES, BATCH * FEAT])

        def const(name, p0=0, p1=P, c0=0, c1=None):
            a, b = AT[name]
            return con[p0:p1, a + c0:(b if c1 is None else a + c1)]

        class Chain:
            def __init__(self, name):
                self.sem, self.n = sem(name), 0

            def __call__(self, eng, ins):
                self.n += 1
                ins.then_inc(self.sem, 1)
                eng.wait_ge(self.sem, self.n)

        def normalise_vector(dve, chain, data, cent, work, stat, groups, width, eps, squares, centred, varred, rooted):
            def wide(s):
                return s.unsqueeze(2).to_broadcast([P, groups, width])
            chain(dve, nc.vector.tensor_reduce(stat[:, 0, 0:groups], data, AX.X, ALU.add))
            chain(dve, nc.vector.tensor_scalar(stat[:, 0, 0:groups], stat[:, 0, 0:groups], 1.0 / width, None, ALU.mult))
            chain(dve, nc.vector.tensor_tensor(cent, data, wide(stat[:, 0, 0:groups]), ALU.subtract))
            nc.vector.tensor_scalar(stat[:, 3, 0:1], stat[:, 0, 0:1], 0.0, None, ALU.mult).then_inc(centred, 1)
            dve.wait_ge(squares, 1)
            chain(dve, nc.vector.tensor_reduce(stat[:, 1, 0:groups], work, AX.X, ALU.add))
            nc.vector.tensor_scalar(stat[:, 1, 0:groups], stat[:, 1, 0:groups], 1.0 / width, eps, ALU.mult, ALU.add)\
                .then_inc(varred, 1)
            dve.wait_ge(rooted, 1)
            chain(dve, nc.vector.reciprocal(stat[:, 2, 0:groups], stat[:, 2, 0:groups]))
            chain(dve, nc.vector.tensor_tensor(cent, cent, wide(stat[:, 2, 0:groups]), ALU.mult))

        def normalise_scalar(act, cent, work, stat, groups, squares, centred, varred, rooted):
            act.wait_ge(centred, 1)
            nc.scalar.activation(work, cent, ACT.Square).then_inc(squares, 1)
            act.wait_ge(varred, 1)
            nc.scalar.activation(stat[:, 2, 0:groups], stat[:, 1, 0:groups], ACT.Sqrt).then_inc(rooted, 1)

        with ExitStack() as st:
            x_sb = sb(st, "x_sb", [P, ROWS * COLS])
            xpad = sb(st, "xpad", [P, ROWS + 2, COLS + 2])
            red = sb(st, "red", [BATCH * REDUCED, ROWS * COLS])
            acc = sb(st, "acc", [P, ROWS * COLS])
            prod = sb(st, "prod", [P, 4, BANK])
            bn = sb(st, "bn", [BATCH * REDUCED, 4])
            ps_red = [pb(st, f"ps_red{k}", [P, BANK]) for k in range(2)]
            ps_tap = [pb(st, f"ps_tap{k}", [P, BANK]) for k in range(4)]
            con_in, x_in, pad_zero, xpad_done = sem("con_in"), sem("x_in"), sem("pad_zero"), sem("xpad_done")
            bn_var, bn_root, bn_done = sem("bn_var"), sem("bn_root"), sem("bn_done")
            red_mm, red_done, tap_mm, tap_prod, tap_added = (sem(n) for n in ("red_mm", "red_done", "tap_mm", "tap_prod", "tap_added"))
            tok_out, hid_in, hid_zero = sem("tok_out"), sem("hid_in"), sem("hid_zero")
            own = Chain("tok_vector")
            NPX = ROWS * COLS // BANK
            R = BANK // COLS
            QR = BATCH * REDUCED
            with nc.Block() as block:
                @block.sync
                def _(sp):
                    sp.dma_start(x_sb[:, :], x.rearrange("b c h w -> (b c) (h w)")).then_inc(x_in, 16)
                    sp.dma_start(con[:, :], packed).then_inc(con_in, 16)
                    sp.wait_ge(hid_zero, 1)
                    sp.dma_start(hid[0:TEXT, TILES - 1, :].rearrange("p (b f) -> p b f", b=BATCH),
                                 txt.rearrange("b t f -> t b f")).then_inc(hid_in, 16)
                    tok_v = tokens_dram.rearrange("b (c h) w -> (b c) (h w)", c=CH)
                    for q in range(NPX):
                        sp.wait_ge(tap_added, q * TAPS + TAPS)
                        sp.dma_start(tok_v[:, q * BANK:(q + 1) * BANK], acc[:, q * BANK:(q + 1) * BANK]).then_inc(tok_out, 16)
                    sp.wait_ge(tok_out, 16 * NPX)
                    for b in range(BATCH):
                        sp.dma_start(hid[:, 0:TILES - 1, b * FEAT:(b + 1) * FEAT],
                                     tokens_dram[b].rearrange("(i p) f -> p i f", p=P)).then_inc(hid_in, 16)
                    sp.wait_ge(hid_in, 16 * (1 + BATCH))

                @block.tensor
                def _(pe):
                    pe.wait_ge(x_in, 16)
                    pe.wait_ge(con_in, 16)
                    for q in range(NPX):
                        if q >= 2:
                            pe.wait_ge(red_done, q - 1)
                        nc.tensor.matmul(ps_red[q % 2][0:QR, :], const("conv1"), x_sb[:, q * BANK:(q + 1) * BANK],
                                         start=True, stop=True).then_inc(red_mm, 1)
                    for q in range(NPX):
                        pe.wait_ge(red_done, q + 1)
                        for k in range(TAPS):
                            n = q * TAPS + k
                            if n >= 4:
                                pe.wait_ge(tap_prod, n - 3)
                            nc.tensor.matmul(ps_tap[n % 4][:, :], const("conv2", 0, QR, k * P, (k + 1) * P),
                                             red[:, q * BANK:(q + 1) * BANK], start=True, stop=True).then_inc(tap_mm, 1)

                @block.scalar
                def _(act):
                    act.wait_ge(x_in, 16)
                    act.wait_ge(pad_zero, 1)
                    nc.scalar.activation(xpad[:, 1:ROWS + 1, 1:COLS + 1],
                                         x_sb[:, :].rearrange("p (h w) -> p h w", h=ROWS), ACT.Copy).then_inc(xpad_done, 1)
                    act.wait_ge(bn_var, 1)
                    nc.scalar.activation(bn[:, 1:2], bn[:, 0:1], ACT.Sqrt).then_inc(bn_root, 1)
                    act.wait_ge(bn_done, 1)
                    for q in range(NPX):
                        act.wait_ge(red_mm, q + 1)
                        nc.scalar.activation(red[:, q * BANK:(q + 1) * BANK], ps_red[q % 2][0:QR, :], ACT.Relu,
                                             bias=bn[:, 3:4], scale=bn[:, 2:3]).then_inc(red_done, 1)

                @block.vector
                def _(dve):
                    nc.vector.memset(xpad[:, :, :], 0.0).then_inc(pad_zero, 1)
                    dve.wait_ge(con_in, 16)
                    b1, gamma, beta, mean, var = (const("bn", 0, QR, k, k + 1) for k in range(5))
                    nc.vector.tensor_scalar(bn[:, 0:1], var, BN_EPS, None, ALU.add).then_inc(bn_var, 1)
                    dve.wait_ge(bn_root, 1)
                    own(dve, nc.vector.reciprocal(bn[:, 2:3], bn[:, 1:2]))
                    own(dve, nc.vector.tensor_tensor(bn[:, 2:3], bn[:, 2:3], gamma, ALU.mult))
                    own(dve, nc.vector.tensor_tensor(bn[:, 3:4], b1, mean, ALU.subtract))
                    own(dve, nc.vector.tensor_tensor(bn[:, 3:4], bn[:, 3:4], bn[:, 2:3], ALU.mult))
                    nc.vector.tensor_tensor(bn[:, 3:4], bn[:, 3:4], beta, ALU.add).then_inc(bn_done, 1)
                    dve.wait_ge(xpad_done, 1)
                    for q in range(NPX):
                        for k in range(TAPS):
                            n = q * TAPS + k
                            dve.wait_ge(tap_mm, n + 1)
                            if n >= 4:
                                dve.wait_ge(tap_added, n - 3)
                            di, dj = k // 3, k % 3
                            nc.vector.scalar_tensor_tensor(
                                prod[:, n % 4, :].rearrange("p (r w) -> p r w", w=COLS),
                                ps_tap[n % 4][:, :].rearrange("p (r w) -> p r w", w=COLS), const("conv2_b", 0, P, k, k + 1),
                                xpad[:, q * R + di:q * R + di + R, dj:dj + COLS], ALU.add, ALU.mult).then_inc(tap_prod, 1)

                @block.gpsimd
                def _(pool):
                    nc.gpsimd.memset(hid[:, TILES - 1, :], 0.0).then_inc(hid_zero, 1)
                    for q in range(NPX):
                        a = acc[:, q * BANK:(q + 1) * BANK]
                        for k in range(TAPS):
                            n = q * TAPS + k
                            pool.wait_ge(tap_prod, n + 1)
                            if k == 0:
                                ins = nc.gpsimd.tensor_copy(a, prod[:, n % 4, :])
                            else:
                                pool.wait_ge(tap_added, n)
                                ins = nc.gpsimd.tensor_tensor(a, a, prod[:, n % 4, :], ALU.add)
                            ins.then_inc(tap_added, 1)

        HALF = BATCH * FEAT
        GROUPS = TILES * BATCH
        with ExitStack() as st:
            stat = sb(st, "stat", [P, 4, GROUPS])
            cent = sb(st, "cent", [P, TILES, HALF])
            work = sb(st, "work", [P, TILES, HALF])
            normT = sb(st, "normT", [P, PADDED])
            hkq = sb(st, "hkq", [P, 2, 2, BANK])
            feat = [sb(st, f"feat{k}", [P, PADDED]) for k in range(2)]
            fold_abs = [cent[:, :, :].rearrange("p i f -> p (i f)"), work[:, :, :].rearrange("p i f -> p (i f)")]
            ps = [pb(st, f"ps2_{k}", [P, BANK]) for k in range(8)]
            names = ("squares", "centred", "varred", "rooted")
            ln1 = [sem("ln1_" + n) for n in names]
            ln1_done, tr_mm, tr_done = sem("ln1_done"), sem("tr_mm"), sem("tr_done")
            l1_mm, l1_done, l2_mm, l2_done, abs_done, feat_done = (
                sem(n) for n in ("l1_mm", "l1_done", "l2_mm", "l2_done", "abs_done", "feat_done"))
            own = Chain("phase_vector")
            with nc.Block() as block:
                v3 = lambda a: a[:, :, :].rearrange("p i (b f) -> p (i b) f", b=BATCH)

                @block.vector
                def _(dve):
                    normalise_vector(dve, own, v3(hid), v3(cent), v3(work), stat, GROUPS, FEAT, LN_EPS, *ln1)
                    nc.vector.tensor_scalar(stat[:, 3, 0:1], stat[:, 0, 0:1], 0.0, None, ALU.mult).then_inc(ln1_done, 1)
                    for k in range(2):
                        dve.wait_ge(l2_done, 2 * len(CHUNKS))
                        nc.vector.scalar_tensor_tensor(fold_abs[k], feat[k][:, :], const("phase", 0, P, 0, 1), feat[k][:, :],
                                                       ALU.mult, ALU.max).then_inc(abs_done, 1)

                @block.tensor
                def _(pe):
                    pe.wait_ge(ln1_done, 1)
                    for c, (c0, w) in enumerate(CHUNKS):
                        if c >= 2:
                            pe.wait_ge(tr_done, c - 1)
                        for t in range(w // P):
                            last = nc.tensor.transpose(ps[c % 2][:, t * P:(t + 1) * P], cent[:, c0 // P + t, :], const("ident"))
                        last.then_inc(tr_mm, 1)
                    for c in range(len(CHUNKS) + 1):
                        if c < len(CHUNKS):
                            c0, w = CHUNKS[c]
                            pe.wait_ge(tr_done, c + 1)
                            for k, name in enumerate(("kw1", "qw1")):
                                n = 2 * c + k
                                if n >= 2:
                                    pe.wait_ge(l1_done, n - 1)
                                nc.tensor.matmul(ps[2 + k][:, 0:w], const(name), normT[:, c0:c0 + w], start=True, stop=True)\
                                    .then_inc(l1_mm, 1)
                        if c >= 1:
                            c0, w = CHUNKS[c - 1]
                            for k, name in enumerate(("kw2", "qw2")):
                                n = 2 * (c - 1) + k
                                pe.wait_ge(l1_done, n + 1)
                                if n >= 4:
                                    pe.wait_ge(l2_done, n - 3)
                                nc.tensor.matmul(ps[4 + n % 4][:, 0:w], const(name), hkq[:, (c - 1) % 2, k, 0:w],
                                                 start=True, stop=True).then_inc(l2_mm, 1)

                @block.scalar
                def _(act):
                    normalise_scalar(act, v3(cent), v3(work), stat, GROUPS, *ln1)
                    for c, (c0, w) in enumerate(CHUNKS):
                        act.wait_ge(tr_mm, c + 1)
                        nc.scalar.activation(normT[:, c0:c0 + w], ps[c % 2][:, 0:w], ACT.Copy).then_inc(tr_done, 1)
                    for c in range(len(CHUNKS) + 1):
                        if c < len(CHUNKS):
                            c0, w = CHUNKS[c]
                            for k, name in enumerate(("kb1", "qb1")):
                                n = 2 * c + k
                                act.wait_ge(l1_mm, n + 1)
                                if n >= 4:
                                    act.wait_ge(l2_mm, n - 3)
                                nc.scalar.activation(hkq[:, c % 2, k, 0:w], ps[2 + k][:, 0:w], ACT.Tanh, bias=const(name))\
                                    .then_inc(l1_done, 1)
                        if c >= 1:
                            c0, w = CHUNKS[c - 1]
                            for k, name in enumerate(("kb2", "qb2")):
                                n = 2 * (c - 1) + k
                                act.wait_ge(l2_mm, n + 1)
                                nc.scalar.activation(feat[k][:, c0:c0 + w], ps[4 + n % 4][:, 0:w], ACT.Tanh, bias=const(name))\
                                    .then_inc(l2_done, 1)
                    for k in range(2):
                        act.wait_ge(abs_done, k + 1)
                        nc.scalar.activation(feat[k][:, :], fold_abs[k], ACT.Sin, bias=const("phase", 0, P, 2, 3),
                                             scale=const("phase", 0, P, 1, 2)).then_inc(feat_done, 1)

            val = sb(st, "val", [P, 2, HALF])
            keyT = sb(st, "keyT", [P, 2, P])
            att = sb(st, "att", [P, 2, BATCH, P])
            state = sb(st, "state", [P, 2, HALF])
            v_mm, v_sb, kt_mm, kt_sb, a_mm, a_sb, m_mm, m_sb, o_mm, o_sb, st_zero = (
                sem(n) for n in ("v_mm", "v_sb", "kt_mm", "kt_sb", "a_mm", "a_sb", "m_mm", "m_sb", "o_mm", "o_sb", "st_zero"))
            ps_v, ps_kt, ps_a, ps_m, ps_o = ps[0], ps[1], (ps[2], ps[3]), (ps[4], ps[7]), (ps[5], ps[6])
            with nc.Block() as block:
                @block.tensor
                def _(pe):
                    for i in range(TILES + 1):
                        if i < TILES:
                            t = slice(i * P, (i + 1) * P)
                            if i >= 1:
                                pe.wait_ge(v_sb, i)
                                pe.wait_ge(kt_sb, i)
                                pe.wait_ge(a_sb, 2 * i)
                            nc.tensor.matmul(ps_v[:, 0:HALF], normT[:, t], const("vw"), start=True, stop=True).then_inc(v_mm, 1)
                            nc.tensor.transpose(ps_kt[:, 0:P], feat[0][:, t], const("ident")).then_inc(kt_mm, 1)
                            for b in range(BATCH):
                                r = slice(b * FEAT, (b + 1) * FEAT)
                                nc.tensor.matmul(ps_a[b][:, 0:P], feat[0][r, t], feat[1][r, t], start=True, stop=True)\
                                    .then_inc(a_mm, 1)
                        if i >= 1:
                            j = i - 1
                            t = slice(j * P, (j + 1) * P)
                            if j == 0:
                                pe.wait_ge(st_zero, 2)
                            else:
                                pe.wait_ge(m_sb, BATCH * j)
                            if j >= 2:
                                pe.wait_ge(o_sb, j - 1)
                            o = ps_o[j % 2][:, 0:HALF]
                            nc.tensor.matmul(o, feat[1][:, t], state[:, j % 2, :], start=True, stop=False)
                            pe.wait_ge(v_sb, j + 1)
                            pe.wait_ge(a_sb, 2 * j + 2)
                            for b in range(BATCH):
                                f = slice(b * FEAT, (b + 1) * FEAT)
                                last = nc.tensor.matmul(o[:, f], att[:, j % 2, b, :], val[:, j % 2, f], start=False, stop=(b == 1))
                            last.then_inc(o_mm, 1)
                            if j < TILES - 1:
                                pe.wait_ge(kt_sb, j + 1)
                                nc.tensor.matmul(ps_m[j % 2][:, 0:HALF], keyT[:, j % 2, :], val[:, j % 2, :], start=True,
                                                 stop=True).then_inc(m_mm, 1)

                @block.scalar
                def _(act):
                    for i in range(TILES):
                        act.wait_ge(kt_mm, i + 1)
                        if i >= 2:
                            act.wait_ge(m_mm, i - 1)
                        nc.scalar.activation(keyT[:, i % 2, :], ps_kt[:, 0:P], ACT.Copy).then_inc(kt_sb, 1)

                @block.vector
                def _(dve):
                    for k in range(2):
                        nc.vector.memset(state[:, k, :], 0.0).then_inc(st_zero, 1)
                    for i in range(TILES + 1):
                        if i < TILES:
                            dve.wait_ge(v_mm, i + 1)
                            if i >= 2:
                                dve.wait_ge(o_mm, i - 1)
                                dve.wait_ge(m_mm, i - 1)
                            nc.vector.tensor_tensor(val[:, i % 2, :], ps_v[:, 0:HALF], const("vb"), ALU.add).then_inc(v_sb, 1)
                            for b in range(BATCH):
                                dve.wait_ge(a_mm, 2 * i + b + 1)
                                nc.vector.tensor_tensor(att[:, i % 2, b, :], ps_a[b][:, 0:P], const("keep"), ALU.mult)\
                                    .then_inc(a_sb, 1)
                        if i >= 1:
                            j = i - 1
                            dve.wait_ge(o_mm, j + 1)
                            nc.vector.scalar_tensor_tensor(hid[:, j, :], ps_o[j % 2][:, 0:HALF], const("inv_norm", 0, P, j, j + 1),
                                                           hid[:, j, :], ALU.mult, ALU.add).then_inc(o_sb, 1)
                            if j < TILES - 1:
                                dve.wait_ge(m_mm, j + 1)
                                dve.wait_ge(m_sb, BATCH * j) if j else dve.wait_ge(st_zero, 2)
                                for b in range(BATCH):
                                    f = slice(b * FEAT, (b + 1) * FEAT)
                                    nc.vector.tensor_tensor(state[f, (j + 1) % 2, f], state[f, j % 2, f], ps_m[j % 2][f, f], ALU.add)\
                                        .then_inc(m_sb, 1)

        mid = top.enter_context(ExitStack())
        sx_tok = sb(mid, "sx_tok", [P, TILES, P])
        values = sb(mid, "values", [P, HEADS, TILES * 32])
        with ExitStack() as st:
            stat = sb(st, "stat3", [P, 4, GROUPS])
            cent = sb(st, "cent3", [P, TILES, HALF])
            work = sb(st, "work3", [P, TILES, HALF])
            normT = work[:, :, :].rearrange("p i f -> p (i f)")
            sxT = cent[:, :, :].rearrange("p i f -> p (i f)")
            part = sb(st, "part", [P, 2, 3, PADDED], bf16)
            rest = sb(st, "rest", [P, 3, BANK])
            ps = [pb(st, f"ps3_{k}", [P, BANK]) for k in range(8)]
            ln2 = [sem("ln2_" + n) for n in names]
            (ln2_done, tr2_mm, tr2_done, sx_mm, sx_done, sxt_mm, sxt_done, val_mm, val_done, val_zero, val_one,
             proj_mm, part1, rest1, part2, part3, part_out) = (sem(n) for n in (
                "ln2_done", "tr2_mm", "tr2_done", "sx_mm", "sx_done", "sxt_mm", "sxt_done", "val_mm", "val_done",
                "val_zero", "val_one", "proj_mm", "part1", "rest1", "part2", "part3", "part_out"))
            own = Chain("proj_vector")
            NC = len(CHUNKS)
            MATS = 1 + NE
            vals = values[:, :, :].rearrange("p h (i f) -> p h i f", f=32)
            with nc.Block() as block:
                @block.vector
                def _(dve):
                    normalise_vector(dve, own, v3(hid), v3(cent), v3(work), stat, GROUPS, FEAT, LN_EPS, *ln2)
                    nc.vector.tensor_scalar(stat[:, 3, 0:1], stat[:, 0, 0:1], 0.0, None, ALU.mult).then_inc(ln2_done, 1)
                    dve.wait_ge(val_one, HEADS)
                    for c, (c0, w) in enumerate(CHUNKS):
                        dve.wait_ge(sxt_mm, c + 1)
                        nc.vector.tensor_copy(sx_tok[:, :, :].rearrange("p i f -> p (i f)")[:, c0:c0 + w], ps[c % 2][:, 0:w])\
                            .then_inc(sxt_done, 1)
                        dve.wait_ge(val_mm, c + 1)
                        nt = w // P
                        for t in range(nt):
                            last = nc.vector.tensor_copy(
                                vals[:, :, c0 // P + t, 0:HD],
                                ps[2 + c % 2][:, t * P:(t + 1) * P].rearrange("p (h f) -> p h f", f=HD))
                        last.then_inc(val_done, 1)
                    for m in range(MATS):
                        for c, (c0, w) in enumerate(CHUNKS):
                            n = m * NC + c
                            dve.wait_ge(part1, n + 1)
                            if n >= 3:
                                dve.wait_ge(part3, n - 2)
                            nc.vector.scalar_tensor_tensor(rest[:, n % 3, 0:w], ps[4 + n % 4][:, 0:w], 1.0 if m == 0 else float(HD) ** 0.5,
                                                           part[:, m % 2, 0, c0:c0 + w], ALU.mult, ALU.subtract).then_inc(rest1, 1)

                @block.tensor
                def _(pe):
                    pe.wait_ge(ln2_done, 1)
                    for c, (c0, w) in enumerate(CHUNKS):
                        if c >= 2:
                            pe.wait_ge(tr2_done, c - 1)
                        for t in range(w // P):
                            last = nc.tensor.transpose(ps[c % 2][:, t * P:(t + 1) * P], cent[:, c0 // P + t, :], const("ident"))
                        last.then_inc(tr2_mm, 1)
                    pe.wait_ge(tr2_done, NC)
                    for c, (c0, w) in enumerate(CHUNKS):
                        if c >= 2:
                            pe.wait_ge(sx_done, c - 1)
                        nc.tensor.matmul(ps[2 + c % 2][:, 0:w], const("hl"), normT[:, c0:c0 + w], start=True, stop=True).then_inc(sx_mm, 1)
                    pe.wait_ge(sx_done, NC)
                    for c, (c0, w) in enumerate(CHUNKS):
                        if c >= 2:
                            pe.wait_ge(sxt_done, c - 1)
                            pe.wait_ge(val_done, c - 1)
                        for t in range(w // P):
                            last = nc.tensor.transpose(ps[c % 2][:, t * P:(t + 1) * P], sxT[:, c0 + t * P:c0 + (t + 1) * P], const("ident"))
                        last.then_inc(sxt_mm, 1)
                        for t in range(w // P):
                            last = nc.tensor.matmul(ps[2 + c % 2][:, t * P:(t + 1) * P], sxT[:, c0 + t * P:c0 + (t + 1) * P], const("wv"),
                                                    start=True, stop=True)
                        last.then_inc(val_mm, 1)
                    for m in range(MATS):
                        wt = const("wk") if m == 0 else const("wq", 0, P, (m - 1) * P, m * P)
                        for c, (c0, w) in enumerate(CHUNKS):
                            n = m * NC + c
                            if n >= 4:
                                pe.wait_ge(rest1, n - 3)
                            nc.tensor.matmul(ps[4 + n % 4][:, 0:w], wt, sxT[:, c0:c0 + w], start=True, stop=True).then_inc(proj_mm, 1)

                @block.scalar
                def _(act):
                    normalise_scalar(act, v3(cent), v3(work), stat, GROUPS, *ln2)
                    act.wait_ge(ln2_done, 1)
                    for c, (c0, w) in enumerate(CHUNKS):
                        act.wait_ge(tr2_mm, c + 1)
                        nc.scalar.activation(normT[:, c0:c0 + w], ps[c % 2][:, 0:w], ACT.Copy).then_inc(tr2_done, 1)
                    act.wait_ge(tr2_mm, NC)
                    for c, (c0, w) in enumerate(CHUNKS):
                        act.wait_ge(sx_mm, c + 1)
                        nc.scalar.activation(sxT[:, c0:c0 + w], ps[2 + c % 2][:, 0:w], ACT.Identity, bias=const("hl_b")).then_inc(sx_done, 1)
                    for m in range(MATS):
                        if m >= 2:
                            act.wait_ge(part_out, 32 * (m - 1))
                        for c in range(NC + 1):
                            if c < NC:
                                c0, w = CHUNKS[c]
                                n = m * NC + c
                                act.wait_ge(proj_mm, n + 1)
                                nc.scalar.activation(part[:, m % 2, 0, c0:c0 + w], ps[4 + n % 4][:, 0:w], ACT.Copy,
                                                     scale=1.0 if m == 0 else float(HD) ** 0.5).then_inc(part1, 1)
                            if c >= 1:
                                c0, w = CHUNKS[c - 1]
                                n = m * NC + c - 1
                                act.wait_ge(rest1, n + 1)
                                nc.scalar.activation(part[:, m % 2, 1, c0:c0 + w], rest[:, n % 3, 0:w], ACT.Copy).then_inc(part2, 1)

                @block.gpsimd
                def _(pool):
                    nc.gpsimd.memset(values[:, :, :], 0.0).then_inc(val_zero, 1)
                    pool.wait_ge(val_zero, 1)
                    for h in range(HEADS):
                        nc.gpsimd.memset(vals[:, h, :, HD:HD + 1], 1.0).then_inc(val_one, 1)
                    for m in range(MATS):
                        if m >= 2:
                            pool.wait_ge(part_out, 32 * (m - 1))
                        for c, (c0, w) in enumerate(CHUNKS):
                            n = m * NC + c
                            pool.wait_ge(part2, n + 1)
                            nc.gpsimd.tensor_tensor(part[:, m % 2, 2, c0:c0 + w], rest[:, n % 3, 0:w], part[:, m % 2, 1, c0:c0 + w],
                                                    ALU.subtract).then_inc(part3, 1)

                @block.sync
                def _(sp):
                    for m in range(MATS):
                        sp.wait_ge(part3, (m + 1) * NC)
                        dst = keys_dram if m == 0 else queries_dram[:, :, m - 1, :]
                        sp.dma_start(dst[:, 0:P, :].rearrange("a p t -> p a t"), part[:, m % 2, :, :]).then_inc(part_out, 16)
                        sp.dma_start(dst[:, P:P + HD, :].rearrange("a p t -> p a t"), part[0:HD, m % 2, :, :]).then_inc(part_out, 16)
                        sp.wait_ge(part_out, 32 * (m + 1))

        attn = sb(mid, "attn", [P, TILES, HEADS, NE * HD])
        K6 = 6 * HD
        KM = K6 + 3 * NE
        QSLOTS = 3
        QGROUPS = -(-TILES // 4)
        EARLY_KEYS = 8 * P
        RING = 4
        with ExitStack() as st:
            keys = sb(st, "keys", [P, PADDED], bf16)
            ahead = sb(st, "ahead", [P, EARLY_KEYS], bf16)
            query = sb(st, "query", [P, QSLOTS, NE, BANK], bf16)
            qlast = sb(st, "qlast", [P, NE, P], bf16)

            def queries_of(i):
                return qlast[:, :, :] if i == TILES - 1 else query[:, i // 4 % QSLOTS, :, i % 4 * P:(i % 4 + 1) * P]

            def load_order(g):
                if g == QGROUPS - 1:
                    return QSLOTS, 1, 1
                return g % QSLOTS, g // QSLOTS + 1, len(range(g % QSLOTS, QGROUPS - 1, QSLOTS))

            vhead = sb(st, "vhead", [P, TILES * 32])
            NP = 8
            prob = sb(st, "prob", [P, NP, BANK])
            osum = sb(st, "osum", [P, 2, BANK])
            identb = sb(st, "identb", [P, P], bf16)
            negs = sb(st, "negs", [P, P], bf16)
            negt = sb(st, "negt", [P, NE, P], bf16)
            pmax = sb(st, "pmax", [P, 2, NE, 8])
            nmax = sb(st, "nmax", [P, 2, NE])
            mrest = sb(st, "mrest", [P, NE])
            mpart = sb(st, "mpart", [P, 2, NE * 32], bf16)
            rden = sb(st, "rden", [P, NE])
            fsum = sb(st, "fsum", [P, NE, HD + 1])
            ps_max = [pb(st, f"ps_max{k}", [P, 2 * BANK]) for k in range(2)]
            ps_ring = [pb(st, f"ps_ring{k}", [P, BANK]) for k in range(RING)]

            prep, head_go, head_done, heads_clear = sem("prep"), sem("head_go"), sem("head_done"), sem("heads_clear")
            k_in = [sem(f"k_in{k}") for k in range(3)]
            q_in = [sem(f"q_in{k}") for k in range(QSLOTS + 1)]
            turns, n_in = sem("turns"), sem("n_in")
            (v_in, qk_mm, exp_done, av_mm, av_read, fold_mm, divided, max_mm, max_read, row_max, split_a, split_b, split_c, max_split,
             bias_mm, bias_in, rec_done, sum_done) = loop_sems = [sem(n) for n in (
                "v_in", "qk_mm", "exp_done", "av_mm", "av_read", "fold_mm", "divided", "max_mm", "max_read", "row_max", "split_a",
                "split_b", "split_c", "max_split", "bias_mm", "bias_in", "rec_done", "sum_done")]

            def max_items(i):
                length = (i + 1) * P
                full, tail = length // (2 * BANK), length % (2 * BANK)
                items = [[(e, u * 2 * BANK, 2 * BANK)] for u in range(full) for e in range(NE)]
                if tail > BANK:
                    items += [[(e, full * 2 * BANK, tail)] for e in range(NE)]
                elif tail:
                    items += [[(e, full * 2 * BANK, tail), (e + 1, full * 2 * BANK, tail)] for e in range(0, NE, 2)]
                return items, full + (tail > 0)

            EARLY = EARLY_KEYS // P
            LAG_AV, LAG_READ, LAG_FOLD, LAG_BIAS = 3, 4, 8, 5
            blocks = [(i, j) for i in range(TILES) for j in range(i + 1)]
            first = {i: i * (i + 1) // 2 for i in range(TILES + 1)}
            total = len(blocks)
            KPIECES = [(0, 16 * P), (16 * P, 32 * P), (32 * P, PADDED)]
            nblock = {b: n for n, b in enumerate(blocks)}

            class Plan:
                def __init__(self, rows, with_weights):
                    self.rows, self.steps = rows, []
                    self.order = {row: n for n, row in enumerate(rows)}
                    queue = [(row, k, sum(w for _, _, w in items) / BANK)
                             for row in rows for k, items in enumerate(max_items(row[0])[0])]
                    self.max_number = {(row, k): n for n, (row, k, _) in enumerate(queue)}
                    work = sum(w for _, _, w in queue)
                    ready, biased, done = {}, 0, 0.0

                    def maxima(k, goal):
                        nonlocal done
                        while queue and done < goal:
                            row, item, w = queue.pop(0)
                            done += w
                            self.steps.append(("max", row[0], item, row[1]))
                            if not queue or queue[0][0] != row:
                                self.steps.append(("rowmax", row[0], 0, row[1]))
                                ready[row] = k

                    def bias(k):
                        nonlocal biased
                        while biased < len(rows) and rows[biased] in ready and k >= ready[rows[biased]] + LAG_BIAS:
                            self.steps.append(("bias", rows[biased][0], 0, rows[biased][1]))
                            biased += 1

                    if with_weights:
                        pending, fold_at = {}, {}
                        for i in range(TILES):
                            end = first[i + 1] - 1
                            for g in range(0, i + 1, 4):
                                pending.setdefault(min(first[i] + g + 3, end) + LAG_AV, []).append((2, "av", i, g))
                            pending.setdefault(end + LAG_READ, []).append((1, "read", i, 0))
                            reuse = first[i + 3] - 1 + LAG_READ if i + 2 < TILES else end + LAG_FOLD
                            fold_at[i] = min(end + LAG_FOLD, reuse)
                            pending.setdefault(fold_at[i], []).append((0, "fold", i, 0))
                        for i in range(TILES):
                            limit = fold_at.get(i + 1, fold_at[i] + 4)
                            pending.setdefault(min(fold_at[i] + 2, limit), []).append((-2, "invert", i, 0))
                            pending.setdefault(min(fold_at[i] + 4, limit), []).append((-1, "scale", i, 0))
                        for k in range(total + LAG_FOLD + 4):
                            self.steps += [(kind, i, g, False) for _, kind, i, g in sorted(pending.get(k, []))]
                            bias(k)
                            if k < total:
                                self.steps.append(("score", *blocks[k], False))
                                maxima(k, (k + 1) * (work + 4) / total - 1)
                        maxima(k, work)
                    else:
                        for k in range(int(work) + LAG_BIAS + 1):
                            maxima(k, k + 1)
                            bias(k)
                        maxima(k, work)
                    bias(k + LAG_BIAS)
                    self.bank_of, self.use_before, last = {}, {}, {}
                    free = list(range(RING))
                    for s in self.steps:
                        if s[0] in ("score", "bias", "fold") or s[0] == "av" and s[2] == 0:
                            bank = free.pop(0)
                            self.bank_of[s], self.use_before[s], last[bank] = bank, last.get(bank), s
                            if s[0] != "av":
                                free.append(bank)
                        elif s[0] == "read":
                            free.append(self.bank_of[("av", s[1], 0, False)])
                    self.av_number = {(s[1], s[2]): n for n, s in enumerate([s for s in self.steps if s[0] == "av"])}
                    self.weights = total if with_weights else 0

            opening = Plan([(i, True) for i in range(EARLY)], False)
            turn = Plan([(i, False) for i in range(EARLY, TILES)] + [(i, True) for i in range(EARLY)], True)

            with nc.Block() as block:
                @block.sync
                def _(sp):
                    def load_keys(head_row, piece):
                        c0, c1 = KPIECES[piece]
                        for k in range(3):
                            r0 = (0, 3 * HD, 5 * HD)[k]
                            sp.dma_start(keys[r0:r0 + (3 - k) * HD, c0:c1],
                                         keys_dram[0:3 - k, bass.ds(head_row, HD), c0:c1]).then_inc(k_in[piece], 16)

                    def load_queries(head_row, g):
                        w = min(BANK, PADDED - g * BANK)
                        for k in range(3):
                            r0 = (0, 3 * HD, 5 * HD)[k]
                            for c in range(3 - k):
                                rows, slot = slice(r0 + c * HD, r0 + (c + 1) * HD), load_order(g)[0]
                                dst = qlast[rows, :, :] if g == QGROUPS - 1 else query[rows, slot, :, :]
                                sp.dma_start(dst, queries_dram[k, bass.ds(head_row, HD), :, g * BANK:g * BANK + w])\
                                    .then_inc(q_in[slot], 16)

                    def load_ahead(head_row):
                        for k in range(3):
                            r0 = (0, 3 * HD, 5 * HD)[k]
                            sp.dma_start(ahead[r0:r0 + (3 - k) * HD, :],
                                         keys_dram[0:3 - k, bass.ds(head_row, HD), 0:EARLY_KEYS]).then_inc(n_in, 16)

                    def clear(done):
                        sp.wait_ge(head_done, done)
                        sp.sem_inc(turns, 1)
                        sp.sem_clear(range(loop_sems[0].num, loop_sems[-1].num + 1))
                        sp.sem_inc(heads_clear, 1)

                    load_ahead(0)
                    for g in range(QSLOTS):
                        load_queries(0, g)
                    for piece in range(3):
                        load_keys(0, piece)
                    clear(4)
                    with sp.Fori(0, TURNS) as h:
                        load_ahead(h * HD + HD)
                        load_queries(h * HD, QGROUPS - 1)
                        for g in range(QSLOTS, QGROUPS - 1):
                            sp.wait_ge(qk_mm, first[4 * (g - QSLOTS + 1)])
                            load_queries(h * HD, g)
                        for g in sorted(range(QSLOTS), key=lambda g: (g - QGROUPS + 1) % QSLOTS):
                            before = max(x for x in range(QGROUPS - 1) if x % QSLOTS == g)
                            sp.wait_ge(qk_mm, first[4 * (before + 1)])
                            load_queries(h * HD + HD, g)
                        for piece in range(3):
                            sp.wait_ge(qk_mm, first[TILES - 1] + KPIECES[piece][1] // P)
                            load_keys(h * HD + HD, piece)
                        clear(4 * h + 8)
                    for piece in range(3):
                        sp.wait_ge(k_in[piece], 48 * (TURNS + 1))
                    for g in range(QSLOTS):
                        slot, nth, loads = load_order(g)
                        sp.wait_ge(q_in[slot], 96 * (TURNS * loads + nth))

                @block.gpsimd
                def _(pool):
                    nc.gpsimd.memset(keys[K6:P, :], 1.0).then_inc(prep, 1)
                    pool.wait_ge(prep, 1)
                    nc.gpsimd.memset(mpart[:, :, :], 0.0).then_inc(prep, 1)
                    nc.gpsimd.tensor_copy(identb[:, :], const("ident")).then_inc(prep, 1)
                    nc.gpsimd.tensor_copy(negs[:, :], const("neg_s")).then_inc(prep, 1)
                    for e in range(NE):
                        nc.gpsimd.tensor_copy(negt[:, e, :], const("neg_t")).then_inc(prep, 1)
                    pool.wait_ge(prep, 4 + NE)
                    def split_maxima(plan):
                        for n in range(len(plan.rows)):
                            diag = [mpart[:, n % 2, 4 * a:][:, 0:3 * 33 + 1:33] for a in range(3)]
                            pool.wait_ge(row_max, n + 1)
                            if n >= 2:
                                pool.wait_ge(bias_mm, n - 1)
                            nc.gpsimd.tensor_copy(diag[0], nmax[:, n % 2, :]).then_inc(split_a, 1)
                            pool.wait_ge(split_a, n + 1)
                            nc.gpsimd.tensor_tensor(mrest[:, :], nmax[:, n % 2, :], diag[0], ALU.subtract).then_inc(split_b, 1)
                            pool.wait_ge(split_b, n + 1)
                            nc.gpsimd.tensor_copy(diag[1], mrest[:, :]).then_inc(split_c, 1)
                            pool.wait_ge(split_c, n + 1)
                            nc.gpsimd.tensor_tensor(diag[2], mrest[:, :], diag[1], ALU.subtract).then_inc(max_split, 1)
                        pool.wait_ge(max_split, len(plan.rows))
                        pool.sem_inc(head_done, 1)

                    split_maxima(opening)
                    pool.wait_ge(heads_clear, 1)
                    with pool.Fori(0, TURNS) as h:
                        for c0, c1 in ((0, 4 * 32), (4 * 32, TILES * 32)):
                            nc.gpsimd.tensor_copy(vhead[:, c0:c1].unsqueeze(1), values[:, bass.ds(h, 1), c0:c1]).then_inc(v_in, 1)
                        split_maxima(turn)
                        pool.wait_ge(heads_clear, h + 2)

                @block.scalar
                def _(act):
                    def follow(plan):
                        for step in plan.steps:
                            kind, i, j, is_next = step
                            if kind == "score":
                                n = nblock[(i, j)]
                                act.wait_ge(qk_mm, n + 1)
                                if n >= NP:
                                    ii, jj = blocks[n - NP]
                                    act.wait_ge(av_mm, plan.av_number[(ii, jj // 4 * 4)] + 1)
                                nc.scalar.activation(prob[:, n % NP, :], ps_ring[plan.bank_of[step]][:, :], ACT.Exp).then_inc(exp_done, 1)
                            elif kind == "bias":
                                act.wait_ge(bias_mm, plan.order[(i, is_next)] + 1)
                                nc.scalar.activation(queries_of(i)[K6:KM],
                                                     ps_ring[plan.bank_of[step]][K6:KM, :].rearrange("p (e s) -> p e s", e=NE),
                                                     ACT.Copy).then_inc(bias_in, 1)
                            elif kind == "read":
                                act.wait_ge(av_mm, plan.av_number[(i, i // 4 * 4)] + 1)
                                if i >= 2:
                                    act.wait_ge(fold_mm, i - 1)
                                k = min(P, 32 * (i + 1))
                                nc.scalar.activation(osum[0:k, i % 2, :], ps_ring[plan.bank_of[("av", i, 0, False)]][0:k, :], ACT.Copy)\
                                    .then_inc(av_read, 1)
                        act.wait_ge(bias_in, len(plan.rows))
                        if plan.weights:
                            act.wait_ge(exp_done, total)
                            act.wait_ge(divided, TILES)
                        act.sem_inc(head_done, 1)

                    follow(opening)
                    act.wait_ge(heads_clear, 1)
                    with act.Fori(0, TURNS) as h:
                        follow(turn)
                        act.wait_ge(heads_clear, h + 2)

                @block.vector
                def _(dve):
                    def follow(plan, h):
                        for step in plan.steps:
                            kind, i, j, is_next = step
                            if kind == "max":
                                n = plan.max_number[((i, is_next), j)]
                                slot = plan.order[(i, is_next)] % 2
                                pieces = max_items(i)[0][j]
                                e0, key0, w = pieces[0]
                                u = key0 // (2 * BANK)
                                dve.wait_ge(max_mm, n + 1)
                                if len(pieces) == 1:
                                    src, dst = ps_max[n % 2][:, 0:w], pmax[:, slot, e0, u:u + 1]
                                else:
                                    src = ps_max[n % 2][:, :].rearrange("p (a c) -> p a c", a=2)[:, :, 0:w]
                                    dst = pmax[:, slot, e0:e0 + 2, u]
                                nc.vector.tensor_reduce(dst, src, AX.X, ALU.max).then_inc(max_read, 1)
                            elif kind == "rowmax":
                                n = plan.order[(i, is_next)]
                                items, parts = max_items(i)
                                dve.wait_ge(max_read, plan.max_number[((i, is_next), len(items) - 1)] + 1)
                                if n >= 2:
                                    dve.wait_ge(max_split, n - 1)
                                nc.vector.tensor_reduce(nmax[:, n % 2, :], pmax[:, n % 2, :, 0:parts], AX.X, ALU.max, negate=True)\
                                    .then_inc(row_max, 1)
                            elif kind == "fold":
                                dve.wait_ge(fold_mm, i + 1)
                                o = ps_ring[plan.bank_of[step]][:, :].rearrange("p (e q f) -> p e f q", e=NE, q=4)
                                if i >= 1:
                                    dve.wait_ge(divided, i)
                                nc.vector.tensor_reduce(fsum[:, :, :], o[:, :, 0:HD + 1, 0:min(4, i + 1)], AX.X, ALU.add)\
                                    .then_inc(sum_done, 1)
                            elif kind == "invert":
                                dve.wait_ge(sum_done, i + 1)
                                nc.vector.reciprocal(rden[:, :], fsum[:, :, HD]).then_inc(rec_done, 1)
                            elif kind == "scale":
                                dve.wait_ge(rec_done, i + 1)
                                nc.vector.tensor_tensor(
                                    attn[:, i, bass.ds(h, 1), :].rearrange("p a (e f) -> p (a e) f", e=NE), fsum[:, :, 0:HD],
                                    rden[:, :].unsqueeze(2).to_broadcast([P, NE, HD]), ALU.mult).then_inc(divided, 1)
                        dve.wait_ge(row_max, len(plan.rows))
                        if plan.weights:
                            dve.wait_ge(divided, TILES)
                        dve.sem_inc(head_done, 1)

                    follow(opening, 0)
                    dve.wait_ge(heads_clear, 1)
                    with dve.Fori(0, TURNS) as h:
                        follow(turn, h)
                        dve.wait_ge(heads_clear, h + 2)

                @block.tensor
                def _(pe):
                    def follow(plan, h):
                        if plan.weights:
                            pe.wait_ge(k_in[0], 48 * h + 48)
                        for step in plan.steps:
                            kind, i, j, is_next = step
                            if step in plan.bank_of:
                                bank = ps_ring[plan.bank_of[step]]
                                before = plan.use_before[step]
                                if before:
                                    if before[0] == "score":
                                        pe.wait_ge(exp_done, nblock[before[1:3]] + 1)
                                    elif before[0] == "bias":
                                        pe.wait_ge(bias_in, plan.order[(before[1], before[3])] + 1)
                                    elif before[0] == "av":
                                        pe.wait_ge(av_read, before[1] + 1)
                                    else:
                                        pe.wait_ge(sum_done, before[1] + 1)
                            if kind == "max":
                                n = plan.max_number[((i, is_next), j)]
                                if j == 0 and i % 4 == 0:
                                    slot, nth, turns_loads = load_order(i // 4)
                                    pe.wait_ge(q_in[slot], 96 * turns_loads * (h + 1 if is_next else h) + 96 * nth)
                                if j == 0 and i == 0:
                                    pe.wait_ge(n_in, 48 * (h + 1) + 48)
                                if j == 0 and not is_next and (i * P) in (KPIECES[1][0], KPIECES[2][0]):
                                    pe.wait_ge(k_in[1 if i * P == KPIECES[1][0] else 2], 48 * h + 48)
                                if n >= 2:
                                    pe.wait_ge(max_read, n - 1)
                                source = ahead if is_next else keys
                                for a, (e, key0, w) in enumerate(max_items(i)[0][j]):
                                    for c in range(0, w, BANK):
                                        cw = min(BANK, w - c)
                                        diag = key0 + c + cw == (i + 1) * P
                                        o = ps_max[n % 2][:, a * BANK + c:a * BANK + c + cw]
                                        last = nc.tensor.matmul(o, queries_of(i)[0:K6, e], source[0:K6, key0 + c:key0 + c + cw],
                                                                start=True, stop=not diag)
                                        if diag:
                                            last = nc.tensor.matmul(o[:, cw - P:cw], identb[:, :], negs[:, :], start=False, stop=True)
                                last.then_inc(max_mm, 1)
                            elif kind == "bias":
                                n = plan.order[(i, is_next)]
                                pe.wait_ge(max_split, n + 1)
                                for e in range(NE):
                                    last = nc.tensor.matmul(bank[K6:K6 + 32, e * P:(e + 1) * P], mpart[:, n % 2, e * 32:(e + 1) * 32],
                                                            identb[:, :], start=True, stop=True)
                                last.then_inc(bias_mm, 1)
                            elif kind == "score":
                                n = nblock[(i, j)]
                                if j == 0 and i >= EARLY:
                                    pe.wait_ge(bias_in, plan.order[(i, False)] + 1)
                                o = bank[:, :].rearrange("p (e s) -> p e s", e=NE)
                                last = nc.tensor.matmul(o, keys[0:KM, j * P:(j + 1) * P], queries_of(i)[0:KM], start=True, stop=(j < i))
                                if j == i:
                                    last = nc.tensor.matmul(o, identb[:, :], negt[:, :, :], start=False, stop=True)
                                last.then_inc(qk_mm, 1)
                            elif kind == "av":
                                hi = min(j + 3, i)
                                pe.wait_ge(exp_done, nblock[(i, hi)] + 1)
                                bank = ps_ring[plan.bank_of[("av", i, 0, False)]]
                                if (i, j) in ((0, 0), (4, 4)):
                                    pe.wait_ge(v_in, 1 + (i > 0))
                                for jj in range(j, hi + 1):
                                    q = jj % 4
                                    last = nc.tensor.matmul(bank[32 * q:32 * q + 32, :], vhead[:, jj * 32:(jj + 1) * 32],
                                                            prob[:, nblock[(i, jj)] % NP, :], start=(jj < 4), stop=(jj + 4 > i))
                                last.then_inc(av_mm, 1)
                            elif kind == "fold":
                                pe.wait_ge(av_read, i + 1)
                                k = min(P, 32 * (i + 1))
                                for e in range(NE):
                                    last = nc.tensor.transpose(bank[:, e * P:e * P + k], osum[0:k, i % 2, e * P:(e + 1) * P],
                                                               const("ident", 0, k, 0, k))
                                last.then_inc(fold_mm, 1)
                        if plan.weights:
                            pe.wait_ge(divided, TILES)
                        pe.wait_ge(bias_in, len(plan.rows))
                        pe.sem_inc(head_done, 1)

                    pe.wait_ge(prep, 4 + NE)
                    follow(opening, -1)
                    pe.wait_ge(heads_clear, 1)
                    with pe.Fori(0, TURNS) as h:
                        follow(turn, h)
                        pe.wait_ge(heads_clear, h + 2)

        with ExitStack() as st:
            nz = sb(st, "nz", [P, TILES, P])
            gT = sb(st, "gT", [P, 2, BANK])
            gate = sb(st, "gate_w", [P, TILES, HEADS * NE])
            gsum = sb(st, "gsum", [P, 2, TILES * HEADS])
            mix = sb(st, "mix", [P, TILES, P])
            prodg = sb(st, "prodg", [P, 1, TILES, NE * HD])
            stat = sb(st, "stat5", [P, 4, TILES * HEADS])
            ps = [pb(st, f"ps5_{k}", [P, BANK]) for k in range(8)]
            fT = values[:, 0:4, :].rearrange("p h c -> p (h c)")
            hT = values[:, 4:8, :].rearrange("p h c -> p (h c)")
            flat = lambda a: a[:, :, :].rearrange("p i f -> p (i f)")
            G = TILES * HEADS
            g16 = lambda a: a[:, :, :].rearrange("p i (g d) -> p (i g) d", d=HD)
            (g_masked, gt_mm, gt_sb, gl_mm, g_sub, g_exp, fn_done, ft_mm, ft_sb, f1_mm, f1_relu, f1_done, f2_mm, fout_done, fo_mm, fo_sb,
             fg_mm, fg_sub, fg_exp, final, stored) = (sem(n) for n in (
                "g_masked", "gt_mm", "gt_sb", "gl_mm", "g_sub", "g_exp", "fn_done", "ft_mm", "ft_sb", "f1_mm", "f1_relu", "f1_done", "f2_mm",
                "fout_done", "fo_mm", "fo_sb", "fg_mm", "fg_sub", "fg_exp", "final", "stored"))
            f2_read = sem("f2_read")
            ln3 = [sem("ln3_" + n) for n in names]
            ln4 = [sem("ln4_" + n) for n in names]
            own = Chain("ffn_vector")
            scratch = attn[:, :, :, :].rearrange("p h i f -> p (h i f)")
            cent = scratch[:, 0:PADDED].rearrange("p (g d) -> p g d", d=HD)
            work = scratch[:, PADDED:2 * PADDED].rearrange("p (g d) -> p g d", d=HD)
            NTP = (TILES + 15) // 16

            def broad(row):
                return row.unsqueeze(1).to_broadcast([P, G, HD])

            with nc.Block() as block:
                @block.vector
                def _(dve):
                    own(dve, nc.vector.tensor_scalar(flat(nz), flat(sx_tok), 0.0, None, ALU.not_equal))
                    for h in range(HEADS):
                        a = attn[:, :, h, :].rearrange("p i (e d) -> p i e d", e=NE)
                        own(dve, nc.vector.tensor_tensor(
                            a, a, nz[:, :, h * HD:(h + 1) * HD].unsqueeze(2).to_broadcast([P, TILES, NE, HD]), ALU.mult))
                    nc.vector.memset(stat[:, 3, 0:1], 0.0).then_inc(g_masked, 1)
                    dve.wait_ge(gl_mm, TILES)
                    for k in range(NTP):
                        nt = min(16, TILES - 16 * k)
                        own(dve, nc.vector.tensor_tensor(
                            gate[:, 16 * k:16 * k + nt, :], ps[2 + k][:, 0:32 * nt].rearrange("p (i c) -> p i c", c=32),
                            const("gate_b").unsqueeze(1).to_broadcast([P, nt, 32]), ALU.add))
                    gate4 = gate[:, :, :].rearrange("p i (g e) -> p (i g) e", e=NE)
                    own(dve, nc.vector.tensor_reduce(gsum[:, 0, :], gate4, AX.X, ALU.max))
                    nc.vector.tensor_tensor(gate4, gate4, gsum[:, 0, :].unsqueeze(2).to_broadcast([P, G, NE]), ALU.subtract).then_inc(g_sub, 1)
                    dve.wait_ge(g_exp, 1)
                    own(dve, nc.vector.tensor_reduce(gsum[:, 1, :], gate4, AX.X, ALU.add))
                    own(dve, nc.vector.reciprocal(gsum[:, 1, :], gsum[:, 1, :]))
                    own(dve, nc.vector.tensor_tensor(gate4, gate4, gsum[:, 1, :].unsqueeze(2).to_broadcast([P, G, NE]), ALU.mult))
                    for h in range(HEADS):
                        a = attn[:, :, h, :].rearrange("p i (e d) -> p i e d", e=NE)
                        own(dve, nc.vector.tensor_tensor(
                            prodg[:, 0, :, :].rearrange("p i (e d) -> p i e d", e=NE), a,
                            gate[:, :, h * NE:(h + 1) * NE].unsqueeze(3).to_broadcast([P, TILES, NE, HD]), ALU.mult))
                        own(dve, nc.vector.tensor_reduce(mix[:, :, h * HD:(h + 1) * HD],
                                                         prodg[:, 0, :, :].rearrange("p i (e d) -> p i d e", e=NE), AX.X, ALU.add))
                    for b in range(BATCH):
                        for n0, n1 in ((0, 1), (1, NH)):
                            m = mix[:, :, (b * NH + n0) * HD:(b * NH + n1) * HD]
                            src = min(n0, BATCH - 1) * NH
                            own(dve, nc.vector.tensor_tensor(m, m, sx_tok[:, :, (src + n0) * HD:(src + n1) * HD], ALU.add))
                    normalise_vector(dve, own, g16(mix), cent, work, stat, G, HD, FFN_EPS, *ln3)
                    own(dve, nc.vector.tensor_tensor(cent, cent, broad(const("ln_g")), ALU.mult))
                    nc.vector.tensor_tensor(g16(mix), cent, broad(const("ln_b")), ALU.add).then_inc(fn_done, 1)
                    for c, (c0, w) in enumerate(CHUNKS):
                        dve.wait_ge(f1_relu, c + 1)
                        nc.vector.scalar_tensor_tensor(hT[:, c0:c0 + w], fT[:, c0:c0 + w], 0.0, hT[:, c0:c0 + w],
                                                       ALU.not_equal, ALU.mult).then_inc(f1_done, 1)
                    c3 = cent.rearrange("p (i g) d -> p i (g d)", i=TILES)
                    for c, (c0, w) in enumerate(CHUNKS):
                        dve.wait_ge(f2_mm, c + 1)
                        i0, nt = c0 // P, w // P
                        cc = c3[:, i0:i0 + nt, :]
                        nc.vector.tensor_tensor(cc, ps[c % 2][:, 0:w].rearrange("p (i f) -> p i f", f=P),
                                                const("fc2_b").unsqueeze(1).to_broadcast([P, nt, P]), ALU.add).then_inc(f2_read, 1)
                    dve.wait_ge(f2_read, len(CHUNKS))
                    own(dve, nc.vector.scalar_tensor_tensor(cent, g16(mix), 0.0, cent, ALU.not_equal, ALU.mult))
                    own(dve, nc.vector.tensor_tensor(g16(mix), cent, g16(mix), ALU.add))
                    normalise_vector(dve, own, g16(mix), cent, work, stat, G, HD, FFN_EPS, *ln4)
                    own(dve, nc.vector.tensor_tensor(cent, cent, broad(const("fn_g")), ALU.mult))
                    nc.vector.tensor_tensor(g16(mix), cent, broad(const("fn_b")), ALU.add).then_inc(fout_done, 1)
                    dve.wait_ge(fg_mm, TILES)
                    lg = ps[2][:, 0:G].rearrange("p (g n) -> p g n", n=NH)
                    own(dve, nc.vector.tensor_reduce(stat[:, 0, 0:GROUPS], lg, AX.X, ALU.max))
                    fgv = gsum[:, 0, :].rearrange("p (g n) -> p g n", n=NH)
                    nc.vector.tensor_tensor(fgv, lg, stat[:, 0, 0:GROUPS].unsqueeze(2).to_broadcast([P, GROUPS, NH]), ALU.subtract)\
                        .then_inc(fg_sub, 1)
                    dve.wait_ge(fg_exp, 1)
                    own(dve, nc.vector.tensor_reduce(stat[:, 1, 0:GROUPS], fgv, AX.X, ALU.add))
                    own(dve, nc.vector.reciprocal(stat[:, 1, 0:GROUPS], stat[:, 1, 0:GROUPS]))
                    own(dve, nc.vector.tensor_tensor(fgv, fgv, stat[:, 1, 0:GROUPS].unsqueeze(2).to_broadcast([P, GROUPS, NH]), ALU.mult))
                    own(dve, nc.vector.tensor_tensor(g16(mix), g16(mix), gsum[:, 0, :].unsqueeze(2).to_broadcast([P, G, HD]), ALU.mult))
                    nc.vector.tensor_tensor(flat(mix), flat(mix), flat(hid), ALU.add).then_inc(final, 1)

                @block.tensor
                def _(pe):
                    pe.wait_ge(g_masked, 1)
                    for i in range(TILES + 1):
                        if i < TILES:
                            if i >= 2:
                                pe.wait_ge(gt_sb, i - 1)
                            for p in range(NE):
                                last = nc.tensor.transpose(ps[i % 2][:, p * P:(p + 1) * P], attn[:, i, 2 * p:2 * p + 2, :].rearrange("p h f -> p (h f)"), const("ident"))
                            last.then_inc(gt_mm, 1)
                        if i >= 1:
                            j = i - 1
                            pe.wait_ge(gt_sb, j + 1)
                            for p in range(NE):
                                c = 32 * (j % 16) + 8 * p
                                last = nc.tensor.matmul(ps[2 + j // 16][:, c:c + 8], gT[:, j % 2, p * P:(p + 1) * P],
                                                        const("gate", 0, P, 8 * (p % 2), 8 * (p % 2) + 8), start=True, stop=True)
                            last.then_inc(gl_mm, 1)
                    pe.wait_ge(fn_done, 1)
                    for c, (c0, w) in enumerate(CHUNKS):
                        if c >= 2:
                            pe.wait_ge(ft_sb, c - 1)
                        for t in range(w // P):
                            last = nc.tensor.transpose(ps[c % 2][:, t * P:(t + 1) * P], mix[:, c0 // P + t, :], const("ident"))
                        last.then_inc(ft_mm, 1)
                    for c, (c0, w) in enumerate(CHUNKS):
                        pe.wait_ge(ft_sb, c + 1)
                        if c >= 2:
                            pe.wait_ge(f1_relu, c - 1)
                        nc.tensor.matmul(ps[2 + c % 2][:, 0:w], const("fc1"), fT[:, c0:c0 + w], start=True, stop=True).then_inc(f1_mm, 1)
                    for c, (c0, w) in enumerate(CHUNKS):
                        pe.wait_ge(f1_done, c + 1)
                        if c >= 2:
                            pe.wait_ge(f2_read, c - 1)
                        for t in range(w // P):
                            last = nc.tensor.matmul(ps[c % 2][:, t * P:(t + 1) * P], hT[:, c0 + t * P:c0 + (t + 1) * P], const("fc2"),
                                                    start=True, stop=True)
                        last.then_inc(f2_mm, 1)
                    pe.wait_ge(fout_done, 1)
                    for c, (c0, w) in enumerate(CHUNKS):
                        if c >= 2:
                            pe.wait_ge(fo_sb, c - 1)
                        for t in range(w // P):
                            last = nc.tensor.transpose(ps[c % 2][:, t * P:(t + 1) * P], mix[:, c0 // P + t, :], const("ident"))
                        last.then_inc(fo_mm, 1)
                    for i in range(TILES):
                        pe.wait_ge(fo_sb, i // 4 + 1)
                        nc.tensor.matmul(ps[2][:, i * 8:(i + 1) * 8], fT[:, i * P:(i + 1) * P], const("fgate"), start=True, stop=True)\
                            .then_inc(fg_mm, 1)

                @block.scalar
                def _(act):
                    for i in range(TILES):
                        act.wait_ge(gt_mm, i + 1)
                        if i >= 2:
                            act.wait_ge(gl_mm, i - 1)
                        nc.scalar.activation(gT[:, i % 2, :], ps[i % 2][:, :], ACT.Copy).then_inc(gt_sb, 1)
                    act.wait_ge(g_sub, 1)
                    nc.scalar.activation(flat(gate), flat(gate), ACT.Exp).then_inc(g_exp, 1)
                    normalise_scalar(act, cent, work, stat, G, *ln3)
                    for c, (c0, w) in enumerate(CHUNKS):
                        act.wait_ge(ft_mm, c + 1)
                        nc.scalar.activation(fT[:, c0:c0 + w], ps[c % 2][:, 0:w], ACT.Copy).then_inc(ft_sb, 1)
                    for c, (c0, w) in enumerate(CHUNKS):
                        act.wait_ge(f1_mm, c + 1)
                        nc.scalar.activation(hT[:, c0:c0 + w], ps[2 + c % 2][:, 0:w], ACT.Relu, bias=const("fc1_b")).then_inc(f1_relu, 1)
                    normalise_scalar(act, cent, work, stat, G, *ln4)
                    for c, (c0, w) in enumerate(CHUNKS):
                        act.wait_ge(fo_mm, c + 1)
                        nc.scalar.activation(fT[:, c0:c0 + w], ps[c % 2][:, 0:w], ACT.Copy).then_inc(fo_sb, 1)
                    act.wait_ge(fg_sub, 1)
                    nc.scalar.activation(gsum[:, 0, :], gsum[:, 0, :], ACT.Exp).then_inc(fg_exp, 1)

                @block.sync
                def _(sp):
                    sp.wait_ge(final, 1)
                    for b in range(BATCH):
                        f = slice(b * FEAT, (b + 1) * FEAT)
                        sp.dma_start(out[b, 0:IMAGE, :].rearrange("(i p) f -> p i f", p=P), mix[:, 0:TILES - 1, f]).then_inc(stored, 16)
                        sp.dma_start(out[b, IMAGE:TOKENS, :], mix[0:TEXT, TILES - 1, f]).then_inc(stored, 16)
                    sp.wait_ge(stored, 16 * 2 * BATCH)


def pack_constants(w):
    c = np.zeros((P, PACKED), np.float32)

    def put(name, array, p0=0, c0=0):
        a = AT[name][0] + c0
        c[p0:p0 + array.shape[0], a:a + array.shape[1]] = array

    def diagonal(name, block, copies, c0=0):
        for k in range(copies):
            put(name, block, k * block.shape[0], c0 + k * block.shape[1])

    def row(name, vector):
        put(name, np.broadcast_to(vector[None, :], (P, vector.shape[0])))

    def column(name, vector, copies):
        put(name, np.tile(vector, copies)[:, None])

    diagonal("conv1", w["L0_tok_conv1_w"].T, BATCH)
    for k in range(TAPS):
        for b in range(BATCH):
            tap = np.broadcast_to(w["L0_tok_conv2_w"][k][:, None], (REDUCED, CH))
            put("conv2", tap, b * REDUCED, k * P + b * CH)
    for k, name in enumerate(("conv1_b", "bn_gamma", "bn_beta", "bn_mean", "bn_var")):
        put("bn", np.tile(w["L0_tok_" + name], BATCH)[:, None], 0, k)
    row("conv2_b", w["L0_tok_conv2_b"])
    for s in "kq":
        diagonal(s + "w1", w[f"L0_attn_{s}w1"].T, BATCH)
        column(s + "b1", w[f"L0_attn_{s}b1"], BATCH)
        diagonal(s + "w2", np.concatenate([w[f"L0_attn_{s}w2"].T] * 2, axis=1), BATCH)
        column(s + "b2", w[f"L0_attn_{s}b2"], 2 * BATCH)
    diagonal("vw", w["L0_attn_vw"].T, BATCH)
    row("vb", np.tile(w["L0_attn_vb"], BATCH))
    hl = w["L0_ffn_hl_w"].reshape(NH * HD, FEAT)
    diagonal("hl", hl.T, BATCH)
    column("hl_b", w["L0_ffn_hl_b"].reshape(-1), BATCH)
    for b in range(BATCH):
        for n in range(NH):
            r = (b * NH + n) * HD
            put("wk", w["L0_ffn_wk"][n].T, r, r)
            put("wv", w["L0_ffn_wv"][n].T, r, r)
            for e in range(NE):
                put("wq", w["L0_ffn_wq"][n, e].T, r, e * P + r)
    for n in range(NH):
        put("gate", w["L0_ffn_gate_w"][n].T, n % 2 * FEAT, n // 2 * 8 + n % 2 * NE)
    row("gate_b", np.tile(w["L0_ffn_gate_b"].reshape(-1), BATCH))
    row("ln_g", w["L0_ffn_ln_g"])
    row("ln_b", w["L0_ffn_ln_b"])
    diagonal("fc1", w["L0_ffn_fc1_w"].T, HEADS)
    column("fc1_b", w["L0_ffn_fc1_b"], HEADS)
    diagonal("fc2", w["L0_ffn_fc2_w"].T, HEADS)
    row("fc2_b", np.tile(w["L0_ffn_fc2_b"], HEADS))
    row("fn_g", w["L0_ffn_fnorm_g"])
    row("fn_b", w["L0_ffn_fnorm_b"])
    diagonal("fgate", w["L0_ffn_fgate_w"].T, BATCH)
    a = np.arange(P)
    put("ident", np.eye(P, dtype=np.float32))
    put("keep", (a[:, None] <= a[None, :]).astype(np.float32))
    put("neg_s", np.where(a[None, :] > a[:, None], NEG, 0.0).astype(np.float32))
    put("neg_t", np.where(a[:, None] > a[None, :], NEG, 0.0).astype(np.float32))
    pos = (a[:, None] + P * np.arange(TILES)[None, :] + 1).astype(np.float64)
    put("inv_norm", (1.0 / np.sqrt(pos * PHASES)).astype(np.float32))
    cosine = (a // PHASES % 2 == 1)
    put("phase", np.stack([np.where(cosine, -1.0, 1.0), np.where(cosine, -PI_BELOW, PI_BELOW),
                           np.where(cosine, np.pi / 2, 0.0)], axis=1).astype(np.float32))
    return c


def kernel(**inputs):
    import concourse.bacc as _bacc
    from concourse.bass_utils import run_bass_kernel_spmd as _run

    inputs = {k: np.ascontiguousarray(v) for k, v in inputs.items()}
    arrays = {"x_dram": inputs["x"], "txt_dram": inputs["txt"], "packed_dram": pack_constants(inputs)}
    nc = _bacc.Bacc("TRN2", target_bir_lowering=False, num_devices=1)
    args = [nc.dram_tensor(n, a.shape, mybir.dt.from_np(a.dtype), kind="ExternalInput").ap() for n, a in arrays.items()]
    out = nc.dram_tensor("out_dram", (BATCH, TOKENS, FEAT), mybir.dt.float32, kind="ExternalOutput").ap()
    build(nc, *args, out)
    r = _run(nc, [arrays], core_ids=[0])
    return r.results[0]["out_dram"]
```

```python
import numpy as np
import concourse.bass as bass
from concourse import mybir
from contextlib import ExitStack

BATCH, CH, ROWS, COLS, TEXT = 2, 64, 64, 64, 77
FEAT = 64
IMAGE = CH * ROWS
TOKENS = IMAGE + TEXT
P = 128
TILES = -(-TOKENS // P)
PADDED = TILES * P
TAPS = 9
REDUCED = 16
PHASES = 32
NH, NE, HD = 4, 4, 16
HEADS = BATCH * NH
TURNS = HEADS
BN_EPS, LN_EPS, FFN_EPS = 1e-5, 1e-5, 1e-8
BANK = 512
CHUNKS = [(c, min(BANK, PADDED - c)) for c in range(0, PADDED, BANK)]
NEG = -3.0e38
PI_BELOW = 3.1415925

WIDTHS = [
    ("conv1", P), ("conv2", TAPS * P), ("bn", 5), ("conv2_b", TAPS),
    ("kw1", P), ("qw1", P), ("kb1", 1), ("qb1", 1), ("kw2", P), ("qw2", P), ("kb2", 1), ("qb2", 1),
    ("vw", P), ("vb", P), ("hl", P), ("hl_b", 1), ("wk", P), ("wq", NE * P), ("wv", P),
    ("gate", 64), ("gate_b", 32), ("ln_g", HD), ("ln_b", HD), ("fc1", P), ("fc1_b", 1), ("fc2", P),
    ("fc2_b", P), ("fn_g", HD), ("fn_b", HD), ("fgate", 8),
    ("ident", P), ("keep", P), ("neg_s", P), ("neg_t", P), ("inv_norm", TILES), ("phase", 3),
]
AT, _n = {}, 0
for _name, _w in WIDTHS:
    AT[_name] = (_n, _n + _w)
    _n += _w
PACKED = _n


def build(nc, x, txt, packed, out):
    fp32, bf16 = mybir.dt.float32, mybir.dt.bfloat16
    ALU, ACT, AX = mybir.AluOpType, mybir.ActivationFunctionType, mybir.AxisListType
    top = ExitStack()

    def sem(name):
        return top.enter_context(nc.semaphore(name))

    tokens_dram = nc.dram_tensor("tokens_scratch", [BATCH, IMAGE, FEAT], fp32, kind="Internal").ap()
    keys_dram = nc.dram_tensor("keys_scratch", [3, P + HD, PADDED], bf16, kind="Internal").ap()
    queries_dram = nc.dram_tensor("queries_scratch", [3, P + HD, NE, PADDED], bf16, kind="Internal").ap()

    with top:
        def sb(stack, name, shape, dt=fp32):
            return stack.enter_context(nc.sbuf_tensor(name, shape, dt))

        def pb(stack, name, shape, dt=fp32):
            return stack.enter_context(nc.psum_tensor(name, shape, dt))

        con = sb(top, "con", [P, PACKED])
        hid = sb(top, "hid", [P, TILES, BATCH * FEAT])

        def const(name, p0=0, p1=P, c0=0, c1=None):
            a, b = AT[name]
            return con[p0:p1, a + c0:(b if c1 is None else a + c1)]

        class Chain:
            def __init__(self, name):
                self.sem, self.n = sem(name), 0

            def __call__(self, eng, ins):
                self.n += 1
                ins.then_inc(self.sem, 1)
                eng.wait_ge(self.sem, self.n)

        PIECES = [(12 * k, min(12 * k + 12, TILES)) for k in range((TILES + 11) // 12)]
        piece_of = lambda c: c // 3

        def group_pieces(groups):
            per = groups // TILES
            return [slice(a * per, b * per) for a, b in PIECES]

        def spread(stat, groups, width):
            return stat.unsqueeze(2).to_broadcast([P, groups.stop - groups.start, width])

        def normalise_vector(dve, chain, data, cent, work, stat, groups, width, eps, squares, centred, varred, rooted):
            chain(dve, nc.vector.tensor_reduce(stat[:, 0, 0:groups], data, AX.X, ALU.add))
            chain(dve, nc.vector.tensor_scalar(stat[:, 0, 0:groups], stat[:, 0, 0:groups], 1.0 / width, None, ALU.mult))
            pieces = group_pieces(groups)
            for g in pieces:
                nc.vector.tensor_tensor(cent[:, g], data[:, g], spread(stat[:, 0, g], g, width), ALU.subtract).then_inc(centred, 1)
            for k, g in enumerate(pieces):
                dve.wait_ge(squares, k + 1)
                chain(dve, nc.vector.tensor_reduce(stat[:, 1, g], work[:, g], AX.X, ALU.add))
            nc.vector.tensor_scalar(stat[:, 1, 0:groups], stat[:, 1, 0:groups], 1.0 / width, eps, ALU.mult, ALU.add)\
                .then_inc(varred, 1)
            dve.wait_ge(rooted, 1)
            chain(dve, nc.vector.reciprocal(stat[:, 2, 0:groups], stat[:, 2, 0:groups]))

        def normalise_scalar(act, cent, work, stat, groups, squares, centred, varred, rooted):
            for k, g in enumerate(group_pieces(groups)):
                act.wait_ge(centred, k + 1)
                nc.scalar.activation(work[:, g], cent[:, g], ACT.Square).then_inc(squares, 1)
            act.wait_ge(varred, 1)
            nc.scalar.activation(stat[:, 2, 0:groups], stat[:, 1, 0:groups], ACT.Sqrt).then_inc(rooted, 1)

        with ExitStack() as st:
            x_sb = sb(st, "x_sb", [P, ROWS * COLS])
            xpad = sb(st, "xpad", [P, ROWS + 2, COLS + 2])
            red = sb(st, "red", [P, 2, BANK])
            rrest = sb(st, "rrest", [P, 2, BANK])
            rmid = sb(st, "rmid", [P, 2, BANK], bf16)
            rpart = sb(st, "rpart", [P, ROWS * COLS], bf16)
            wrest = sb(st, "wrest", [P, TAPS * P])
            wmid = sb(st, "wmid", [P, TAPS * P], bf16)
            wpart = [sb(st, f"wpart{k}", [P, TAPS * P], bf16) for k in range(2)]
            acc = sb(st, "acc", [P, ROWS * COLS])
            SLOTS = 8
            prod = sb(st, "prod", [P, SLOTS, BANK])
            bn = sb(st, "bn", [P, 4])
            ps_red = [pb(st, f"ps_red{k}", [P, BANK]) for k in range(2)]
            ps_tap = [pb(st, f"ps_tap{k}", [P, BANK]) for k in range(4)]
            con_in, pad_zero, xpad_done, pair_sum = sem("con_in"), sem("pad_zero"), sem("xpad_done"), sem("pair_sum")
            x_in = [sem(f"x_in{k}") for k in range(2)]
            bn_var, bn_root, bn_done = sem("bn_var"), sem("bn_root"), sem("bn_done")
            w_one, w_rest, w_mid, w_done = (sem(n) for n in ("w_one", "w_rest", "w_mid", "w_done"))
            red_mm, red_done, red_one, red_rest, red_mid, red_low, red_parts, tap_mm, tap_prod, tap_added = (sem(n) for n in (
                "red_mm", "red_done", "red_one", "red_rest", "red_mid", "red_low", "red_parts", "tap_mm", "tap_prod", "tap_added"))
            tok_out, hid_in, hid_zero = sem("tok_out"), sem("hid_in"), sem("hid_zero")
            own = Chain("tok_vector")
            NPX = ROWS * COLS // BANK
            R = BANK // COLS
            Q = [slice(32 * k, 32 * k + 32) for k in range(4)]
            TERMS = [(0, 2), (3,), (5,), (6,), (8,)]
            term_of = [0, 0, 0, 1, 1, 2, 3, 3, 4]
            px = lambda q: slice(q * BANK, (q + 1) * BANK)
            with nc.Block() as block:
                @block.sync
                def _(sp):
                    for half in range(2):
                        f = slice(half * NPX // 2 * BANK, (half + 1) * NPX // 2 * BANK)
                        sp.dma_start(x_sb[:, f], x.rearrange("b c h w -> (b c) (h w)")[:, f]).then_inc(x_in[half], 16)
                        if half == 0:
                            sp.dma_start(con[:, :], packed).then_inc(con_in, 16)
                    sp.wait_ge(hid_zero, 1)
                    sp.dma_start(hid[0:TEXT, TILES - 1, :].rearrange("p (b f) -> p b f", b=BATCH),
                                 txt.rearrange("b t f -> t b f")).then_inc(hid_in, 16)
                    tok_v = tokens_dram.rearrange("b (c h) w -> (b c) (h w)", c=CH)
                    for q in range(NPX):
                        sp.wait_ge(tap_added, (q + 1) * len(TERMS))
                        sp.dma_start(tok_v[:, px(q)], acc[:, px(q)]).then_inc(tok_out, 16)
                    sp.wait_ge(tok_out, 16 * NPX)
                    for b in range(BATCH):
                        sp.dma_start(hid[:, 0:TILES - 1, b * FEAT:(b + 1) * FEAT],
                                     tokens_dram[b].rearrange("(i p) f -> p i f", p=P)).then_inc(hid_in, 16)
                    sp.wait_ge(hid_in, 16 * (1 + BATCH))

                @block.tensor
                def _(pe):
                    def reduce_map(q):
                        pe.wait_ge(x_in[2 * q // NPX], 16)
                        if q >= 2:
                            pe.wait_ge(red_done, q - 1)
                        nc.tensor.matmul(ps_red[q % 2][:, :], const("conv1"), x_sb[:, px(q)], start=True, stop=True).then_inc(red_mm, 1)

                    pe.wait_ge(con_in, 16)
                    reduce_map(0)
                    reduce_map(1)
                    pe.wait_ge(w_done, 5)
                    for q in range(NPX):
                        if q + 2 < NPX:
                            reduce_map(q + 2)
                        pe.wait_ge(red_parts, q + 1)
                        pe.wait_ge(red_low, q + 1)
                        for k in range(TAPS):
                            n = q * TAPS + k
                            if n >= 4:
                                pe.wait_ge(tap_prod, n - 3)
                            for half in range(2):
                                last = nc.tensor.matmul(ps_tap[n % 4][:, :], wpart[half][:, k * P:(k + 1) * P], rpart[:, px(q)],
                                                        start=(half == 0), stop=(half == 1))
                            last.then_inc(tap_mm, 1)

                @block.scalar
                def _(act):
                    act.wait_ge(con_in, 16)
                    nc.scalar.activation(wpart[0][:, :], const("conv2"), ACT.Copy).then_inc(w_one, 1)
                    act.wait_ge(w_rest, 1)
                    nc.scalar.activation(wmid[:, :], wrest[:, :], ACT.Copy).then_inc(w_mid, 1)
                    act.wait_ge(w_mid, 1)
                    nc.scalar.activation(wpart[0][Q[3], :], wmid[Q[3], :], ACT.Copy).then_inc(w_done, 1)
                    act.wait_ge(bn_var, 1)
                    nc.scalar.activation(bn[:, 1:2], bn[:, 0:1], ACT.Sqrt).then_inc(bn_root, 1)
                    act.wait_ge(bn_done, 1)
                    for q in range(NPX + 1):
                        if q < NPX:
                            act.wait_ge(red_mm, q + 1)
                            if q >= 2:
                                act.wait_ge(red_rest, q - 1)
                            nc.scalar.activation(red[:, q % 2, :], ps_red[q % 2][:, :], ACT.Relu,
                                                 bias=bn[:, 3:4], scale=bn[:, 2:3]).then_inc(red_done, 1)
                            act.wait_ge(red_done, q + 1)
                            nc.scalar.activation(rpart[:, px(q)], red[:, q % 2, :], ACT.Copy).then_inc(red_one, 1)
                        if q >= 1:
                            p = q - 1
                            act.wait_ge(red_rest, p + 1)
                            if p >= 2:
                                act.wait_ge(red_low, p - 1)
                            nc.scalar.activation(rmid[:, p % 2, :], rrest[:, p % 2, :], ACT.Copy).then_inc(red_mid, 1)
                            act.wait_ge(red_mid, p + 1)
                            nc.scalar.activation(rpart[Q[1], px(p)], rmid[Q[1], p % 2, :], ACT.Copy).then_inc(red_parts, 1)
                        if q == 1:
                            act.wait_ge(pad_zero, 1)
                            act.wait_ge(x_in[1], 16)
                            nc.scalar.activation(xpad[:, 1:ROWS + 1, 1:COLS + 1],
                                                 x_sb[:, :].rearrange("p (h w) -> p h w", h=ROWS), ACT.Copy).then_inc(xpad_done, 1)

                @block.vector
                def _(dve):
                    dve.wait_ge(con_in, 16)
                    b1, gamma, beta, mean, var = (const("bn", 0, P, k, k + 1) for k in range(5))
                    nc.vector.tensor_scalar(bn[:, 0:1], var, BN_EPS, None, ALU.add).then_inc(bn_var, 1)
                    dve.wait_ge(w_one, 1)
                    nc.vector.tensor_tensor(wrest[:, :], const("conv2"), wpart[0][:, :], ALU.subtract).then_inc(w_rest, 1)
                    dve.wait_ge(w_mid, 1)
                    nc.vector.tensor_tensor(wpart[1][Q[0], :], wrest[Q[0], :], wmid[Q[0], :], ALU.subtract).then_inc(w_done, 1)
                    for k in (1, 2):
                        nc.vector.tensor_copy(wpart[1][Q[k], :], wmid[Q[k], :]).then_inc(w_done, 1)
                    nc.vector.memset(wpart[1][Q[3], :], 0.0).then_inc(w_done, 1)
                    dve.wait_ge(bn_root, 1)
                    own(dve, nc.vector.reciprocal(bn[:, 2:3], bn[:, 1:2]))
                    own(dve, nc.vector.tensor_tensor(bn[:, 2:3], bn[:, 2:3], gamma, ALU.mult))
                    own(dve, nc.vector.tensor_tensor(bn[:, 3:4], b1, mean, ALU.subtract))
                    own(dve, nc.vector.tensor_tensor(bn[:, 3:4], bn[:, 3:4], bn[:, 2:3], ALU.mult))
                    nc.vector.tensor_tensor(bn[:, 3:4], bn[:, 3:4], beta, ALU.add).then_inc(bn_done, 1)

                    def rest(q):
                        dve.wait_ge(red_one, q + 1)
                        if q >= 2:
                            dve.wait_ge(red_mid, q - 1)
                        nc.vector.tensor_tensor(rrest[:, q % 2, :], red[:, q % 2, :], rpart[:, px(q)], ALU.subtract).then_inc(red_rest, 1)

                    def low(q):
                        dve.wait_ge(red_mid, q + 1)
                        nc.vector.tensor_tensor(rpart[Q[2], px(q)], rrest[Q[2], q % 2, :], rmid[Q[2], q % 2, :], ALU.subtract)\
                            .then_inc(red_low, 1)

                    rest(0)
                    low(0)
                    dve.wait_ge(xpad_done, 1)
                    for q in range(NPX):
                        for k in range(TAPS):
                            n = q * TAPS + k
                            if k == 1 and q + 1 < NPX:
                                rest(q + 1)
                            if k == 5 and q + 1 < NPX:
                                low(q + 1)
                            dve.wait_ge(tap_mm, n + 1)
                            if n >= SLOTS:
                                m = n - SLOTS
                                dve.wait_ge(tap_added, m // TAPS * len(TERMS) + term_of[m % TAPS] + 1)
                            di, dj = k // 3, k % 3
                            ins = nc.vector.scalar_tensor_tensor(
                                prod[:, n % SLOTS, :].rearrange("p (r w) -> p r w", w=COLS),
                                ps_tap[n % 4][:, :].rearrange("p (r w) -> p r w", w=COLS), const("conv2_b", 0, P, k, k + 1),
                                xpad[:, q * R + di:q * R + di + R, dj:dj + COLS], ALU.add, ALU.mult)
                            ins.then_inc(tap_prod, 1)
                            if k % 3 == 1:
                                dve.wait_ge(tap_prod, n + 1)
                                nc.vector.tensor_tensor(prod[:, (n - 1) % SLOTS, :], prod[:, (n - 1) % SLOTS, :],
                                                        prod[:, n % SLOTS, :], ALU.add).then_inc(pair_sum, 1)

                @block.gpsimd
                def _(pool):
                    nc.gpsimd.memset(hid[:, TILES - 1, :], 0.0).then_inc(hid_zero, 1)
                    nc.gpsimd.memset(xpad[:, :, :], 0.0).then_inc(pad_zero, 1)
                    for q in range(NPX):
                        a = acc[:, px(q)]
                        for t, taps in enumerate(TERMS):
                            k = taps[-1]
                            n = q * TAPS + k
                            pool.wait_ge(tap_prod, n + 1)
                            if t in (0, 1, 3):
                                pool.wait_ge(pair_sum, 3 * q + (0, 1, None, 2)[t] + 1)
                            other = prod[:, (q * TAPS + taps[0]) % SLOTS, :] if t == 0 else a
                            if q + t > 0:
                                pool.wait_ge(tap_added, q * len(TERMS) + t)
                            nc.gpsimd.tensor_tensor(a, other, prod[:, n % SLOTS, :], ALU.add).then_inc(tap_added, 1)

        HALF = BATCH * FEAT
        GROUPS = TILES * BATCH
        with ExitStack() as st:
            stat = sb(st, "stat", [P, 4, GROUPS])
            cent = sb(st, "cent", [P, TILES, HALF])
            work = sb(st, "work", [P, TILES, HALF])
            normT = sb(st, "normT", [P, PADDED])
            hkq = sb(st, "hkq", [P, 2, 2, BANK])
            feat = [sb(st, f"feat{k}", [P, PADDED]) for k in range(2)]
            fold_abs = [cent[:, :, :].rearrange("p i f -> p (i f)"), work[:, :, :].rearrange("p i f -> p (i f)")]
            ps = [pb(st, f"ps2_{k}", [P, BANK]) for k in range(8)]
            names = ("squares", "centred", "varred", "rooted")
            ln1 = [sem("ln1_" + n) for n in names]
            ln1_done, tr_mm, tr_done = sem("ln1_done"), sem("tr_mm"), sem("tr_done")
            l1_mm, l1_done, l2_mm, l2_done, abs_done, feat_done = (
                sem(n) for n in ("l1_mm", "l1_done", "l2_mm", "l2_done", "abs_done", "feat_done"))
            own = Chain("phase_vector")
            with nc.Block() as block:
                v3 = lambda a: a[:, :, :].rearrange("p i (b f) -> p (i b) f", b=BATCH)

                @block.vector
                def _(dve):
                    normalise_vector(dve, own, v3(hid), v3(cent), v3(work), stat, GROUPS, FEAT, LN_EPS, *ln1)
                    for g in group_pieces(GROUPS):
                        nc.vector.tensor_tensor(v3(cent)[:, g], v3(cent)[:, g], spread(stat[:, 2, g], g, FEAT), ALU.mult)\
                            .then_inc(ln1_done, 1)
                    for k in range(2):
                        dve.wait_ge(l2_done, 2 * len(CHUNKS))
                        nc.vector.scalar_tensor_tensor(fold_abs[k], feat[k][:, :], const("phase", 0, P, 0, 1), feat[k][:, :],
                                                       ALU.mult, ALU.max).then_inc(abs_done, 1)

                @block.tensor
                def _(pe):
                    for c, (c0, w) in enumerate(CHUNKS):
                        pe.wait_ge(ln1_done, piece_of(c) + 1)
                        if c >= 2:
                            pe.wait_ge(tr_done, c - 1)
                        for t in range(w // P):
                            last = nc.tensor.transpose(ps[c % 2][:, t * P:(t + 1) * P], cent[:, c0 // P + t, :], const("ident"))
                        last.then_inc(tr_mm, 1)
                    for c in range(len(CHUNKS) + 1):
                        if c < len(CHUNKS):
                            c0, w = CHUNKS[c]
                            pe.wait_ge(tr_done, c + 1)
                            for k, name in enumerate(("kw1", "qw1")):
                                n = 2 * c + k
                                if n >= 2:
                                    pe.wait_ge(l1_done, n - 1)
                                nc.tensor.matmul(ps[2 + k][:, 0:w], const(name), normT[:, c0:c0 + w], start=True, stop=True)\
                                    .then_inc(l1_mm, 1)
                        if c >= 1:
                            c0, w = CHUNKS[c - 1]
                            for k, name in enumerate(("kw2", "qw2")):
                                n = 2 * (c - 1) + k
                                pe.wait_ge(l1_done, n + 1)
                                if n >= 4:
                                    pe.wait_ge(l2_done, n - 3)
                                nc.tensor.matmul(ps[4 + n % 4][:, 0:w], const(name), hkq[:, (c - 1) % 2, k, 0:w],
                                                 start=True, stop=True).then_inc(l2_mm, 1)

                @block.scalar
                def _(act):
                    normalise_scalar(act, v3(cent), v3(work), stat, GROUPS, *ln1)
                    for c, (c0, w) in enumerate(CHUNKS):
                        act.wait_ge(tr_mm, c + 1)
                        nc.scalar.activation(normT[:, c0:c0 + w], ps[c % 2][:, 0:w], ACT.Copy).then_inc(tr_done, 1)
                    for c in range(len(CHUNKS) + 1):
                        if c < len(CHUNKS):
                            c0, w = CHUNKS[c]
                            for k, name in enumerate(("kb1", "qb1")):
                                n = 2 * c + k
                                act.wait_ge(l1_mm, n + 1)
                                if n >= 4:
                                    act.wait_ge(l2_mm, n - 3)
                                nc.scalar.activation(hkq[:, c % 2, k, 0:w], ps[2 + k][:, 0:w], ACT.Tanh, bias=const(name))\
                                    .then_inc(l1_done, 1)
                        if c >= 1:
                            c0, w = CHUNKS[c - 1]
                            for k, name in enumerate(("kb2", "qb2")):
                                n = 2 * (c - 1) + k
                                act.wait_ge(l2_mm, n + 1)
                                nc.scalar.activation(feat[k][:, c0:c0 + w], ps[4 + n % 4][:, 0:w], ACT.Tanh, bias=const(name))\
                                    .then_inc(l2_done, 1)
                    for k in range(2):
                        act.wait_ge(abs_done, k + 1)
                        nc.scalar.activation(feat[k][:, :], fold_abs[k], ACT.Sin, bias=const("phase", 0, P, 2, 3),
                                             scale=const("phase", 0, P, 1, 2)).then_inc(feat_done, 1)

            val = sb(st, "val", [P, 2, HALF])
            keyT = sb(st, "keyT", [P, 2, P])
            att = sb(st, "att", [P, 2, BATCH, P])
            state = sb(st, "state", [P, 2, HALF])
            v_mm, v_sb, kt_mm, kt_sb, a_mm, a_sb, m_mm, m_sb, o_mm, o_sb, st_zero = (
                sem(n) for n in ("v_mm", "v_sb", "kt_mm", "kt_sb", "a_mm", "a_sb", "m_mm", "m_sb", "o_mm", "o_sb", "st_zero"))
            ps_v, ps_kt, ps_a, ps_m, ps_o = ps[0], ps[1], (ps[2], ps[3]), (ps[4], ps[7]), (ps[5], ps[6])
            with nc.Block() as block:
                @block.tensor
                def _(pe):
                    for i in range(TILES + 1):
                        if i < TILES:
                            t = slice(i * P, (i + 1) * P)
                            if i >= 1:
                                pe.wait_ge(v_sb, i)
                                pe.wait_ge(kt_sb, i)
                                pe.wait_ge(a_sb, 2 * i)
                            nc.tensor.matmul(ps_v[:, 0:HALF], normT[:, t], const("vw"), start=True, stop=True).then_inc(v_mm, 1)
                            nc.tensor.transpose(ps_kt[:, 0:P], feat[0][:, t], const("ident")).then_inc(kt_mm, 1)
                            for b in range(BATCH):
                                r = slice(b * FEAT, (b + 1) * FEAT)
                                nc.tensor.matmul(ps_a[b][:, 0:P], feat[0][r, t], feat[1][r, t], start=True, stop=True)\
                                    .then_inc(a_mm, 1)
                        if i >= 1:
                            j = i - 1
                            t = slice(j * P, (j + 1) * P)
                            if j == 0:
                                pe.wait_ge(st_zero, 2)
                            else:
                                pe.wait_ge(m_sb, BATCH * j)
                            if j >= 2:
                                pe.wait_ge(o_sb, j - 1)
                            o = ps_o[j % 2][:, 0:HALF]
                            nc.tensor.matmul(o, feat[1][:, t], state[:, j % 2, :], start=True, stop=False)
                            pe.wait_ge(v_sb, j + 1)
                            pe.wait_ge(a_sb, 2 * j + 2)
                            for b in range(BATCH):
                                f = slice(b * FEAT, (b + 1) * FEAT)
                                last = nc.tensor.matmul(o[:, f], att[:, j % 2, b, :], val[:, j % 2, f], start=False, stop=(b == 1))
                            last.then_inc(o_mm, 1)
                            if j < TILES - 1:
                                pe.wait_ge(kt_sb, j + 1)
                                nc.tensor.matmul(ps_m[j % 2][:, 0:HALF], keyT[:, j % 2, :], val[:, j % 2, :], start=True,
                                                 stop=True).then_inc(m_mm, 1)

                @block.scalar
                def _(act):
                    for i in range(TILES):
                        act.wait_ge(kt_mm, i + 1)
                        if i >= 2:
                            act.wait_ge(m_mm, i - 1)
                        nc.scalar.activation(keyT[:, i % 2, :], ps_kt[:, 0:P], ACT.Copy).then_inc(kt_sb, 1)

                @block.vector
                def _(dve):
                    for k in range(2):
                        nc.vector.memset(state[:, k, :], 0.0).then_inc(st_zero, 1)
                    for i in range(TILES + 1):
                        if i < TILES:
                            dve.wait_ge(v_mm, i + 1)
                            if i >= 2:
                                dve.wait_ge(o_mm, i - 1)
                                dve.wait_ge(m_mm, i - 1)
                            nc.vector.tensor_tensor(val[:, i % 2, :], ps_v[:, 0:HALF], const("vb"), ALU.add).then_inc(v_sb, 1)
                            for b in range(BATCH):
                                dve.wait_ge(a_mm, 2 * i + b + 1)
                                nc.vector.tensor_tensor(att[:, i % 2, b, :], ps_a[b][:, 0:P], const("keep"), ALU.mult)\
                                    .then_inc(a_sb, 1)
                        if i >= 1:
                            j = i - 1
                            dve.wait_ge(o_mm, j + 1)
                            nc.vector.scalar_tensor_tensor(hid[:, j, :], ps_o[j % 2][:, 0:HALF], const("inv_norm", 0, P, j, j + 1),
                                                           hid[:, j, :], ALU.mult, ALU.add).then_inc(o_sb, 1)
                            if j < TILES - 1:
                                dve.wait_ge(m_mm, j + 1)
                                dve.wait_ge(m_sb, BATCH * j) if j else dve.wait_ge(st_zero, 2)
                                for b in range(BATCH):
                                    f = slice(b * FEAT, (b + 1) * FEAT)
                                    nc.vector.tensor_tensor(state[f, (j + 1) % 2, f], state[f, j % 2, f], ps_m[j % 2][f, f], ALU.add)\
                                        .then_inc(m_sb, 1)

        mid = top.enter_context(ExitStack())
        sx_tok = sb(mid, "sx_tok", [P, TILES, P])
        values = sb(mid, "values", [P, HEADS, TILES * 32])
        with ExitStack() as st:
            stat = sb(st, "stat3", [P, 4, GROUPS])
            cent = sb(st, "cent3", [P, TILES, HALF])
            work = sb(st, "work3", [P, TILES, HALF])
            normT = work[:, :, :].rearrange("p i f -> p (i f)")
            sxT = cent[:, :, :].rearrange("p i f -> p (i f)")
            part = sb(st, "part", [P, 2, 3, PADDED], bf16)
            rest = sb(st, "rest", [P, 3, BANK])
            ps = [pb(st, f"ps3_{k}", [P, BANK]) for k in range(8)]
            ln2 = [sem("ln2_" + n) for n in names]
            (ln2_done, tr2_mm, tr2_done, sx_mm, sx_done, sxt_mm, sxt_done, val_mm, val_done, val_zero, val_one,
             proj_mm, part1, rest1, part2, part3, part_out) = (sem(n) for n in (
                "ln2_done", "tr2_mm", "tr2_done", "sx_mm", "sx_done", "sxt_mm", "sxt_done", "val_mm", "val_done",
                "val_zero", "val_one", "proj_mm", "part1", "rest1", "part2", "part3", "part_out"))
            own = Chain("proj_vector")
            NC = len(CHUNKS)
            MATS = 1 + NE
            vals = values[:, :, :].rearrange("p h (i f) -> p h i f", f=32)
            with nc.Block() as block:
                @block.vector
                def _(dve):
                    normalise_vector(dve, own, v3(hid), v3(cent), v3(work), stat, GROUPS, FEAT, LN_EPS, *ln2)
                    for g in group_pieces(GROUPS):
                        nc.vector.tensor_tensor(v3(cent)[:, g], v3(cent)[:, g], spread(stat[:, 2, g], g, FEAT), ALU.mult)\
                            .then_inc(ln2_done, 1)
                    dve.wait_ge(val_one, HEADS)
                    for c, (c0, w) in enumerate(CHUNKS):
                        dve.wait_ge(sxt_mm, c + 1)
                        nc.vector.tensor_copy(sx_tok[:, :, :].rearrange("p i f -> p (i f)")[:, c0:c0 + w], ps[c % 2][:, 0:w])\
                            .then_inc(sxt_done, 1)
                        dve.wait_ge(val_mm, c + 1)
                        nt = w // P
                        for t in range(nt):
                            last = nc.vector.tensor_copy(
                                vals[:, :, c0 // P + t, 0:HD],
                                ps[2 + c % 2][:, t * P:(t + 1) * P].rearrange("p (h f) -> p h f", f=HD))
                        last.then_inc(val_done, 1)
                    for m in range(MATS):
                        for c, (c0, w) in enumerate(CHUNKS):
                            n = m * NC + c
                            dve.wait_ge(part1, n + 1)
                            if n >= 3:
                                dve.wait_ge(part3, n - 2)
                            nc.vector.scalar_tensor_tensor(rest[:, n % 3, 0:w], ps[4 + n % 4][:, 0:w], 1.0 if m == 0 else float(HD) ** 0.5,
                                                           part[:, m % 2, 0, c0:c0 + w], ALU.mult, ALU.subtract).then_inc(rest1, 1)

                @block.tensor
                def _(pe):
                    for c, (c0, w) in enumerate(CHUNKS):
                        pe.wait_ge(ln2_done, piece_of(c) + 1)
                        if c >= 2:
                            pe.wait_ge(tr2_done, c - 1)
                        for t in range(w // P):
                            last = nc.tensor.transpose(ps[c % 2][:, t * P:(t + 1) * P], cent[:, c0 // P + t, :], const("ident"))
                        last.then_inc(tr2_mm, 1)
                    pe.wait_ge(tr2_done, NC)
                    for c, (c0, w) in enumerate(CHUNKS):
                        if c >= 2:
                            pe.wait_ge(sx_done, c - 1)
                        nc.tensor.matmul(ps[2 + c % 2][:, 0:w], const("hl"), normT[:, c0:c0 + w], start=True, stop=True).then_inc(sx_mm, 1)
                    pe.wait_ge(sx_done, NC)
                    for c, (c0, w) in enumerate(CHUNKS):
                        if c >= 2:
                            pe.wait_ge(sxt_done, c - 1)
                            pe.wait_ge(val_done, c - 1)
                        for t in range(w // P):
                            last = nc.tensor.transpose(ps[c % 2][:, t * P:(t + 1) * P], sxT[:, c0 + t * P:c0 + (t + 1) * P], const("ident"))
                        last.then_inc(sxt_mm, 1)
                        for t in range(w // P):
                            last = nc.tensor.matmul(ps[2 + c % 2][:, t * P:(t + 1) * P], sxT[:, c0 + t * P:c0 + (t + 1) * P], const("wv"),
                                                    start=True, stop=True)
                        last.then_inc(val_mm, 1)
                    for m in range(MATS):
                        wt = const("wk") if m == 0 else const("wq", 0, P, (m - 1) * P, m * P)
                        for c, (c0, w) in enumerate(CHUNKS):
                            n = m * NC + c
                            if n >= 4:
                                pe.wait_ge(rest1, n - 3)
                            nc.tensor.matmul(ps[4 + n % 4][:, 0:w], wt, sxT[:, c0:c0 + w], start=True, stop=True).then_inc(proj_mm, 1)

                @block.scalar
                def _(act):
                    normalise_scalar(act, v3(cent), v3(work), stat, GROUPS, *ln2)
                    act.wait_ge(ln2_done, 1)
                    for c, (c0, w) in enumerate(CHUNKS):
                        act.wait_ge(tr2_mm, c + 1)
                        nc.scalar.activation(normT[:, c0:c0 + w], ps[c % 2][:, 0:w], ACT.Copy).then_inc(tr2_done, 1)
                    act.wait_ge(tr2_mm, NC)
                    for c, (c0, w) in enumerate(CHUNKS):
                        act.wait_ge(sx_mm, c + 1)
                        nc.scalar.activation(sxT[:, c0:c0 + w], ps[2 + c % 2][:, 0:w], ACT.Identity, bias=const("hl_b")).then_inc(sx_done, 1)
                    for m in range(MATS):
                        if m >= 2:
                            act.wait_ge(part_out, 32 * (m - 1))
                        for c in range(NC + 1):
                            if c < NC:
                                c0, w = CHUNKS[c]
                                n = m * NC + c
                                act.wait_ge(proj_mm, n + 1)
                                nc.scalar.activation(part[:, m % 2, 0, c0:c0 + w], ps[4 + n % 4][:, 0:w], ACT.Copy,
                                                     scale=1.0 if m == 0 else float(HD) ** 0.5).then_inc(part1, 1)
                            if c >= 1:
                                c0, w = CHUNKS[c - 1]
                                n = m * NC + c - 1
                                act.wait_ge(rest1, n + 1)
                                nc.scalar.activation(part[:, m % 2, 1, c0:c0 + w], rest[:, n % 3, 0:w], ACT.Copy).then_inc(part2, 1)

                @block.gpsimd
                def _(pool):
                    nc.gpsimd.memset(values[:, :, :], 0.0).then_inc(val_zero, 1)
                    pool.wait_ge(val_zero, 1)
                    for h in range(HEADS):
                        nc.gpsimd.memset(vals[:, h, :, HD:HD + 1], 1.0).then_inc(val_one, 1)
                    for m in range(MATS):
                        if m >= 2:
                            pool.wait_ge(part_out, 32 * (m - 1))
                        for c, (c0, w) in enumerate(CHUNKS):
                            n = m * NC + c
                            pool.wait_ge(part2, n + 1)
                            nc.gpsimd.tensor_tensor(part[:, m % 2, 2, c0:c0 + w], rest[:, n % 3, 0:w], part[:, m % 2, 1, c0:c0 + w],
                                                    ALU.subtract).then_inc(part3, 1)

                @block.sync
                def _(sp):
                    for m in range(MATS):
                        sp.wait_ge(part3, (m + 1) * NC)
                        dst = keys_dram if m == 0 else queries_dram[:, :, m - 1, :]
                        sp.dma_start(dst[:, 0:P, :].rearrange("a p t -> p a t"), part[:, m % 2, :, :]).then_inc(part_out, 16)
                        sp.dma_start(dst[:, P:P + HD, :].rearrange("a p t -> p a t"), part[0:HD, m % 2, :, :]).then_inc(part_out, 16)
                        sp.wait_ge(part_out, 32 * (m + 1))

        attn = sb(mid, "attn", [P, TILES, HEADS, NE * HD])
        K6 = 6 * HD
        KM = K6 + 3 * NE
        QSLOTS = 3
        QGROUPS = -(-TILES // 4)
        EARLY_KEYS = 8 * P
        RING = 4
        with ExitStack() as st:
            keys = sb(st, "keys", [P, PADDED], bf16)
            ahead = sb(st, "ahead", [P, EARLY_KEYS], bf16)
            query = sb(st, "query", [P, QSLOTS, NE, BANK], bf16)
            qlast = sb(st, "qlast", [P, NE, P], bf16)

            def queries_of(i):
                return qlast[:, :, :] if i == TILES - 1 else query[:, i // 4 % QSLOTS, :, i % 4 * P:(i % 4 + 1) * P]

            def load_order(g):
                if g == QGROUPS - 1:
                    return QSLOTS, 1, 1
                return g % QSLOTS, g // QSLOTS + 1, len(range(g % QSLOTS, QGROUPS - 1, QSLOTS))

            vhead = sb(st, "vhead", [P, TILES * 32])
            NP = 8
            prob = sb(st, "prob", [P, NP, BANK])
            osum = sb(st, "osum", [P, 2, BANK])
            identb = sb(st, "identb", [P, P], bf16)
            negs = sb(st, "negs", [P, P], bf16)
            negt = sb(st, "negt", [P, NE, P], bf16)
            pmax = sb(st, "pmax", [P, 2, NE, 8])
            nmax = sb(st, "nmax", [P, 2, NE])
            mrest = sb(st, "mrest", [P, NE])
            mpart = sb(st, "mpart", [P, 2, NE * 32], bf16)
            rden = sb(st, "rden", [P, NE])
            fsum = sb(st, "fsum", [P, NE, HD + 1])
            ps_max = [pb(st, f"ps_max{k}", [P, 2 * BANK]) for k in range(2)]
            ps_ring = [pb(st, f"ps_ring{k}", [P, BANK]) for k in range(RING)]

            prep, head_go, head_done, heads_clear = sem("prep"), sem("head_go"), sem("head_done"), sem("heads_clear")
            k_in = [sem(f"k_in{k}") for k in range(3)]
            q_in = [sem(f"q_in{k}") for k in range(QSLOTS + 1)]
            turns, n_in = sem("turns"), sem("n_in")
            (v_in, qk_mm, exp_done, av_mm, av_read, fold_mm, divided, max_mm, max_read, row_max, split_a, split_b, split_c, max_split,
             bias_mm, bias_in, rec_done, sum_done) = loop_sems = [sem(n) for n in (
                "v_in", "qk_mm", "exp_done", "av_mm", "av_read", "fold_mm", "divided", "max_mm", "max_read", "row_max", "split_a",
                "split_b", "split_c", "max_split", "bias_mm", "bias_in", "rec_done", "sum_done")]

            def max_items(i):
                length = (i + 1) * P
                full, tail = length // (2 * BANK), length % (2 * BANK)
                items = [[(e, u * 2 * BANK, 2 * BANK)] for u in range(full) for e in range(NE)]
                if tail > BANK:
                    items += [[(e, full * 2 * BANK, tail)] for e in range(NE)]
                elif tail:
                    items += [[(e, full * 2 * BANK, tail), (e + 1, full * 2 * BANK, tail)] for e in range(0, NE, 2)]
                return items, full + (tail > 0)

            EARLY = EARLY_KEYS // P
            LAG_AV, LAG_READ, LAG_FOLD, LAG_BIAS = 3, 1, 2, 5
            blocks = [(i, j) for i in range(TILES) for j in range(i + 1)]
            first = {i: i * (i + 1) // 2 for i in range(TILES + 1)}
            total = len(blocks)
            KPIECES = [(0, 16 * P), (16 * P, 32 * P), (32 * P, PADDED)]
            nblock = {b: n for n, b in enumerate(blocks)}
            SHORT = first[3]
            quadrant = lambda i, j: j if i < 3 else (nblock[(i, j)] - SHORT) % 4
            groups = [blocks[first[i]:first[i + 1]] for i in range(3)] + [blocks[n:n + 4] for n in range(SHORT, total, 4)]
            group_of = {b: g for g, members in enumerate(groups) for b in members}

            class Plan:
                def __init__(self, rows, with_weights):
                    self.rows, self.steps = rows, []
                    self.order = {row: n for n, row in enumerate(rows)}
                    queue = [(row, k, sum(w for _, _, w in items) / BANK)
                             for row in rows for k, items in enumerate(max_items(row[0])[0])]
                    self.max_number = {(row, k): n for n, (row, k, _) in enumerate(queue)}
                    work = sum(w for _, _, w in queue)
                    ready, biased, done = {}, 0, 0.0

                    def maxima(k, goal):
                        nonlocal done
                        while queue and done < goal:
                            row, item, w = queue.pop(0)
                            done += w
                            self.steps.append(("max", row[0], item, row[1]))
                            if not queue or queue[0][0] != row:
                                self.steps.append(("rowmax", row[0], 0, row[1]))
                                ready[row] = k

                    def bias(k):
                        nonlocal biased
                        while biased < len(rows) and rows[biased] in ready and k >= ready[rows[biased]] + LAG_BIAS:
                            self.steps.append(("bias", rows[biased][0], 0, rows[biased][1]))
                            biased += 1

                    if with_weights:
                        pending, fold_at = {}, {}
                        av_at = [nblock[members[-1]] + LAG_AV for members in groups]
                        read_at = [av_at[group_of[(i, i)]] + LAG_READ for i in range(TILES)]
                        for g, k in enumerate(av_at):
                            pending.setdefault(k, []).append((2, "av", g, 0))
                        for i in range(TILES):
                            pending.setdefault(read_at[i], []).append((1, "read", i, 0))
                            fold_at[i] = min([read_at[i] + LAG_FOLD] + read_at[i + 2:i + 3])
                            pending.setdefault(fold_at[i], []).append((0, "fold", i, 0))
                        for i in range(TILES):
                            limit = fold_at.get(i + 1, fold_at[i] + 4)
                            pending.setdefault(min(fold_at[i] + 2, limit), []).append((-2, "invert", i, 0))
                            pending.setdefault(min(fold_at[i] + 4, limit), []).append((-1, "scale", i, 0))
                        for k in range(total + LAG_AV + LAG_READ + LAG_FOLD + 4):
                            self.steps += [(kind, i, g, False) for _, kind, i, g in sorted(pending.get(k, []))]
                            bias(k)
                            if k < total:
                                self.steps.append(("score", *blocks[k], False))
                                maxima(k, (k + 1) * (work + 3) / total - 1)
                        maxima(k, work)
                    else:
                        for k in range(int(work) + LAG_BIAS + 1):
                            maxima(k, k + 1)
                            bias(k)
                        maxima(k, work)
                    bias(k + LAG_BIAS)
                    self.bank_of, self.use_before, last = {}, {}, {}
                    free = list(range(RING))
                    for s in self.steps:
                        uses = [s] if s[0] in ("score", "bias", "fold") else []
                        if s[0] == "av":
                            uses = [("sums", i) for i, j in groups[s[1]] if j == 0]
                        for use in uses:
                            bank = free.pop(0)
                            self.bank_of[use], self.use_before[use], last[bank] = bank, last.get(bank), use
                            if s[0] != "av":
                                free.append(bank)
                        if s[0] == "read":
                            free.append(self.bank_of[("sums", s[1])])
                    self.weights = total if with_weights else 0

            opening = Plan([(i, True) for i in range(EARLY)], False)
            turn = Plan([(i, False) for i in range(EARLY, TILES)] + [(i, True) for i in range(EARLY)], True)

            with nc.Block() as block:
                @block.sync
                def _(sp):
                    def load_keys(head_row, piece):
                        c0, c1 = KPIECES[piece]
                        for k in range(3):
                            r0 = (0, 3 * HD, 5 * HD)[k]
                            sp.dma_start(keys[r0:r0 + (3 - k) * HD, c0:c1],
                                         keys_dram[0:3 - k, bass.ds(head_row, HD), c0:c1]).then_inc(k_in[piece], 16)

                    def load_queries(head_row, g):
                        w = min(BANK, PADDED - g * BANK)
                        for k in range(3):
                            r0 = (0, 3 * HD, 5 * HD)[k]
                            for c in range(3 - k):
                                rows, slot = slice(r0 + c * HD, r0 + (c + 1) * HD), load_order(g)[0]
                                dst = qlast[rows, :, :] if g == QGROUPS - 1 else query[rows, slot, :, :]
                                sp.dma_start(dst, queries_dram[k, bass.ds(head_row, HD), :, g * BANK:g * BANK + w])\
                                    .then_inc(q_in[slot], 16)

                    def load_ahead(head_row):
                        for k in range(3):
                            r0 = (0, 3 * HD, 5 * HD)[k]
                            sp.dma_start(ahead[r0:r0 + (3 - k) * HD, :],
                                         keys_dram[0:3 - k, bass.ds(head_row, HD), 0:EARLY_KEYS]).then_inc(n_in, 16)

                    def clear(done):
                        sp.wait_ge(head_done, done)
                        sp.sem_inc(turns, 1)
                        sp.sem_clear(range(loop_sems[0].num, loop_sems[-1].num + 1))
                        sp.sem_inc(heads_clear, 1)

                    load_ahead(0)
                    for g in range(QSLOTS):
                        load_queries(0, g)
                    for piece in range(3):
                        load_keys(0, piece)
                    clear(4)
                    with sp.Fori(0, TURNS) as h:
                        load_ahead(h * HD + HD)
                        load_queries(h * HD, QGROUPS - 1)
                        for g in range(QSLOTS, QGROUPS - 1):
                            sp.wait_ge(qk_mm, first[4 * (g - QSLOTS + 1)])
                            load_queries(h * HD, g)
                        for g in sorted(range(QSLOTS), key=lambda g: (g - QGROUPS + 1) % QSLOTS):
                            before = max(x for x in range(QGROUPS - 1) if x % QSLOTS == g)
                            sp.wait_ge(qk_mm, first[4 * (before + 1)])
                            load_queries(h * HD + HD, g)
                        for piece in range(3):
                            sp.wait_ge(qk_mm, first[TILES - 1] + KPIECES[piece][1] // P)
                            load_keys(h * HD + HD, piece)
                        clear(4 * h + 8)
                    for piece in range(3):
                        sp.wait_ge(k_in[piece], 48 * (TURNS + 1))
                    for g in range(QSLOTS):
                        slot, nth, loads = load_order(g)
                        sp.wait_ge(q_in[slot], 96 * (TURNS * loads + nth))

                @block.gpsimd
                def _(pool):
                    nc.gpsimd.memset(keys[K6:P, :], 1.0).then_inc(prep, 1)
                    pool.wait_ge(prep, 1)
                    nc.gpsimd.memset(mpart[:, :, :], 0.0).then_inc(prep, 1)
                    nc.gpsimd.tensor_copy(identb[:, :], const("ident")).then_inc(prep, 1)
                    nc.gpsimd.tensor_copy(negs[:, :], const("neg_s")).then_inc(prep, 1)
                    for e in range(NE):
                        nc.gpsimd.tensor_copy(negt[:, e, :], const("neg_t")).then_inc(prep, 1)
                    pool.wait_ge(prep, 4 + NE)
                    def split_maxima(plan):
                        for n in range(len(plan.rows)):
                            diag = [mpart[:, n % 2, 4 * a:][:, 0:3 * 33 + 1:33] for a in range(3)]
                            pool.wait_ge(row_max, n + 1)
                            if n >= 2:
                                pool.wait_ge(bias_mm, n - 1)
                            nc.gpsimd.tensor_copy(diag[0], nmax[:, n % 2, :]).then_inc(split_a, 1)
                            pool.wait_ge(split_a, n + 1)
                            nc.gpsimd.tensor_tensor(mrest[:, :], nmax[:, n % 2, :], diag[0], ALU.subtract).then_inc(split_b, 1)
                            pool.wait_ge(split_b, n + 1)
                            nc.gpsimd.tensor_copy(diag[1], mrest[:, :]).then_inc(split_c, 1)
                            pool.wait_ge(split_c, n + 1)
                            nc.gpsimd.tensor_tensor(diag[2], mrest[:, :], diag[1], ALU.subtract).then_inc(max_split, 1)
                        pool.wait_ge(max_split, len(plan.rows))
                        pool.sem_inc(head_done, 1)

                    split_maxima(opening)
                    pool.wait_ge(heads_clear, 1)
                    with pool.Fori(0, TURNS) as h:
                        for c0, c1 in ((0, 4 * 32), (4 * 32, TILES * 32)):
                            nc.gpsimd.tensor_copy(vhead[:, c0:c1].unsqueeze(1), values[:, bass.ds(h, 1), c0:c1]).then_inc(v_in, 1)
                        split_maxima(turn)
                        pool.wait_ge(heads_clear, h + 2)

                @block.scalar
                def _(act):
                    def follow(plan):
                        for step in plan.steps:
                            kind, i, j, is_next = step
                            if kind == "score":
                                n = nblock[(i, j)]
                                act.wait_ge(qk_mm, n + 1)
                                if n >= NP:
                                    act.wait_ge(av_mm, group_of[blocks[n - NP]] + 1)
                                nc.scalar.activation(prob[:, n % NP, :], ps_ring[plan.bank_of[step]][:, :], ACT.Exp).then_inc(exp_done, 1)
                            elif kind == "bias":
                                act.wait_ge(bias_mm, plan.order[(i, is_next)] + 1)
                                nc.scalar.activation(queries_of(i)[K6:KM],
                                                     ps_ring[plan.bank_of[step]][K6:KM, :].rearrange("p (e s) -> p e s", e=NE),
                                                     ACT.Copy).then_inc(bias_in, 1)
                            elif kind == "read":
                                act.wait_ge(av_mm, group_of[(i, i)] + 1)
                                if i >= 2:
                                    act.wait_ge(fold_mm, i - 1)
                                k = min(P, 32 * (i + 1))
                                nc.scalar.activation(osum[0:k, i % 2, :], ps_ring[plan.bank_of[("sums", i)]][0:k, :], ACT.Copy)\
                                    .then_inc(av_read, 1)
                        act.wait_ge(bias_in, len(plan.rows))
                        if plan.weights:
                            act.wait_ge(exp_done, total)
                            act.wait_ge(divided, TILES)
                        act.sem_inc(head_done, 1)

                    follow(opening)
                    act.wait_ge(heads_clear, 1)
                    with act.Fori(0, TURNS) as h:
                        follow(turn)
                        act.wait_ge(heads_clear, h + 2)

                @block.vector
                def _(dve):
                    def follow(plan, h):
                        for step in plan.steps:
                            kind, i, j, is_next = step
                            if kind == "max":
                                n = plan.max_number[((i, is_next), j)]
                                slot = plan.order[(i, is_next)] % 2
                                pieces = max_items(i)[0][j]
                                e0, key0, w = pieces[0]
                                u = key0 // (2 * BANK)
                                dve.wait_ge(max_mm, n + 1)
                                if len(pieces) == 1:
                                    src, dst = ps_max[n % 2][:, 0:w], pmax[:, slot, e0, u:u + 1]
                                else:
                                    src = ps_max[n % 2][:, :].rearrange("p (a c) -> p a c", a=2)[:, :, 0:w]
                                    dst = pmax[:, slot, e0:e0 + 2, u]
                                nc.vector.tensor_reduce(dst, src, AX.X, ALU.max).then_inc(max_read, 1)
                            elif kind == "rowmax":
                                n = plan.order[(i, is_next)]
                                items, parts = max_items(i)
                                dve.wait_ge(max_read, plan.max_number[((i, is_next), len(items) - 1)] + 1)
                                if n >= 2:
                                    dve.wait_ge(max_split, n - 1)
                                nc.vector.tensor_reduce(nmax[:, n % 2, :], pmax[:, n % 2, :, 0:parts], AX.X, ALU.max, negate=True)\
                                    .then_inc(row_max, 1)
                            elif kind == "fold":
                                dve.wait_ge(fold_mm, i + 1)
                                o = ps_ring[plan.bank_of[step]][:, :].rearrange("p (e q f) -> p e f q", e=NE, q=4)
                                if i >= 1:
                                    dve.wait_ge(divided, i)
                                nc.vector.tensor_reduce(fsum[:, :, :], o[:, :, 0:HD + 1, 0:min(4, i + 1)], AX.X, ALU.add)\
                                    .then_inc(sum_done, 1)
                            elif kind == "invert":
                                dve.wait_ge(sum_done, i + 1)
                                nc.vector.reciprocal(rden[:, :], fsum[:, :, HD]).then_inc(rec_done, 1)
                            elif kind == "scale":
                                dve.wait_ge(rec_done, i + 1)
                                nc.vector.tensor_tensor(
                                    attn[:, i, bass.ds(h, 1), :].rearrange("p a (e f) -> p (a e) f", e=NE), fsum[:, :, 0:HD],
                                    rden[:, :].unsqueeze(2).to_broadcast([P, NE, HD]), ALU.mult).then_inc(divided, 1)
                        dve.wait_ge(row_max, len(plan.rows))
                        if plan.weights:
                            dve.wait_ge(divided, TILES)
                        dve.sem_inc(head_done, 1)

                    follow(opening, 0)
                    dve.wait_ge(heads_clear, 1)
                    with dve.Fori(0, TURNS) as h:
                        follow(turn, h)
                        dve.wait_ge(heads_clear, h + 2)

                @block.tensor
                def _(pe):
                    def bank_let_go(plan, use):
                        before = plan.use_before[use]
                        if before:
                            if before[0] == "score":
                                pe.wait_ge(exp_done, nblock[before[1:3]] + 1)
                            elif before[0] == "bias":
                                pe.wait_ge(bias_in, plan.order[(before[1], before[3])] + 1)
                            elif before[0] == "sums":
                                pe.wait_ge(av_read, before[1] + 1)
                            else:
                                pe.wait_ge(sum_done, before[1] + 1)
                        return ps_ring[plan.bank_of[use]]

                    def follow(plan, h):
                        if plan.weights:
                            pe.wait_ge(k_in[0], 48 * h + 48)
                        for step in plan.steps:
                            kind, i, j, is_next = step
                            if step in plan.bank_of:
                                bank = bank_let_go(plan, step)
                            if kind == "max":
                                n = plan.max_number[((i, is_next), j)]
                                if j == 0 and i % 4 == 0:
                                    slot, nth, turns_loads = load_order(i // 4)
                                    pe.wait_ge(q_in[slot], 96 * turns_loads * (h + 1 if is_next else h) + 96 * nth)
                                if j == 0 and i == 0:
                                    pe.wait_ge(n_in, 48 * (h + 1) + 48)
                                if j == 0 and not is_next and (i * P) in (KPIECES[1][0], KPIECES[2][0]):
                                    pe.wait_ge(k_in[1 if i * P == KPIECES[1][0] else 2], 48 * h + 48)
                                if n >= 2:
                                    pe.wait_ge(max_read, n - 1)
                                source = ahead if is_next else keys
                                for a, (e, key0, w) in enumerate(max_items(i)[0][j]):
                                    for c in range(0, w, BANK):
                                        cw = min(BANK, w - c)
                                        diag = key0 + c + cw == (i + 1) * P
                                        o = ps_max[n % 2][:, a * BANK + c:a * BANK + c + cw]
                                        last = nc.tensor.matmul(o, queries_of(i)[0:K6, e], source[0:K6, key0 + c:key0 + c + cw],
                                                                start=True, stop=not diag)
                                        if diag:
                                            last = nc.tensor.matmul(o[:, cw - P:cw], identb[:, :], negs[:, :], start=False, stop=True)
                                last.then_inc(max_mm, 1)
                            elif kind == "bias":
                                n = plan.order[(i, is_next)]
                                pe.wait_ge(max_split, n + 1)
                                for e in range(NE):
                                    last = nc.tensor.matmul(bank[K6:K6 + 32, e * P:(e + 1) * P], mpart[:, n % 2, e * 32:(e + 1) * 32],
                                                            identb[:, :], start=True, stop=True)
                                last.then_inc(bias_mm, 1)
                            elif kind == "score":
                                n = nblock[(i, j)]
                                if j == 0 and i >= EARLY:
                                    pe.wait_ge(bias_in, plan.order[(i, False)] + 1)
                                o = bank[:, :].rearrange("p (e s) -> p e s", e=NE)
                                last = nc.tensor.matmul(o, keys[0:KM, j * P:(j + 1) * P], queries_of(i)[0:KM], start=True, stop=(j < i))
                                if j == i:
                                    last = nc.tensor.matmul(o, identb[:, :], negt[:, :, :], start=False, stop=True)
                                last.then_inc(qk_mm, 1)
                            elif kind == "av":
                                members = groups[i]
                                pe.wait_ge(exp_done, nblock[members[-1]] + 1)
                                for ii, jj in members:
                                    if (ii, jj) in ((0, 0), (4, 4)):
                                        pe.wait_ge(v_in, 1 + (ii > 0))
                                    bank = bank_let_go(plan, ("sums", ii)) if jj == 0 else ps_ring[plan.bank_of[("sums", ii)]]
                                    q = quadrant(ii, jj)
                                    last = nc.tensor.matmul(bank[32 * q:32 * q + 32, :], vhead[:, jj * 32:(jj + 1) * 32],
                                                            prob[:, nblock[(ii, jj)] % NP, :], start=(jj < 4), stop=(jj + 4 > ii))
                                last.then_inc(av_mm, 1)
                            elif kind == "fold":
                                pe.wait_ge(av_read, i + 1)
                                k = min(P, 32 * (i + 1))
                                for e in range(NE):
                                    last = nc.tensor.transpose(bank[:, e * P:e * P + k], osum[0:k, i % 2, e * P:(e + 1) * P],
                                                               const("ident", 0, k, 0, k))
                                last.then_inc(fold_mm, 1)
                        if plan.weights:
                            pe.wait_ge(divided, TILES)
                        pe.wait_ge(bias_in, len(plan.rows))
                        pe.sem_inc(head_done, 1)

                    pe.wait_ge(prep, 4 + NE)
                    follow(opening, -1)
                    pe.wait_ge(heads_clear, 1)
                    with pe.Fori(0, TURNS) as h:
                        follow(turn, h)
                        pe.wait_ge(heads_clear, h + 2)

        with ExitStack() as st:
            nz = sb(st, "nz", [P, TILES, P])
            gate = sb(st, "gate_w", [P, TILES, HEADS * NE])
            gsum = sb(st, "gsum", [P, 2, TILES * HEADS])
            mix = sb(st, "mix", [P, TILES, P])
            prodg = sb(st, "prodg", [P, 1, TILES, NE * HD])
            stat = sb(st, "stat5", [P, 4, TILES * HEADS])
            ps = [pb(st, f"ps5_{k}", [P, BANK]) for k in range(8)]
            fT = values[:, 0:4, :].rearrange("p h c -> p (h c)")
            hT = values[:, 4:8, :].rearrange("p h c -> p (h c)")
            vflat = values[:, :, :].rearrange("p h c -> p (h c)")
            gT = vflat[:, 0:8 * BANK].rearrange("p (k c) -> p k c", k=8)
            glT = vflat[:, 8 * BANK:10 * BANK].rearrange("p (k c) -> p k c", k=2)
            flat = lambda a: a[:, :, :].rearrange("p i f -> p (i f)")
            G = TILES * HEADS
            g16 = lambda a: a[:, :, :].rearrange("p i (g d) -> p (i g) d", d=HD)
            (g_masked, gt_mm, gt_sb, gl_mm, g_sub, g_exp, fn_done, ft_mm, ft_sb, f1_mm, f1_relu, f1_done, f2_mm, fout_done, fo_mm, fo_sb,
             fg_mm, fg_sub, fg_exp, final, stored) = (sem(n) for n in (
                "g_masked", "gt_mm", "gt_sb", "gl_mm", "g_sub", "g_exp", "fn_done", "ft_mm", "ft_sb", "f1_mm", "f1_relu", "f1_done", "f2_mm",
                "fout_done", "fo_mm", "fo_sb", "fg_mm", "fg_sub", "fg_exp", "final", "stored"))
            f2_read = sem("f2_read")
            ln3 = [sem("ln3_" + n) for n in names]
            ln4 = [sem("ln4_" + n) for n in names]
            own = Chain("ffn_vector")
            scratch = attn[:, :, :, :].rearrange("p h i f -> p (h i f)")
            cent = scratch[:, 0:PADDED].rearrange("p (g d) -> p g d", d=HD)
            work = scratch[:, PADDED:2 * PADDED].rearrange("p (g d) -> p g d", d=HD)
            PAIRS, NC = HEADS // 2, len(CHUNKS)
            gate_bank, glT_bank, gl_banks = [ps[0], ps[1], ps[5], ps[6]], ps[7], ps[2:5]
            gl_sb, gb_mm, gb_read = sem("gl_sb"), sem("gb_mm"), sem("gb_read")

            def broad(row, groups):
                return row.unsqueeze(1).to_broadcast([P, groups.stop - groups.start, HD])

            with nc.Block() as block:
                @block.vector
                def _(dve):
                    own(dve, nc.vector.tensor_scalar(flat(nz), flat(sx_tok), 0.0, None, ALU.not_equal))
                    for a0, a1 in PIECES:
                        tiles = slice(a0, a1)
                        for h in range(HEADS):
                            a = attn[:, tiles, h, :].rearrange("p i (e d) -> p i e d", e=NE)
                            m = nz[:, tiles, h * HD:(h + 1) * HD].unsqueeze(2)
                            masked = nc.vector.tensor_tensor(a, a, m.to_broadcast([P, tiles.stop - tiles.start, NE, HD]), ALU.mult)
                            if h < HEADS - 1:
                                own(dve, masked)
                            else:
                                masked.then_inc(g_masked, 1)
                    dve.wait_ge(g_masked, len(PIECES))
                    bias = const("gate_b").rearrange("p (q c) -> p q c", q=PAIRS).unsqueeze(1)
                    for c, (c0, w) in enumerate(CHUNKS):
                        i0, nt = c0 // P, w // P
                        dve.wait_ge(gb_mm, c + 1)
                        nc.vector.tensor_tensor(
                            gate[:, i0:i0 + nt, :].rearrange("p i (q c) -> p i q c", q=PAIRS),
                            gl_banks[c % 3][:, 0:w].rearrange("p (i q c) -> p i q c", q=PAIRS, c=32)[:, :, :, 0:8],
                            bias.to_broadcast([P, nt, PAIRS, 8]), ALU.add).then_inc(gb_read, 1)
                    dve.wait_ge(gb_read, NC)
                    gate4 = gate[:, :, :].rearrange("p i (g e) -> p (i g) e", e=NE)
                    own(dve, nc.vector.tensor_reduce(gsum[:, 0, :], gate4, AX.X, ALU.max))
                    nc.vector.tensor_tensor(gate4, gate4, gsum[:, 0, :].unsqueeze(2).to_broadcast([P, G, NE]), ALU.subtract).then_inc(g_sub, 1)
                    dve.wait_ge(g_exp, 1)
                    own(dve, nc.vector.tensor_reduce(gsum[:, 1, :], gate4, AX.X, ALU.add))
                    own(dve, nc.vector.reciprocal(gsum[:, 1, :], gsum[:, 1, :]))
                    own(dve, nc.vector.tensor_tensor(gate4, gate4, gsum[:, 1, :].unsqueeze(2).to_broadcast([P, G, NE]), ALU.mult))
                    for h in range(HEADS):
                        a = attn[:, :, h, :].rearrange("p i (e d) -> p i e d", e=NE)
                        own(dve, nc.vector.tensor_tensor(
                            prodg[:, 0, :, :].rearrange("p i (e d) -> p i e d", e=NE), a,
                            gate[:, :, h * NE:(h + 1) * NE].unsqueeze(3).to_broadcast([P, TILES, NE, HD]), ALU.mult))
                        own(dve, nc.vector.tensor_reduce(mix[:, :, h * HD:(h + 1) * HD],
                                                         prodg[:, 0, :, :].rearrange("p i (e d) -> p i d e", e=NE), AX.X, ALU.add))
                    for b in range(BATCH):
                        for n0, n1 in ((0, 1), (1, NH)):
                            m = mix[:, :, (b * NH + n0) * HD:(b * NH + n1) * HD]
                            src = min(n0, BATCH - 1) * NH
                            own(dve, nc.vector.tensor_tensor(m, m, sx_tok[:, :, (src + n0) * HD:(src + n1) * HD], ALU.add))
                    normalise_vector(dve, own, g16(mix), cent, work, stat, G, HD, FFN_EPS, *ln3)
                    for g in group_pieces(G):
                        own(dve, nc.vector.tensor_tensor(cent[:, g], cent[:, g], spread(stat[:, 2, g], g, HD), ALU.mult))
                        own(dve, nc.vector.tensor_tensor(cent[:, g], cent[:, g], broad(const("ln_g"), g), ALU.mult))
                        nc.vector.tensor_tensor(g16(mix)[:, g], cent[:, g], broad(const("ln_b"), g), ALU.add).then_inc(fn_done, 1)
                    for c, (c0, w) in enumerate(CHUNKS):
                        dve.wait_ge(f1_relu, c + 1)
                        nc.vector.scalar_tensor_tensor(hT[:, c0:c0 + w], fT[:, c0:c0 + w], 0.0, hT[:, c0:c0 + w],
                                                       ALU.not_equal, ALU.mult).then_inc(f1_done, 1)
                    c3 = cent.rearrange("p (i g) d -> p i (g d)", i=TILES)
                    for c, (c0, w) in enumerate(CHUNKS):
                        dve.wait_ge(f2_mm, c + 1)
                        i0, nt = c0 // P, w // P
                        cc = c3[:, i0:i0 + nt, :]
                        nc.vector.tensor_tensor(cc, ps[c % 2][:, 0:w].rearrange("p (i f) -> p i f", f=P),
                                                const("fc2_b").unsqueeze(1).to_broadcast([P, nt, P]), ALU.add).then_inc(f2_read, 1)
                    dve.wait_ge(f2_read, len(CHUNKS))
                    own(dve, nc.vector.scalar_tensor_tensor(cent, g16(mix), 0.0, cent, ALU.not_equal, ALU.mult))
                    own(dve, nc.vector.tensor_tensor(g16(mix), cent, g16(mix), ALU.add))
                    normalise_vector(dve, own, g16(mix), cent, work, stat, G, HD, FFN_EPS, *ln4)
                    for g in group_pieces(G):
                        own(dve, nc.vector.tensor_tensor(cent[:, g], cent[:, g], spread(stat[:, 2, g], g, HD), ALU.mult))
                        own(dve, nc.vector.tensor_tensor(cent[:, g], cent[:, g], broad(const("fn_g"), g), ALU.mult))
                        nc.vector.tensor_tensor(g16(mix)[:, g], cent[:, g], broad(const("fn_b"), g), ALU.add).then_inc(fout_done, 1)
                    dve.wait_ge(fg_mm, TILES)
                    lg = ps[2][:, 0:G].rearrange("p (g n) -> p g n", n=NH)
                    own(dve, nc.vector.tensor_reduce(stat[:, 0, 0:GROUPS], lg, AX.X, ALU.max))
                    fgv = gsum[:, 0, :].rearrange("p (g n) -> p g n", n=NH)
                    nc.vector.tensor_tensor(fgv, lg, stat[:, 0, 0:GROUPS].unsqueeze(2).to_broadcast([P, GROUPS, NH]), ALU.subtract)\
                        .then_inc(fg_sub, 1)
                    dve.wait_ge(fg_exp, 1)
                    own(dve, nc.vector.tensor_reduce(stat[:, 1, 0:GROUPS], fgv, AX.X, ALU.add))
                    own(dve, nc.vector.reciprocal(stat[:, 1, 0:GROUPS], stat[:, 1, 0:GROUPS]))
                    own(dve, nc.vector.tensor_tensor(fgv, fgv, stat[:, 1, 0:GROUPS].unsqueeze(2).to_broadcast([P, GROUPS, NH]), ALU.mult))
                    own(dve, nc.vector.tensor_tensor(g16(mix), g16(mix), gsum[:, 0, :].unsqueeze(2).to_broadcast([P, G, HD]), ALU.mult))
                    nc.vector.tensor_tensor(flat(mix), flat(mix), flat(hid), ALU.add).then_inc(final, 1)

                @block.tensor
                def _(pe):
                    for c in range(NC + 2):
                        if c < NC:
                            c0, w = CHUNKS[c]
                            pe.wait_ge(g_masked, piece_of(c) + 1)
                            for p in range(PAIRS):
                                if c >= 1:
                                    pe.wait_ge(gt_sb, PAIRS * (c - 1) + p + 1)
                                for t in range(w // P):
                                    last = nc.tensor.transpose(gate_bank[p][:, t * P:(t + 1) * P],
                                                               attn[:, c0 // P + t, 2 * p:2 * p + 2, :].rearrange("p h f -> p (h f)"),
                                                               const("ident"))
                                last.then_inc(gt_mm, 1)
                        if 1 <= c <= NC:
                            d = c - 1
                            w = CHUNKS[d][1]
                            pe.wait_ge(gt_sb, PAIRS * (d + 1))
                            if d >= 1:
                                pe.wait_ge(gl_sb, d)
                            for p in range(PAIRS):
                                last = nc.tensor.matmul(glT_bank[32 * p:32 * p + 32, 0:w], const("gate", 0, P, 32 * (p % 2), 32 * (p % 2) + 32),
                                                        gT[:, (PAIRS * d + p) % 8, 0:w], start=True, stop=True)
                            last.then_inc(gl_mm, 1)
                        if c >= 2:
                            d = c - 2
                            pe.wait_ge(gl_sb, d + 1)
                            if d >= 3:
                                pe.wait_ge(gb_read, d - 2)
                            for t in range(CHUNKS[d][1] // P):
                                last = nc.tensor.transpose(gl_banks[d % 3][:, t * P:(t + 1) * P], glT[:, d % 2, t * P:(t + 1) * P], const("ident"))
                            last.then_inc(gb_mm, 1)
                    for c, (c0, w) in enumerate(CHUNKS):
                        pe.wait_ge(fn_done, piece_of(c) + 1)
                        if c >= 2:
                            pe.wait_ge(ft_sb, c - 1)
                        for t in range(w // P):
                            last = nc.tensor.transpose(ps[c % 2][:, t * P:(t + 1) * P], mix[:, c0 // P + t, :], const("ident"))
                        last.then_inc(ft_mm, 1)
                    for c, (c0, w) in enumerate(CHUNKS):
                        pe.wait_ge(ft_sb, c + 1)
                        if c >= 2:
                            pe.wait_ge(f1_relu, c - 1)
                        nc.tensor.matmul(ps[2 + c % 2][:, 0:w], const("fc1"), fT[:, c0:c0 + w], start=True, stop=True).then_inc(f1_mm, 1)
                    for c, (c0, w) in enumerate(CHUNKS):
                        pe.wait_ge(f1_done, c + 1)
                        if c >= 2:
                            pe.wait_ge(f2_read, c - 1)
                        for t in range(w // P):
                            last = nc.tensor.matmul(ps[c % 2][:, t * P:(t + 1) * P], hT[:, c0 + t * P:c0 + (t + 1) * P], const("fc2"),
                                                    start=True, stop=True)
                        last.then_inc(f2_mm, 1)
                    for c, (c0, w) in enumerate(CHUNKS):
                        pe.wait_ge(fout_done, piece_of(c) + 1)
                        if c >= 2:
                            pe.wait_ge(fo_sb, c - 1)
                        for t in range(w // P):
                            last = nc.tensor.transpose(ps[c % 2][:, t * P:(t + 1) * P], mix[:, c0 // P + t, :], const("ident"))
                        last.then_inc(fo_mm, 1)
                    for i in range(TILES):
                        pe.wait_ge(fo_sb, i // 4 + 1)
                        nc.tensor.matmul(ps[2][:, i * 8:(i + 1) * 8], fT[:, i * P:(i + 1) * P], const("fgate"), start=True, stop=True)\
                            .then_inc(fg_mm, 1)

                @block.scalar
                def _(act):
                    for c in range(NC + 1):
                        if c < NC:
                            w = CHUNKS[c][1]
                            for p in range(PAIRS):
                                act.wait_ge(gt_mm, PAIRS * c + p + 1)
                                if c >= 2:
                                    act.wait_ge(gl_mm, c - 1)
                                nc.scalar.activation(gT[:, (PAIRS * c + p) % 8, 0:w], gate_bank[p][:, 0:w], ACT.Copy).then_inc(gt_sb, 1)
                        if c >= 1:
                            d = c - 1
                            act.wait_ge(gl_mm, d + 1)
                            if d >= 2:
                                act.wait_ge(gb_mm, d - 1)
                            nc.scalar.activation(glT[:, d % 2, 0:CHUNKS[d][1]], glT_bank[:, 0:CHUNKS[d][1]], ACT.Copy).then_inc(gl_sb, 1)
                    act.wait_ge(g_sub, 1)
                    nc.scalar.activation(flat(gate), flat(gate), ACT.Exp).then_inc(g_exp, 1)
                    normalise_scalar(act, cent, work, stat, G, *ln3)
                    for c, (c0, w) in enumerate(CHUNKS):
                        act.wait_ge(ft_mm, c + 1)
                        nc.scalar.activation(fT[:, c0:c0 + w], ps[c % 2][:, 0:w], ACT.Copy).then_inc(ft_sb, 1)
                    for c, (c0, w) in enumerate(CHUNKS):
                        act.wait_ge(f1_mm, c + 1)
                        nc.scalar.activation(hT[:, c0:c0 + w], ps[2 + c % 2][:, 0:w], ACT.Relu, bias=const("fc1_b")).then_inc(f1_relu, 1)
                    normalise_scalar(act, cent, work, stat, G, *ln4)
                    for c, (c0, w) in enumerate(CHUNKS):
                        act.wait_ge(fo_mm, c + 1)
                        nc.scalar.activation(fT[:, c0:c0 + w], ps[c % 2][:, 0:w], ACT.Copy).then_inc(fo_sb, 1)
                    act.wait_ge(fg_sub, 1)
                    nc.scalar.activation(gsum[:, 0, :], gsum[:, 0, :], ACT.Exp).then_inc(fg_exp, 1)

                @block.sync
                def _(sp):
                    sp.wait_ge(final, 1)
                    for b in range(BATCH):
                        f = slice(b * FEAT, (b + 1) * FEAT)
                        sp.dma_start(out[b, 0:IMAGE, :].rearrange("(i p) f -> p i f", p=P), mix[:, 0:TILES - 1, f]).then_inc(stored, 16)
                        sp.dma_start(out[b, IMAGE:TOKENS, :], mix[0:TEXT, TILES - 1, f]).then_inc(stored, 16)
                    sp.wait_ge(stored, 16 * 2 * BATCH)


def pack_constants(w):
    c = np.zeros((P, PACKED), np.float32)

    def put(name, array, p0=0, c0=0):
        a = AT[name][0] + c0
        c[p0:p0 + array.shape[0], a:a + array.shape[1]] = array

    def diagonal(name, block, copies, c0=0):
        for k in range(copies):
            put(name, block, k * block.shape[0], c0 + k * block.shape[1])

    def row(name, vector):
        put(name, np.broadcast_to(vector[None, :], (P, vector.shape[0])))

    def column(name, vector, copies):
        put(name, np.tile(vector, copies)[:, None])

    for copy in range(4):
        diagonal("conv1", w["L0_tok_conv1_w"].T, BATCH, copy * BATCH * REDUCED)
        for k in range(TAPS):
            for b in range(BATCH):
                tap = np.broadcast_to(w["L0_tok_conv2_w"][k][:, None], (REDUCED, CH))
                put("conv2", tap, (copy * BATCH + b) * REDUCED, k * P + b * CH)
    for k, name in enumerate(("conv1_b", "bn_gamma", "bn_beta", "bn_mean", "bn_var")):
        put("bn", np.tile(w["L0_tok_" + name], 4 * BATCH)[:, None], 0, k)
    row("conv2_b", w["L0_tok_conv2_b"])
    for s in "kq":
        diagonal(s + "w1", w[f"L0_attn_{s}w1"].T, BATCH)
        column(s + "b1", w[f"L0_attn_{s}b1"], BATCH)
        diagonal(s + "w2", np.concatenate([w[f"L0_attn_{s}w2"].T] * 2, axis=1), BATCH)
        column(s + "b2", w[f"L0_attn_{s}b2"], 2 * BATCH)
    diagonal("vw", w["L0_attn_vw"].T, BATCH)
    row("vb", np.tile(w["L0_attn_vb"], BATCH))
    hl = w["L0_ffn_hl_w"].reshape(NH * HD, FEAT)
    diagonal("hl", hl.T, BATCH)
    column("hl_b", w["L0_ffn_hl_b"].reshape(-1), BATCH)
    for b in range(BATCH):
        for n in range(NH):
            r = (b * NH + n) * HD
            put("wk", w["L0_ffn_wk"][n].T, r, r)
            put("wv", w["L0_ffn_wv"][n].T, r, r)
            for e in range(NE):
                put("wq", w["L0_ffn_wq"][n, e].T, r, e * P + r)
    for n in range(NH):
        put("gate", w["L0_ffn_gate_w"][n].T, n % 2 * FEAT, n // 2 * 32 + n % 2 * NE)
    row("gate_b", np.tile(w["L0_ffn_gate_b"].reshape(-1), BATCH))
    row("ln_g", w["L0_ffn_ln_g"])
    row("ln_b", w["L0_ffn_ln_b"])
    diagonal("fc1", w["L0_ffn_fc1_w"].T, HEADS)
    column("fc1_b", w["L0_ffn_fc1_b"], HEADS)
    diagonal("fc2", w["L0_ffn_fc2_w"].T, HEADS)
    row("fc2_b", np.tile(w["L0_ffn_fc2_b"], HEADS))
    row("fn_g", w["L0_ffn_fnorm_g"])
    row("fn_b", w["L0_ffn_fnorm_b"])
    diagonal("fgate", w["L0_ffn_fgate_w"].T, BATCH)
    a = np.arange(P)
    put("ident", np.eye(P, dtype=np.float32))
    put("keep", (a[:, None] <= a[None, :]).astype(np.float32))
    put("neg_s", np.where(a[None, :] > a[:, None], NEG, 0.0).astype(np.float32))
    put("neg_t", np.where(a[:, None] > a[None, :], NEG, 0.0).astype(np.float32))
    pos = (a[:, None] + P * np.arange(TILES)[None, :] + 1).astype(np.float64)
    put("inv_norm", (1.0 / np.sqrt(pos * PHASES)).astype(np.float32))
    cosine = (a // PHASES % 2 == 1)
    put("phase", np.stack([np.where(cosine, -1.0, 1.0), np.where(cosine, -PI_BELOW, PI_BELOW),
                           np.where(cosine, np.pi / 2, 0.0)], axis=1).astype(np.float32))
    return c


def kernel(**inputs):
    import concourse.bacc as _bacc
    from concourse.bass_utils import run_bass_kernel_spmd as _run

    inputs = {k: np.ascontiguousarray(v) for k, v in inputs.items()}
    arrays = {"x_dram": inputs["x"], "txt_dram": inputs["txt"], "packed_dram": pack_constants(inputs)}
    nc = _bacc.Bacc("TRN2", target_bir_lowering=False, num_devices=1)
    args = [nc.dram_tensor(n, a.shape, mybir.dt.from_np(a.dtype), kind="ExternalInput").ap() for n, a in arrays.items()]
    out = nc.dram_tensor("out_dram", (BATCH, TOKENS, FEAT), mybir.dt.float32, kind="ExternalOutput").ap()
    build(nc, *args, out)
    r = _run(nc, [arrays], core_ids=[0])
    return r.results[0]["out_dram"]
```
